# Optimizing a Trainium2 kernel written in Bass

```python
import numpy as np
import jax
import jax.numpy as jnp

def _softmax(x, axis=-1):
    return jax.nn.softmax(x, axis=axis)

def _gelu(x):
    return jax.nn.gelu(x, approximate=True)

def _silu(x):
    return jax.nn.silu(x)

def _sigmoid(x):
    return jax.nn.sigmoid(x)

def _layernorm(x, axis=-1, eps=1e-05):
    m = jnp.mean(x, axis=axis, keepdims=True)
    v = jnp.var(x, axis=axis, keepdims=True)
    return (x - m) / jnp.sqrt(v + eps)

def _scatter_add(tgt, idx, src, axis=0):
    return tgt.at[idx].add(src)

def _segment_sum(src, seg, n):
    return jax.ops.segment_sum(src, seg, n)
kernel_name = 'mk_early_fusion_d1_tok_img256_r4_6adcf0'

def setup_inputs(seed: int=0):
    np.random.seed(seed)
    _w = jnp.asarray

    def _rec_inputs():
        import jax
        import jax.numpy as jnp
        _rk = jax.random.key(seed)
        x = -4.65018e-05 + 0.999886 * jax.random.normal(jax.random.fold_in(_rk, 1), (128, 3, 128, 128), jnp.float32)
        txt = -7.32986e-11 + 0.999998 * jax.random.normal(jax.random.fold_in(_rk, 2), (128, 32, 64), jnp.float32)
        return (x, txt)
    x, txt = _rec_inputs()

    def _L0_tok_setup():
        import jax, jax.numpy as jnp
        import numpy as np
        B = 64
        IMG = 128
        P = 32
        DIM = 64
        DEPTH = 4
        HEADS = 4
        DH = 64
        MLP = 128
        PD = 3 * P * P
        GRID = IMG // P
        NPATCH = GRID * GRID

        def _ln(x, g, b):
            m = jnp.mean(x, -1, keepdims=True)
            v = jnp.mean((x - m) ** 2, -1, keepdims=True)
            return (x - m) * jax.lax.rsqrt(v + 1e-05) * g + b
        key = jax.random.key(seed)
        ks = jax.random.split(key, 10)

        def n(k, shape, s=0.02):
            return jax.random.normal(k, shape, jnp.float32) * s
        return {'img': jax.random.normal(ks[0], (B, 3, IMG, IMG), jnp.float32), 'ln_p1_g': jnp.ones((PD,), jnp.float32), 'ln_p1_b': jnp.zeros((PD,), jnp.float32), 'W_patch': n(ks[1], (PD, DIM)), 'b_patch': jnp.zeros((DIM,), jnp.float32), 'ln_p2_g': jnp.ones((DIM,), jnp.float32), 'ln_p2_b': jnp.zeros((DIM,), jnp.float32), 'cls': n(ks[2], (1, 1, DIM), 1.0), 'pos': n(ks[3], (1, NPATCH + 1, DIM), 1.0), 'attn_ln_g': jnp.ones((DEPTH, DIM), jnp.float32), 'attn_ln_b': jnp.zeros((DEPTH, DIM), jnp.float32), 'Wqkv': n(ks[4], (DEPTH, DIM, 3 * HEADS * DH)), 'Wo': n(ks[5], (DEPTH, HEADS * DH, DIM)), 'bo': jnp.zeros((DEPTH, DIM), jnp.float32), 'ff_ln_g': jnp.ones((DEPTH, DIM), jnp.float32), 'ff_ln_b': jnp.zeros((DEPTH, DIM), jnp.float32), 'W1': n(ks[6], (DEPTH, DIM, MLP)), 'b1': jnp.zeros((DEPTH, MLP), jnp.float32), 'W2': n(ks[7], (DEPTH, MLP, DIM)), 'b2': jnp.zeros((DEPTH, DIM), jnp.float32), 'ln_f_g': jnp.ones((DIM,), jnp.float32), 'ln_f_b': jnp.zeros((DIM,), jnp.float32)}
    _L0_tok_all = _L0_tok_setup()
    _L0_tok_in = {k: v for k, v in _L0_tok_all.items() if k in ('ln_p1_g', 'ln_p1_b', 'W_patch', 'b_patch', 'ln_p2_g', 'ln_p2_b', 'cls', 'pos', 'attn_ln_g', 'attn_ln_b', 'Wqkv', 'Wo', 'bo', 'ff_ln_g', 'ff_ln_b', 'W1', 'b1', 'W2', 'b2', 'ln_f_g', 'ln_f_b')}
    del _L0_tok_all

    def _L0_attn_setup():
        import jax, jax.numpy as jnp
        import numpy as np
        key = jax.random.key(seed)
        B, S, D = (4, 1024, 64)
        rnn_out = jax.random.normal(key, (B, S, D), dtype=jnp.float32)
        return {'rnn_out': rnn_out}
    _L0_attn_all = _L0_attn_setup()
    _L0_attn_in = {k: v for k, v in _L0_attn_all.items() if k in ()}
    del _L0_attn_all

    def _L0_ffn_setup():
        import jax, jax.numpy as jnp
        import numpy as np
        B, N, D = (16, 1024, 64)
        NUM_EXPERTS, TOP_K, HEADS = (4, 2, 4)
        N_EDGES = 262144
        LN_EPS = 1e-05

        def _layernorm(x, g, b):
            mu = x.mean(-1, keepdims=True)
            var = ((x - mu) ** 2).mean(-1, keepdims=True)
            return (x - mu) * jax.lax.rsqrt(var + LN_EPS) * g + b

        def _forward(x, edge_index, W_gat, att_src, att_dst, b_gat, ln_gamma, ln_beta, W1, b1, W2, b2):
            Bc, Nc, Dc = x.shape
            M = Bc * Nc
            x_flat = x.reshape(M, Dc)
            h = (x_flat @ W_gat).reshape(M, HEADS, NUM_EXPERTS)
            loops = jnp.arange(M, dtype=edge_index.dtype)
            src = jnp.concatenate([edge_index[0], loops])
            dst = jnp.concatenate([edge_index[1], loops])
            a_src = (h * att_src).sum(-1)
            a_dst = (h * att_dst).sum(-1)
            e = jax.nn.leaky_relu(a_src[src] + a_dst[dst], negative_slope=0.2)
            e_max = jax.ops.segment_max(e, dst, num_segments=M)
            ee = jnp.exp(e - e_max[dst])
            denom = jax.ops.segment_sum(ee, dst, num_segments=M)
            alpha = ee / (denom[dst] + 1e-16)
            msg = h[src] * alpha[:, :, None]
            agg = jax.ops.segment_sum(msg, dst, num_segments=M).reshape(M, HEADS * NUM_EXPERTS) + b_gat
            scores = _layernorm(agg, ln_gamma, ln_beta).reshape(M, HEADS, NUM_EXPERTS).mean(1)
            scores = scores.reshape(Bc, Nc, NUM_EXPERTS)
            topk_s, topk_i = jax.lax.top_k(scores, TOP_K)
            w = jax.nn.softmax(topk_s, axis=-1)
            out = jnp.zeros_like(x)
            for ei in range(NUM_EXPERTS):
                g = jnp.where(topk_i == ei, w, 0.0).sum(-1)
                hh = jax.nn.gelu(x @ W1[ei] + b1[ei], approximate=False)
                out = out + g[..., None] * (hh @ W2[ei] + b2[ei])
            return out
        key = jax.random.key(seed)
        ks = jax.random.split(key, 8)
        s = 0.05
        return {'x': jax.random.normal(ks[0], (B, N, D), jnp.float32), 'W_gat': jax.random.normal(ks[1], (D, HEADS * NUM_EXPERTS), jnp.float32) * s, 'att_src': jax.random.normal(ks[2], (HEADS, NUM_EXPERTS), jnp.float32) * s, 'att_dst': jax.random.normal(ks[3], (HEADS, NUM_EXPERTS), jnp.float32) * s, 'b_gat': jnp.zeros((HEADS * NUM_EXPERTS,), jnp.float32), 'ln_gamma': jnp.ones((HEADS * NUM_EXPERTS,), jnp.float32), 'ln_beta': jnp.zeros((HEADS * NUM_EXPERTS,), jnp.float32), 'W1': jax.random.normal(ks[4], (NUM_EXPERTS, D, 2 * D), jnp.float32) * s, 'b1': jnp.zeros((NUM_EXPERTS, 2 * D), jnp.float32), 'W2': jax.random.normal(ks[5], (NUM_EXPERTS, 2 * D, D), jnp.float32) * s, 'b2': jnp.zeros((NUM_EXPERTS, D), jnp.float32), 'edge_index': jax.random.randint(ks[6], (2, N_EDGES), 0, B * N, jnp.int32)}
    _L0_ffn_all = _L0_ffn_setup()
    _L0_ffn_in = {k: v for k, v in _L0_ffn_all.items() if k in ('W_gat', 'att_src', 'att_dst', 'b_gat', 'ln_gamma', 'ln_beta', 'W1', 'b1', 'W2', 'b2', 'edge_index')}
    del _L0_ffn_all
    return {'x': x, 'txt': txt, 'L0_tok_ln_p1_g': _L0_tok_in['ln_p1_g'], 'L0_tok_ln_p1_b': _L0_tok_in['ln_p1_b'], 'L0_tok_W_patch': _L0_tok_in['W_patch'], 'L0_tok_b_patch': _L0_tok_in['b_patch'], 'L0_tok_ln_p2_g': _L0_tok_in['ln_p2_g'], 'L0_tok_ln_p2_b': _L0_tok_in['ln_p2_b'], 'L0_tok_cls': _L0_tok_in['cls'], 'L0_tok_pos': _L0_tok_in['pos'], 'L0_tok_attn_ln_g': _L0_tok_in['attn_ln_g'], 'L0_tok_attn_ln_b': _L0_tok_in['attn_ln_b'], 'L0_tok_Wqkv': _L0_tok_in['Wqkv'], 'L0_tok_Wo': _L0_tok_in['Wo'], 'L0_tok_bo': _L0_tok_in['bo'], 'L0_tok_ff_ln_g': _L0_tok_in['ff_ln_g'], 'L0_tok_ff_ln_b': _L0_tok_in['ff_ln_b'], 'L0_tok_W1': _L0_tok_in['W1'], 'L0_tok_b1': _L0_tok_in['b1'], 'L0_tok_W2': _L0_tok_in['W2'], 'L0_tok_b2': _L0_tok_in['b2'], 'L0_tok_ln_f_g': _L0_tok_in['ln_f_g'], 'L0_tok_ln_f_b': _L0_tok_in['ln_f_b'], 'L0_ffn_W_gat': _L0_ffn_in['W_gat'], 'L0_ffn_att_src': _L0_ffn_in['att_src'], 'L0_ffn_att_dst': _L0_ffn_in['att_dst'], 'L0_ffn_b_gat': _L0_ffn_in['b_gat'], 'L0_ffn_ln_gamma': _L0_ffn_in['ln_gamma'], 'L0_ffn_ln_beta': _L0_ffn_in['ln_beta'], 'L0_ffn_W1': _L0_ffn_in['W1'], 'L0_ffn_b1': _L0_ffn_in['b1'], 'L0_ffn_W2': _L0_ffn_in['W2'], 'L0_ffn_b2': _L0_ffn_in['b2'], 'L0_ffn_edge_index': _L0_ffn_in['edge_index']}

def reference(x, txt, L0_tok_ln_p1_g, L0_tok_ln_p1_b, L0_tok_W_patch, L0_tok_b_patch, L0_tok_ln_p2_g, L0_tok_ln_p2_b, L0_tok_cls, L0_tok_pos, L0_tok_attn_ln_g, L0_tok_attn_ln_b, L0_tok_Wqkv, L0_tok_Wo, L0_tok_bo, L0_tok_ff_ln_g, L0_tok_ff_ln_b, L0_tok_W1, L0_tok_b1, L0_tok_W2, L0_tok_b2, L0_tok_ln_f_g, L0_tok_ln_f_b, L0_ffn_W_gat, L0_ffn_att_src, L0_ffn_att_dst, L0_ffn_b_gat, L0_ffn_ln_gamma, L0_ffn_ln_beta, L0_ffn_W1, L0_ffn_b1, L0_ffn_W2, L0_ffn_b2, L0_ffn_edge_index):
    import jax
    import jax.numpy as jnp

    def _L0_tok_ref(img, ln_p1_g, ln_p1_b, W_patch, b_patch, ln_p2_g, ln_p2_b, cls, pos, attn_ln_g, attn_ln_b, Wqkv, Wo, bo, ff_ln_g, ff_ln_b, W1, b1, W2, b2, ln_f_g, ln_f_b):
        import jax, jax.numpy as jnp
        import numpy as np
        B = 64
        IMG = 128
        P = 32
        DIM = 64
        DEPTH = 4
        HEADS = 4
        DH = 64
        MLP = 128
        PD = 3 * P * P
        GRID = IMG // P
        NPATCH = GRID * GRID

        def _ln(x, g, b):
            m = jnp.mean(x, -1, keepdims=True)
            v = jnp.mean((x - m) ** 2, -1, keepdims=True)
            return (x - m) * jax.lax.rsqrt(v + 1e-05) * g + b
        Bsz = img.shape[0]
        x = img.reshape(Bsz, 3, GRID, P, GRID, P)
        x = x.transpose(0, 2, 4, 1, 3, 5).reshape(Bsz, NPATCH, PD)
        x = _ln(x, ln_p1_g, ln_p1_b) @ W_patch + b_patch
        x = _ln(x, ln_p2_g, ln_p2_b)
        x = jnp.concatenate([jnp.broadcast_to(cls, (Bsz, 1, DIM)), x], axis=1) + pos
        scale = DH ** (-0.5)
        for i in range(DEPTH):
            h = _ln(x, attn_ln_g[i], attn_ln_b[i])
            qkv = h @ Wqkv[i]
            q, k, v = jnp.split(qkv, 3, axis=-1)

            def to_heads(t):
                return t.reshape(Bsz, -1, HEADS, DH).transpose(0, 2, 1, 3)
            q, k, v = (to_heads(q), to_heads(k), to_heads(v))
            a = jax.nn.softmax(jnp.einsum('bhqd,bhkd->bhqk', q, k) * scale, axis=-1)
            o = jnp.einsum('bhqk,bhkd->bhqd', a, v)
            o = o.transpose(0, 2, 1, 3).reshape(Bsz, -1, HEADS * DH)
            x = x + o @ Wo[i] + bo[i]
            h = _ln(x, ff_ln_g[i], ff_ln_b[i])
            x = x + jax.nn.gelu(h @ W1[i] + b1[i], approximate=False) @ W2[i] + b2[i]
        return _ln(x, ln_f_g, ln_f_b)

    def _L0_attn_ref(rnn_out):
        import jax, jax.numpy as jnp
        import numpy as np
        scores = jnp.einsum('bsd,btd->bst', rnn_out, rnn_out)
        weights = jax.nn.softmax(scores, axis=1)
        attn_out = jnp.einsum('bst,bsd->btd', weights, rnn_out)
        return attn_out

    def _L0_ffn_ref(x, W_gat, att_src, att_dst, b_gat, ln_gamma, ln_beta, W1, b1, W2, b2, edge_index):
        import jax, jax.numpy as jnp
        import numpy as np
        B, N, D = (16, 1024, 64)
        NUM_EXPERTS, TOP_K, HEADS = (4, 2, 4)
        N_EDGES = 262144
        LN_EPS = 1e-05

        def _layernorm(x, g, b):
            mu = x.mean(-1, keepdims=True)
            var = ((x - mu) ** 2).mean(-1, keepdims=True)
            return (x - mu) * jax.lax.rsqrt(var + LN_EPS) * g + b

        def _forward(x, edge_index, W_gat, att_src, att_dst, b_gat, ln_gamma, ln_beta, W1, b1, W2, b2):
            Bc, Nc, Dc = x.shape
            M = Bc * Nc
            x_flat = x.reshape(M, Dc)
            h = (x_flat @ W_gat).reshape(M, HEADS, NUM_EXPERTS)
            loops = jnp.arange(M, dtype=edge_index.dtype)
            src = jnp.concatenate([edge_index[0], loops])
            dst = jnp.concatenate([edge_index[1], loops])
            a_src = (h * att_src).sum(-1)
            a_dst = (h * att_dst).sum(-1)
            e = jax.nn.leaky_relu(a_src[src] + a_dst[dst], negative_slope=0.2)
            e_max = jax.ops.segment_max(e, dst, num_segments=M)
            ee = jnp.exp(e - e_max[dst])
            denom = jax.ops.segment_sum(ee, dst, num_segments=M)
            alpha = ee / (denom[dst] + 1e-16)
            msg = h[src] * alpha[:, :, None]
            agg = jax.ops.segment_sum(msg, dst, num_segments=M).reshape(M, HEADS * NUM_EXPERTS) + b_gat
            scores = _layernorm(agg, ln_gamma, ln_beta).reshape(M, HEADS, NUM_EXPERTS).mean(1)
            scores = scores.reshape(Bc, Nc, NUM_EXPERTS)
            topk_s, topk_i = jax.lax.top_k(scores, TOP_K)
            w = jax.nn.softmax(topk_s, axis=-1)
            out = jnp.zeros_like(x)
            for ei in range(NUM_EXPERTS):
                g = jnp.where(topk_i == ei, w, 0.0).sum(-1)
                hh = jax.nn.gelu(x @ W1[ei] + b1[ei], approximate=False)
                out = out + g[..., None] * (hh @ W2[ei] + b2[ei])
            return out
        return _forward(x, edge_index, W_gat, att_src, att_dst, b_gat, ln_gamma, ln_beta, W1, b1, W2, b2)
    h = _L0_tok_ref(x, L0_tok_ln_p1_g, L0_tok_ln_p1_b, L0_tok_W_patch, L0_tok_b_patch, L0_tok_ln_p2_g, L0_tok_ln_p2_b, L0_tok_cls, L0_tok_pos, L0_tok_attn_ln_g, L0_tok_attn_ln_b, L0_tok_Wqkv, L0_tok_Wo, L0_tok_bo, L0_tok_ff_ln_g, L0_tok_ff_ln_b, L0_tok_W1, L0_tok_b1, L0_tok_W2, L0_tok_b2, L0_tok_ln_f_g, L0_tok_ln_f_b)
    h = jnp.concatenate([h, txt], axis=1)
    h = h + _L0_attn_ref(_layernorm(h, axis=-1))
    h = h + _L0_ffn_ref(_layernorm(h, axis=-1), L0_ffn_W_gat, L0_ffn_att_src, L0_ffn_att_dst, L0_ffn_b_gat, L0_ffn_ln_gamma, L0_ffn_ln_beta, L0_ffn_W1, L0_ffn_b1, L0_ffn_W2, L0_ffn_b2, L0_ffn_edge_index)
    return h

_drawn_inputs = setup_inputs


def setup_inputs(seed=0):
    import zlib

    import numpy as np

    out = dict(_drawn_inputs(seed))
    spreads = {'L0_tok_ln_p1_g': (1.0, 0.2),
     'L0_tok_ln_p1_b': (0.0, 0.1),
     'L0_tok_b_patch': (0.0, 0.1),
     'L0_tok_ln_p2_g': (1.0, 0.2),
     'L0_tok_ln_p2_b': (0.0, 0.1),
     'L0_tok_attn_ln_g': (1.0, 0.6),
     'L0_tok_attn_ln_b': (0.0, 0.8),
     'L0_tok_bo': (0.0, 0.1),
     'L0_tok_ff_ln_g': (1.0, 0.6),
     'L0_tok_ff_ln_b': (0.0, 0.8),
     'L0_tok_b1': (0.0, 0.788),
     'L0_tok_b2': (0.0, 0.1),
     'L0_tok_ln_f_g': (1.0, 0.2),
     'L0_tok_ln_f_b': (0.0, 0.1),
     'L0_ffn_b_gat': (0.0, 0.418),
     'L0_ffn_ln_gamma': (1.0, 0.2),
     'L0_ffn_ln_beta': (0.0, 0.455),
     'L0_ffn_b1': (0.0, 0.718),
     'L0_ffn_b2': (0.0, 0.1)}
    factors = {'L0_tok_Wqkv': 4.032,
     'L0_tok_Wo': 4.543,
     'L0_tok_W1': 3.561,
     'L0_tok_W2': 3.081,
     'L0_ffn_att_src': 8.0,
     'L0_ffn_att_dst': 8.0}
    for name, (base, spread) in spreads.items():
        noise = np.random.default_rng([zlib.crc32(name.encode()), seed]).standard_normal(out[name].shape)
        drawn = base * np.exp(spread * noise) if base else spread * noise
        out[name] = jnp.asarray(drawn.astype(out[name].dtype))
    for name, factor in factors.items():
        out[name] = (out[name] * factor).astype(out[name].dtype)
    return out
```

```python
from contextlib import ExitStack

import concourse.bass as bass
from concourse import mybir

F32 = mybir.dt.float32
I32 = mybir.dt.int32
U32 = mybir.dt.uint32
BF16 = mybir.dt.bfloat16
ALU = mybir.AluOpType
ACT = mybir.ActivationFunctionType
AX = mybir.AxisListType

B = 128
IMG = 128
PATCH = 32
GRID = IMG // PATCH
CH = 3
PD = CH * PATCH * PATCH
D = 64
NV = GRID * GRID + 1
NTXT = 32
NF = NV + NTXT
LAYERS = 4
HEADS = 4
DH = 64
MLP = 128
EXPERTS = 4
GH = 4
GF = GH * EXPERTS
NODES = B * NF
EDGES = 262144
EPS = 1e-5
MASK = 32768.0


class Chain:

    def __init__(self, eng, sem, per_round, round_no, before=0):
        self.eng, self.sem, self.per_round, self.round_no, self.n = eng, sem, per_round, round_no, 0
        self.before = before

    def step(self, ins):
        ins.then_inc(self.sem, 1)
        self.n += 1

    def settle(self):
        self.eng.wait_ge(self.sem, self.round_no * self.per_round + (self.before + self.n))

    def close(self):
        assert self.n == self.per_round, self.n


def wait_apart(eng, sem, value, passed):
    eng.wait_ge(sem, value)
    eng.sem_inc(passed, 1)


def spread(ap, at, count):
    shape = list(ap.shape)
    shape.insert(at, count)
    return ap.unsqueeze(at).to_broadcast(shape)


def tools(nc, ctx):
    sems = []

    def give_back():
        if sems:
            nc.clear_and_free_semaphores(sems)
            nc.all_engine_barrier()

    ctx.callback(give_back)

    def sb(name, shape, dt=F32):
        return ctx.enter_context(nc.sbuf_tensor(name, shape, dt))

    def ps(name, shape, dt=F32):
        return ctx.enter_context(nc.psum_tensor(name, shape, dt))

    def sem(name):
        sems.append(nc.alloc_semaphore(name))
        return sems[-1]

    return sb, ps, sem


def embed_patches(nc, x, ln1_g, ln1_b, W, b_patch, ln2_g, ln2_b, cls, pos, tokens):
    GI = 32
    NG = B // GI
    LOADS = 4
    CJ = CH * PATCH
    WN = D + 1
    EPI = 14
    PREP = 6
    with ExitStack() as ctx:
        sb, ps, sem = tools(nc, ctx)
        plane = [sb(f"plane{c}", [128, GI * IMG]) for c in range(CH)]
        squares = sb("squares", [128, GI * IMG])
        sq_sum = sb("sq_sum", [128, CH, GI * GRID])
        w_raw = sb("w_raw", [128, CJ, D])
        w_ext = sb("w_ext", [128, CJ, WN])
        scratch = sb("scratch_e", [128, CJ // 2, D])
        g_in = sb("g_in", [128, CJ])
        b_in = sb("b_in", [128, CJ])
        w_sum = sb("w_sum", [128, 2, D])
        ones = sb("ones_e", [128, 128])
        col_sum = sb("col_sum", [128, D])
        const = sb("const", [128, D])
        rows = sb("rows_e", [128, 3, D])
        posP = sb("posP", [128, GRID, D])
        cls_t = sb("cls_t", [1, 2, D])
        cls_all = sb("cls_all", [128, D])
        stat = sb("stat_e", [128, 4, GRID])
        half = sb("half_e", [128, GRID])
        y = sb("y_e", [128, GRID, D])
        y2 = sb("y2_e", [128, GRID, D])
        out_t = sb("out_e", [128, GRID, D])
        acc = ps("acc_e", [128, GRID, 512])
        aux = ps("aux_e", [128, 2, D])
        cls_ps = ps("cls_ps", [128, D])

        params_in = sem("e_params_in")
        plane_in = [sem(f"e_plane_in{c}") for c in range(CH)]
        squared = sem("e_squared")
        sq_summed = sem("e_sq_summed")
        plane_used = [sem(f"e_plane_used{c}") for c in range(CH)]
        consts_set = sem("e_consts_set")
        w_ready = sem("e_w_ready")
        sums_ready = sem("e_sums_ready")
        cls_row = sem("e_cls_row")
        cls_here = sem("e_cls_here")
        cls_done = sem("e_cls_done")
        prep = sem("e_prep")
        acc_ready = sem("e_acc_ready")
        acc_read = sem("e_acc_read")
        var_ready = sem("e_var_ready")
        rstd_ready = sem("e_rstd_ready")
        chain_sem = sem("e_chain")
        out_ready = sem("e_out_ready")
        stored = sem("e_stored")

        block = ctx.enter_context(nc.Block())
        w_view = W.rearrange("(c i j) d -> c i j d", c=CH, i=PATCH)
        tok_view = tokens.rearrange("(b t) d -> b t d", t=NV)

        @block.sync
        def _(sync):
            for gy in range(GRID):
                at = slice(32 * gy, 32 * gy + 32)
                for c in range(CH):
                    cj = slice(c * PATCH, (c + 1) * PATCH)
                    sync.dma_start(w_raw[at, cj, :], w_view[c]).then_inc(params_in, 16)
                    sync.dma_start(g_in[at, cj], ln1_g.rearrange("(c i j) -> c i j", c=CH, i=PATCH)[c])\
                        .then_inc(params_in, 16)
                    sync.dma_start(b_in[at, cj], ln1_b.rearrange("(c i j) -> c i j", c=CH, i=PATCH)[c])\
                        .then_inc(params_in, 16)
            for n, row in enumerate((b_patch, ln2_g, ln2_b)):
                sync.dma_start(rows[:, n, :], row.partition_broadcast(128)).then_inc(params_in, 16)
            patch_pos = pos[0, 1:NV, :].rearrange("(gy gx) d -> gx gy d", gy=GRID)
            for b in range(GI):
                sync.dma_start(posP[b * GRID:(b + 1) * GRID, :, :], patch_pos).then_inc(params_in, 16)
            sync.dma_start(cls_t[:, 0, :], cls[0]).then_inc(params_in, 16)
            sync.dma_start(cls_t[:, 1, :], pos[0, 0:1, :]).then_inc(params_in, 16)
            sync.wait_ge(cls_done, 1)
            sync.dma_start(tok_view[:, 0, :], cls_all[:]).then_inc(stored, 16)
            with sync.Fori(0, NG) as g:
                sync.wait_ge(out_ready, g + 1)
                for gx in range(GRID):
                    dst = tok_view[bass.ds(g * GI, GI), 1 + gx:NV, :][:, 0:NV - 1 - gx:GRID, :]
                    sync.dma_start(dst, out_t[gx:128:GRID, :, :]).then_inc(stored, 16)
            sync.wait_ge(stored, 16 * (1 + NG * GRID))

        n_params = 16 * (GRID * CH * 3 + 3 + GI + 2)

        @block.gpsimd
        def _(pool):
            pool.memset(ones[:], 1.0).then_inc(consts_set, 1)
            pool.memset(half[:], -0.5).then_inc(consts_set, 1)
            pool.wait_ge(consts_set, 2)
            with pool.Fori(0, 2 * NG) as n:
                pool.wait_ge(var_ready, n + 1)
                pool.tensor_tensor(stat[:, 2, :], stat[:, 1, :], half[:], ALU.pow).then_inc(rstd_ready, 1)

        @block.scalar
        def _(act):
            for c in range(CH):
                act.sem_inc(plane_used[c], 2)
            act.sem_inc(sq_summed, 1)
            with act.Fori(0, NG) as g:
                for c in range(CH):
                    act.wait_ge(plane_used[c], 2 * g + 2)
                    for q in range(LOADS):
                        n = GI // LOADS
                        act.dma_start(plane[c][:, q * n * IMG:(q + 1) * n * IMG].rearrange("p (b x) -> p b x", b=n),
                                      x[bass.ds(g * GI + q * n, n), c, :, :].rearrange("b y x -> y b x"))\
                            .then_inc(plane_in[c], 16)
                for c in range(CH):
                    act.wait_ge(plane_in[c], 16 * LOADS * (g + 1))
                    act.wait_ge(sq_summed, CH * g + c + 1)
                    act.activation(squares[:], plane[c][:], ACT.Square).then_inc(squared, 1)
                    act.wait_ge(squared, CH * g + c + 1)
                    act.sem_inc(plane_used[c], 1)

        @block.tensor
        def _(pe):
            pe.wait_ge(w_ready, 2)
            for n in range(2):
                last = pe.matmul(aux[:, n, :], ones[0:32, :], w_sum[0:32, n, :], start=True, stop=True)
            last.then_inc(sums_ready, 1)
            pe.wait_ge(cls_row, 1)
            pe.matmul(cls_ps[:], ones[0:1, :], cls_t[0:1, 0, :], start=True, stop=False)
            pe.matmul(cls_ps[:], ones[0:1, :], cls_t[0:1, 1, :], start=False, stop=True).then_inc(cls_here, 1)
            pe.sem_inc(acc_read, 1)
            with pe.Fori(0, NG) as g:
                pe.wait_ge(acc_read, g + 1)
                for c in range(CH):
                    pe.wait_ge(plane_in[c], 16 * LOADS * (g + 1))
                    for j in range(PATCH):
                        for gy in range(GRID):
                            at = slice(32 * gy, 32 * gy + 32)
                            last = pe.matmul(acc[:, gy, 0:WN], plane[c][at, j:GI * IMG:PATCH],
                                             w_ext[at, c * PATCH + j, :],
                                             start=(c == 0 and j == 0), stop=(c == CH - 1 and j == PATCH - 1))
                    last.then_inc(plane_used[c], 1)
                pe.wait_ge(sq_summed, CH * (g + 1) + 1)
                for gy in range(GRID):
                    at = slice(32 * gy, 32 * gy + 32)
                    for c in range(CH):
                        last = pe.matmul(acc[:, gy, WN:WN + 1], sq_sum[at, c, :], ones[at, 0:1],
                                         start=(c == 0), stop=(c == CH - 1))
                last.then_inc(acc_ready, 1)

        @block.vector
        def _(dve):
            ch = Chain(dve, prep, PREP, 0)
            dve.wait_ge(params_in, n_params)
            dve.wait_ge(consts_set, 2)
            for part in range(2):
                h = slice(part * CJ // 2, (part + 1) * CJ // 2)
                ch.settle()
                ch.step(dve.tensor_tensor(scratch[:], w_raw[:, h, :], spread(b_in[:, h], 2, D), ALU.mult))
                ch.settle()
                ch.step(dve.reduce_sum(w_sum[:, part, :], scratch[:].rearrange("p n d -> p d n"), AX.X))
            ch.settle()
            ch.step(dve.tensor_tensor(w_sum[:, 0, :], w_sum[:, 0, :], w_sum[:, 1, :], ALU.add))
            dve.tensor_tensor(w_ext[:, :, 0:D], w_raw[:], spread(g_in[:], 2, D), ALU.mult).then_inc(w_ready, 1)
            ch.step(dve.memset(w_ext[:, :, D:WN], 1.0))
            dve.wait_ge(w_ready, 1)
            ch.settle()
            ch.close()
            dve.reduce_sum(w_sum[:, 1, :], w_ext[:, :, 0:D].rearrange("p n d -> p d n"), AX.X).then_inc(w_ready, 1)
            dve.sem_inc(cls_row, 1)
            dve.wait_ge(sums_ready, 1)
            dve.tensor_tensor(const[:], aux[:, 0, :], rows[:, 0, :], ALU.add).then_inc(w_ready, 1)
            dve.tensor_copy(col_sum[:], aux[:, 1, :]).then_inc(w_ready, 1)
            dve.wait_ge(cls_here, 1)
            dve.tensor_copy(cls_all[:], cls_ps[:]).then_inc(cls_done, 1)
            dve.wait_ge(w_ready, 4)

            mean, var, rstd, tot = (stat[:, n, :] for n in range(4))
            dve.sem_inc(acc_ready, 1)
            with dve.Fori(0, NG) as g:
                for c in range(CH):
                    dve.wait_ge(squared, CH * g + c + 1)
                    if c == 0:
                        dve.wait_ge(acc_ready, g + 1)
                    dve.reduce_sum(sq_sum[:, c, :], squares[:].rearrange("p (n j) -> p n j", j=PATCH), AX.X)\
                        .then_inc(sq_summed, 1)
                ch = Chain(dve, chain_sem, EPI, g)
                dve.wait_ge(acc_ready, g + 2)
                ch.step(dve.tensor_scalar(mean, acc[:, :, D], 1.0 / PD, None, ALU.mult))
                ch.step(dve.tensor_scalar(tot, acc[:, :, WN], 1.0 / PD, EPS, ALU.mult, ALU.add))
                ch.settle()
                ch.step(dve.tensor_tensor(var, mean, mean, ALU.mult))
                ch.step(dve.tensor_tensor(y2[:], spread(mean, 2, D), spread(col_sum[:], 1, GRID), ALU.mult))
                ch.settle()
                dve.tensor_tensor(var, tot, var, ALU.subtract).then_inc(var_ready, 1)
                dve.tensor_tensor(y[:], acc[:, :, 0:D], y2[:], ALU.subtract).then_inc(acc_read, 1)
                dve.wait_ge(acc_read, g + 2)
                dve.wait_ge(rstd_ready, 2 * g + 1)
                ch.step(dve.tensor_tensor(y2[:], y[:], spread(rstd, 2, D), ALU.mult))
                ch.settle()
                ch.step(dve.tensor_tensor(y[:], y2[:], spread(const[:], 1, GRID), ALU.add))
                ch.settle()
                ch.step(dve.reduce_sum(tot, y[:], AX.X))
                ch.settle()
                ch.step(dve.scalar_tensor_tensor(y2[:], spread(tot, 2, D), -1.0 / D, y[:], ALU.mult, ALU.add))
                ch.settle()
                ch.step(dve.tensor_tensor(y[:], y2[:], y2[:], ALU.mult))
                ch.settle()
                ch.step(dve.reduce_sum(tot, y[:], AX.X))
                ch.settle()
                dve.tensor_scalar(var, tot, 1.0 / D, EPS, ALU.mult, ALU.add).then_inc(var_ready, 1)
                dve.wait_ge(rstd_ready, 2 * g + 2)
                ch.step(dve.tensor_tensor(y[:], y2[:], spread(rstd, 2, D), ALU.mult))
                ch.settle()
                ch.step(dve.tensor_tensor(y2[:], y[:], spread(rows[:, 1, :], 1, GRID), ALU.mult))
                ch.settle()
                ch.step(dve.tensor_tensor(y[:], y2[:], spread(rows[:, 2, :], 1, GRID), ALU.add))
                ch.settle()
                dve.wait_ge(stored, 16 + 16 * GRID * g)
                ch.step(dve.tensor_tensor(y2[:], y[:], posP[:], ALU.add))
                ch.settle()
                dve.tensor_copy(out_t[:], y2[:]).then_inc(out_ready, 1)
                ch.close()


def block_masks(pool, done, images, tokens, left, right):
    n = 0
    for mask, scale in ((left, 1.0), (right, MASK)):
        reps = mask.shape[1]
        pattern = [[0, reps], [1, images * tokens]]
        used = mask[0:images + 1]
        pool.memset(mask, 0.0).then_inc(done, 1)
        pool.wait_ge(done, n + 1)
        pool.memset(used, scale).then_inc(done, 1)
        pool.wait_ge(done, n + 2)
        pool.affine_select(out=used, in_=used, compare_op=ALU.is_ge, fill=0.0, base=tokens,
                           pattern=pattern, channel_multiplier=-tokens).then_inc(done, 1)
        pool.wait_ge(done, n + 3)
        pool.affine_select(out=used, in_=used, compare_op=ALU.is_ge, fill=0.0, base=-1,
                           pattern=[[0, reps], [-1, images * tokens]], channel_multiplier=tokens).then_inc(done, 1)
        pool.wait_ge(done, n + 4)
        pool.memset(mask[0:1], 1.0 if scale == 1.0 else -MASK).then_inc(done, 1)
        n += 5
    return n


def identity(pool, done, n, ident):
    pool.memset(ident, 0.0).then_inc(done, 1)
    pool.wait_ge(done, n + 1)
    pool.affine_select(out=ident, in_=ident, compare_op=ALU.not_equal, fill=1.0, base=0,
                       pattern=[[-1, ident.shape[1]]], channel_multiplier=1).then_inc(done, 1)
    return n + 2


def run_vit(nc, tokens, ln_g, ln_b, Wqkv, Wo, bo, ff_g, ff_b, W1, b1, W2, b2, f_g, f_b, txt, fused):
    IPT = 4
    T = IPT * NV
    NT = 2
    C = NT * T
    TILES = B // IPT
    SUBS = 2
    CHUNKS = TILES // (NT * SUBS)
    HD = HEADS * DH
    NW = 11
    STEPS = 13
    SCALE = DH ** -0.5
    subs = range(SUBS)
    with ExitStack() as ctx:
        sb, ps, sem = tools(nc, ctx)
        X = sb("X", [T, TILES, D])
        wqkv = sb("wqkv", [D, 3 * HD])
        wo = sb("wo", [128, HD // 128, D])
        w1 = sb("w1v", [D, MLP])
        w2 = sb("w2v", [MLP, D])
        b1c = sb("b1c", [MLP, 1])
        bias = sb("bias_v", [128, 2, D])
        first = sb("first_v", [128, T])
        gains = sb("gains_v", [D, 4])
        rows = sb("rows_v", [T, 2, D])
        ident = sb("ident_v", [T, T])
        maskL = sb("maskL_v", [128, 1, T])
        maskR = sb("maskR_v", [128, HEADS, T])
        half = sb("half_v", [T, NT])
        xc = [sb(f"xc_v{s}", [T, NT, D]) for s in subs]
        xh = [sb(f"xh_v{s}", [T, NT, D]) for s in subs]
        stat = [sb(f"stat_v{s}", [T, 3, NT]) for s in subs]
        hT = [sb(f"hT_v{s}", [D, C]) for s in subs]
        qz = [sb(f"qz_v{s}", [128, HEADS, C]) for s in subs]
        kT = [sb(f"kT_v{s}", [128, 2, C]) for s in subs]
        v = [sb(f"v_v{s}", [T, NT, HD]) for s in subs]
        P = [sb(f"P_v{s}", [T, NT * HEADS, T]) for s in subs]
        mx = [sb(f"mx_v{s}", [T, 2, NT * HEADS]) for s in subs]
        pT = [sb(f"pT_v{s}", [T, NT, HEADS * T]) for s in subs]
        oT = [sb(f"oT_v{s}", [128, 2, C]) for s in subs]
        act1 = [sb(f"act1_v{s}", [MLP, C]) for s in subs]
        xf = sb("xf", [T, TILES, D])
        yf = sb("yf", [T, TILES, D])
        fstat = sb("fstat", [T, 3, TILES])
        fhalf = sb("fhalf", [T, TILES])
        psum = ps("psum_v", [128, 8, 512])

        tokens_in = sem("v_tokens_in")
        weights_in = sem("v_weights_in")
        layer_done = sem("v_layer_done")
        consts = sem("v_consts")
        zeroed = sem("v_zeroed")
        chain = [sem(f"v_chain{s}") for s in subs]
        var_ready = [sem(f"v_var{s}") for s in subs]
        rstd_ready = [sem(f"v_rstd{s}") for s in subs]
        xh_ready = [sem(f"v_xh{s}") for s in subs]
        t_ready = [sem(f"v_t{s}") for s in subs]
        hT_ready = [sem(f"v_hT{s}") for s in subs]
        qk_ready = [sem(f"v_qk{s}") for s in subs]
        v_ready = [sem(f"v_v{s}") for s in subs]
        qk_out = [sem(f"v_qk_out{s}") for s in subs]
        v_out = [sem(f"v_v_out{s}") for s in subs]
        s_ready = [sem(f"v_s{s}") for s in subs]
        shifted = [sem(f"v_shifted{s}") for s in subs]
        exped = [sem(f"v_exped{s}") for s in subs]
        p_ready = [sem(f"v_p{s}") for s in subs]
        pT_ready = [sem(f"v_pT{s}") for s in subs]
        pT_out = [sem(f"v_pT_out{s}") for s in subs]
        o_ready = [sem(f"v_o{s}") for s in subs]
        o_out = [sem(f"v_o_out{s}") for s in subs]
        wo_ready = [sem(f"v_wo{s}") for s in subs]
        h1_ready = [sem(f"v_h1{s}") for s in subs]
        gelu_ready = [sem(f"v_gelu{s}") for s in subs]
        w2_ready = [sem(f"v_w2{s}") for s in subs]
        final = sem("v_final")
        pe_passed = sem("v_pe_passed")
        dve_passed = sem("v_dve_passed")
        fvar = sem("v_fvar")
        frstd = sem("v_frstd")
        out_ready = sem("v_out_ready")
        stored = sem("v_stored")
        block = ctx.enter_context(nc.Block())

        def bank(s, n):
            return psum[:, SUBS * 2 * s + n, :]

        def banks(s, n):
            return psum[:, SUBS * 2 * s + n:SUBS * 2 * s + n + 2, :]

        def tiles(c, s):
            return bass.ds((c * SUBS + s) * NT, NT)

        @block.sync
        def _(sync):
            sync.dma_start(X[:], tokens.rearrange("(n p) d -> p n d", p=T)).then_inc(tokens_in, 16)
            sync.dma_start(rows[:, 0, :], f_g.partition_broadcast(T)).then_inc(tokens_in, 16)
            sync.dma_start(rows[:, 1, :], f_b.partition_broadcast(T)).then_inc(tokens_in, 16)
            fused_view = fused.rearrange("(b t) d -> b t d", t=NF)
            sync.dma_start(fused_view[:, NV:NF, :], txt).then_inc(stored, 16)
            sync.wait_ge(zeroed, 2)
            with sync.Fori(0, LAYERS) as l:
                sync.wait_ge(layer_done, l + 1)
                one = bass.ds(l, 1)
                sync.dma_start(wqkv[:], Wqkv[one].rearrange("l k n -> (l k) n")).then_inc(weights_in, 16)
                sync.dma_start(wo[:], Wo[one].rearrange("l (c k) n -> (l k) c n", k=128)).then_inc(weights_in, 16)
                sync.dma_start(w1[:], W1[one].rearrange("l k n -> (l k) n")).then_inc(weights_in, 16)
                sync.dma_start(w2[:], W2[one].rearrange("l k n -> (l k) n")).then_inc(weights_in, 16)
                sync.dma_start(b1c[:], b1[one].rearrange("l k -> k l")).then_inc(weights_in, 16)
                for n, row in enumerate((bo, b2)):
                    sync.dma_start(bias[0:1, n, :], row[one]).then_inc(weights_in, 16)
                for n, col in enumerate((ln_g, ln_b, ff_g, ff_b)):
                    sync.dma_start(gains[:, n:n + 1], col[one].rearrange("l k -> k l")).then_inc(weights_in, 16)
            sync.wait_ge(out_ready, 1)
            for i in range(IPT):
                sync.dma_start(fused_view[i:B:IPT, 0:NV, :].rearrange("n t d -> t n d"),
                               xf[i * NV:(i + 1) * NV, :, :]).then_inc(stored, 16)
            sync.wait_ge(stored, 16 * (IPT + 1))

        @block.gpsimd
        def _(pool):
            n = block_masks(pool, consts, IPT, NV, maskL[:], maskR[:])
            n = identity(pool, consts, n, ident[:])
            pool.memset(first[:], 0.0).then_inc(consts, 1)
            pool.wait_ge(consts, n + 1)
            pool.memset(first[0:1, :], 1.0).then_inc(consts, 1)
            pool.memset(half[:], -0.5).then_inc(consts, 1)
            pool.memset(fhalf[:], -0.5).then_inc(consts, 1)
            pool.memset(bias[:], 0.0).then_inc(zeroed, 1)
            pool.wait_ge(consts, n + 4)
            with pool.Fori(0, LAYERS * CHUNKS * 2) as r:
                for s in subs:
                    pool.wait_ge(var_ready[s], r + 1)
                    pool.tensor_tensor(stat[s][:, 2, :], stat[s][:, 1, :], half[:], ALU.pow)\
                        .then_inc(rstd_ready[s], 1)
            pool.wait_ge(fvar, 1)
            pool.tensor_tensor(fstat[:, 2, :], fstat[:, 1, :], fhalf[:], ALU.pow).then_inc(frstd, 1)

        N_CONSTS = 10 + 2 + 4

        @block.scalar
        def _(act):
            with act.Fori(0, LAYERS) as l:
                act.wait_ge(weights_in, 16 * NW * (l + 1))
                with act.Fori(0, CHUNKS) as c:
                    r = l * CHUNKS + c
                    for s in subs:
                        act.wait_ge(t_ready[s], 2 * r + 1)
                        act.activation(hT[s][:], bank(s, 3)[0:D, 0:C], ACT.Identity,
                                       bias=gains[:, 1:2], scale=gains[:, 0:1]).then_inc(hT_ready[s], 1)
                    for s in subs:
                        act.wait_ge(qk_ready[s], r + 1)
                        q = bank(s, 0)[:, 0:2 * C].rearrange("p (h c) -> p h c", h=2)
                        act.activation(qz[s][0:DH, 0:HEADS:2, :], q[0:DH], ACT.Copy).then_inc(qk_out[s], 1)
                        act.activation(qz[s][DH:128, 1:HEADS:2, :], q[DH:128], ACT.Copy).then_inc(qk_out[s], 1)
                        act.activation(kT[s][:], bank(s, 1)[:, 0:2 * C].rearrange("p (h c) -> p h c", h=2),
                                       ACT.Copy).then_inc(qk_out[s], 1)
                    for s in subs:
                        act.wait_ge(shifted[s], r + 1)
                        act.activation(P[s][:], P[s][:], ACT.Exp, scale=SCALE).then_inc(exped[s], 1)
                    for s in subs:
                        act.wait_ge(pT_ready[s], r + 1)
                        act.activation(pT[s][:], banks(s, 2)[0:T, :, 0:HEADS * T], ACT.Copy).then_inc(pT_out[s], 1)
                    for s in subs:
                        act.wait_ge(o_ready[s], r + 1)
                        act.activation(oT[s][:], bank(s, 0)[:, 0:2 * C].rearrange("p (h c) -> p h c", h=2),
                                       ACT.Copy).then_inc(o_out[s], 1)
                    for s in subs:
                        act.wait_ge(t_ready[s], 2 * r + 2)
                        act.activation(hT[s][:], bank(s, 3)[0:D, 0:C], ACT.Identity,
                                       bias=gains[:, 3:4], scale=gains[:, 2:3]).then_inc(hT_ready[s], 1)
                    for s in subs:
                        act.wait_ge(h1_ready[s], r + 1)
                        act.activation(act1[s][:], bank(s, 2)[:, 0:C], ACT.Gelu, bias=b1c[:]).then_inc(gelu_ready[s], 1)

        @block.tensor
        def _(pe):
            pe.wait_ge(consts, N_CONSTS)
            pe.wait_ge(zeroed, 2)
            with pe.Fori(0, LAYERS) as l:
                wait_apart(pe, weights_in, 16 * NW * (l + 1), pe_passed)
                with pe.Fori(0, CHUNKS) as c:
                    r = l * CHUNKS + c

                    def transposed(s, nth):
                        wait_apart(pe, xh_ready[s], 2 * r + nth, pe_passed)
                        for t in range(NT):
                            last = pe.transpose(bank(s, 3)[0:D, t * T:(t + 1) * T], xh[s][:, t, :], ident[:])
                        last.then_inc(t_ready[s], 1)

                    for s in subs:
                        transposed(s, 1)
                    for s in subs:
                        pe.wait_ge(hT_ready[s], 2 * r + 1)
                        for m in range(4):
                            last = pe.matmul(bank(s, m // 2)[:, (m % 2) * C:(m % 2 + 1) * C],
                                             wqkv[:, m * 128:(m + 1) * 128], hT[s][:], start=True, stop=True)
                        last.then_inc(qk_ready[s], 1)
                        for t in range(NT):
                            last = pe.matmul(bank(s, 2)[0:T, t * HD:(t + 1) * HD], hT[s][:, t * T:(t + 1) * T],
                                             wqkv[:, 2 * HD:3 * HD], start=True, stop=True)
                        last.then_inc(v_ready[s], 1)
                    for s in subs:
                        pe.wait_ge(qk_out[s], 3 * (r + 1))
                        for t in range(NT):
                            at = slice(t * T, (t + 1) * T)
                            pe.matmul(bank(s, t)[0:T, 0:HEADS * T], maskL[:, 0, :],
                                      maskR[:].rearrange("p h t -> p (h t)"),
                                      start=True, stop=False, skip_group_check=True)
                            for h in range(HEADS):
                                last = pe.matmul(bank(s, t)[0:T, h * T:(h + 1) * T], qz[s][:, h, at],
                                                 kT[s][:, h // 2, at], start=False, stop=(h == HEADS - 1),
                                                 skip_group_check=True)
                        last.then_inc(s_ready[s], 1)
                    for s in subs:
                        pe.wait_ge(p_ready[s], r + 1)
                        pe.wait_ge(v_out[s], r + 1)
                        for t in range(NT):
                            for h in range(HEADS):
                                last = pe.transpose(bank(s, 2 + t)[0:T, h * T:(h + 1) * T],
                                                    P[s][:, t * HEADS + h, :], ident[:])
                        last.then_inc(pT_ready[s], 1)
                    for s in subs:
                        pe.wait_ge(pT_out[s], r + 1)
                        for t in range(NT):
                            for h in range(HEADS):
                                to = bank(s, 0)[DH * (h % 2):DH * (h % 2) + DH,
                                                (h // 2) * C + t * T:(h // 2) * C + (t + 1) * T]
                                last = pe.matmul(to, v[s][:, t, h * DH:(h + 1) * DH],
                                                 pT[s][:, t, h * T:(h + 1) * T], start=True, stop=True)
                        last.then_inc(o_ready[s], 1)
                    for s in subs:
                        pe.wait_ge(o_out[s], r + 1)
                        for t in range(NT):
                            to = bank(s, 1)[0:T, t * D:(t + 1) * D]
                            pe.matmul(to, first[:], bias[:, 0, :], start=True, stop=False)
                            for m in range(2):
                                last = pe.matmul(to, oT[s][:, m, t * T:(t + 1) * T], wo[:, m, :],
                                                 start=False, stop=(m == 1))
                        last.then_inc(wo_ready[s], 1)
                    for s in subs:
                        transposed(s, 2)
                    for s in subs:
                        pe.wait_ge(hT_ready[s], 2 * r + 2)
                        pe.matmul(bank(s, 2)[:, 0:C], w1[:], hT[s][:], start=True, stop=True)\
                            .then_inc(h1_ready[s], 1)
                    for s in subs:
                        pe.wait_ge(gelu_ready[s], r + 1)
                        for t in range(NT):
                            to = bank(s, 1)[0:T, (NT + t) * D:(NT + t + 1) * D]
                            pe.matmul(to, first[:], bias[:, 1, :], start=True, stop=False)
                            last = pe.matmul(to, act1[s][:, t * T:(t + 1) * T], w2[:], start=False, stop=True)
                        last.then_inc(w2_ready[s], 1)

        @block.vector
        def _(dve):
            for s in subs:
                last = dve.memset(qz[s][:], 0.0)
            last.then_inc(zeroed, 1)
            dve.wait_ge(consts, N_CONSTS)
            dve.wait_ge(tokens_in, 48)
            dve.sem_inc(layer_done, 1)
            with dve.Fori(0, LAYERS) as l:
                with dve.Fori(0, CHUNKS) as c:
                    r = l * CHUNKS + c
                    ch = [Chain(dve, chain[s], STEPS, r) for s in subs]

                    def normalise(nth):
                        total, var, rstd = (lambda s: stat[s][:, 0, :]), (lambda s: stat[s][:, 1, :]), \
                            (lambda s: stat[s][:, 2, :])
                        for s in subs:
                            if nth == 2:
                                ch[s].settle()
                                dve.sem_inc(dve_passed, 1)
                            ch[s].step(dve.reduce_sum(total(s), X[:, tiles(c, s), :], AX.X))
                        for s in subs:
                            ch[s].settle()
                            ch[s].step(dve.scalar_tensor_tensor(xc[s][:], spread(total(s), 2, D), -1.0 / D,
                                                                X[:, tiles(c, s), :], ALU.mult, ALU.add))
                        for s in subs:
                            ch[s].settle()
                            ch[s].step(dve.tensor_tensor(xh[s][:], xc[s][:], xc[s][:], ALU.mult))
                        for s in subs:
                            ch[s].settle()
                            ch[s].step(dve.reduce_sum(total(s), xh[s][:], AX.X))
                        for s in subs:
                            ch[s].settle()
                            dve.tensor_scalar(var(s), total(s), 1.0 / D, EPS, ALU.mult, ALU.add)\
                                .then_inc(var_ready[s], 1)
                        for s in subs:
                            dve.wait_ge(rstd_ready[s], 2 * r + nth)
                            dve.tensor_tensor(xh[s][:], xc[s][:], spread(rstd(s), 2, D), ALU.mult)\
                                .then_inc(xh_ready[s], 1)

                    normalise(1)
                    for s in subs:
                        dve.wait_ge(v_ready[s], r + 1)
                        dve.tensor_copy(v[s][:].rearrange("p t n -> p (t n)"), bank(s, 2)[0:T, :])\
                            .then_inc(v_out[s], 1)
                    scores = [banks(s, 0)[0:T, :, 0:HEADS * T].rearrange("p t (h k) -> p t h k", h=HEADS)
                              for s in subs]
                    for s in subs:
                        dve.wait_ge(s_ready[s], r + 1)
                        ch[s].step(dve.reduce_max(mx[s][:, 0, :].rearrange("p (t h) -> p t h", t=NT),
                                                  scores[s], AX.X))
                    for s in subs:
                        ch[s].settle()
                        dve.tensor_tensor(P[s][:].rearrange("p (t h) k -> p t h k", t=NT), scores[s],
                                          spread(mx[s][:, 0, :].rearrange("p (t h) -> p t h", t=NT), 3, T),
                                          ALU.subtract).then_inc(shifted[s], 1)
                    for s in subs:
                        dve.wait_ge(exped[s], r + 1)
                        ch[s].step(dve.reduce_sum(mx[s][:, 0, :], P[s][:], AX.X))
                    for s in subs:
                        ch[s].settle()
                        ch[s].step(dve.reciprocal(mx[s][:, 1, :], mx[s][:, 0, :]))
                    for s in subs:
                        ch[s].settle()
                        dve.tensor_tensor(P[s][:], P[s][:], spread(mx[s][:, 1, :], 2, T), ALU.mult)\
                            .then_inc(p_ready[s], 1)
                    for s in subs:
                        dve.wait_ge(wo_ready[s], r + 1)
                        ch[s].step(dve.tensor_tensor(
                            X[:, tiles(c, s), :], X[:, tiles(c, s), :],
                            bank(s, 1)[0:T, 0:NT * D].rearrange("p (t d) -> p t d", t=NT), ALU.add))
                    normalise(2)
                    for s in subs:
                        dve.wait_ge(w2_ready[s], r + 1)
                        ch[s].step(dve.tensor_tensor(
                            X[:, tiles(c, s), :], X[:, tiles(c, s), :],
                            bank(s, 1)[0:T, NT * D:2 * NT * D].rearrange("p (t d) -> p t d", t=NT), ALU.add))
                    for s in subs:
                        ch[s].settle()
                    ch[0].close()
                    ch[1].close()
                dve.sem_inc(layer_done, 1)
            total, var, rstd = fstat[:, 0, :], fstat[:, 1, :], fstat[:, 2, :]
            ch = Chain(dve, final, 6, 0)
            ch.step(dve.reduce_sum(total, X[:], AX.X))
            ch.settle()
            ch.step(dve.scalar_tensor_tensor(yf[:], spread(total, 2, D), -1.0 / D, X[:], ALU.mult, ALU.add))
            ch.settle()
            ch.step(dve.tensor_tensor(xf[:], yf[:], yf[:], ALU.mult))
            ch.settle()
            ch.step(dve.reduce_sum(total, xf[:], AX.X))
            ch.settle()
            dve.tensor_scalar(var, total, 1.0 / D, EPS, ALU.mult, ALU.add).then_inc(fvar, 1)
            dve.wait_ge(frstd, 1)
            ch.step(dve.tensor_tensor(xf[:], yf[:], spread(rstd, 2, D), ALU.mult))
            ch.settle()
            ch.step(dve.tensor_tensor(yf[:], xf[:], spread(rows[:, 0, :], 1, TILES), ALU.mult))
            ch.settle()
            ch.close()
            dve.tensor_tensor(xf[:], yf[:], spread(rows[:, 1, :], 1, TILES), ALU.add).then_inc(out_ready, 1)


def fuse_and_expert(nc, fused, gat_w, W1, b1, W2, b2, hidden, gat_h, expert_out):
    IPT = 2
    T = IPT * NF
    NT = 2
    C = NT * T
    TILES = B // IPT
    SUBS = 2
    ROUNDS = TILES // (NT * SUBS)
    EH = 2 * D
    STEPS = 14
    subs = range(SUBS)
    with ExitStack() as ctx:
        sb, ps, sem = tools(nc, ctx)
        H = sb("H", [T, TILES, D])
        wg = sb("wg", [D, GF])
        w1 = sb("w1f", [D, EXPERTS, EH])
        w2 = sb("w2f", [EH, EXPERTS, D])
        b1c = sb("b1f", [EH, EXPERTS])
        bias = sb("bias_f", [128, EXPERTS * D])
        first = sb("first_f", [128, T])
        ident = sb("ident_f", [T, T])
        maskL = sb("maskL_f", [128, 1, T])
        maskR = sb("maskR_f", [128, NT, T])
        half = sb("half_f", [T, NT])
        xr = [sb(f"xr_f{s}", [T, NT, D]) for s in subs]
        xc = [sb(f"xc_f{s}", [T, NT, D]) for s in subs]
        sq = [sb(f"sq_f{s}", [T, NT, D]) for s in subs]
        xh = [sb(f"xh_f{s}", [T, NT, D]) for s in subs]
        stat = [sb(f"stat_f{s}", [T, 3, NT]) for s in subs]
        hT = [sb(f"hT_f{s}", [D, C]) for s in subs]
        P = [sb(f"P_f{s}", [T, NT, T]) for s in subs]
        mx = [sb(f"mx_f{s}", [T, 2, NT]) for s in subs]
        pT = [sb(f"pT_f{s}", [T, C]) for s in subs]
        act1 = [sb(f"act1_f{s}", [EH, EXPERTS, C]) for s in subs]
        gh = [sb(f"gh_f{s}", [T, NT, GF]) for s in subs]
        eo = [sb(f"eo_f{s}", [T, NT, EXPERTS * D]) for s in subs]
        psum = ps("psum_f", [128, 8, 512])

        loaded = sem("f_loaded")
        consts = sem("f_consts")
        zeroed = sem("f_zeroed")
        chain = [sem(f"f_chain{s}") for s in subs]
        var_ready = [sem(f"f_var{s}") for s in subs]
        rstd_ready = [sem(f"f_rstd{s}") for s in subs]
        xh_ready = [sem(f"f_xh{s}") for s in subs]
        t_ready = [sem(f"f_t{s}") for s in subs]
        hT_ready = [sem(f"f_hT{s}") for s in subs]
        s_ready = [sem(f"f_s{s}") for s in subs]
        shifted = [sem(f"f_shifted{s}") for s in subs]
        exped = [sem(f"f_exped{s}") for s in subs]
        p_ready = [sem(f"f_p{s}") for s in subs]
        pT_ready = [sem(f"f_pT{s}") for s in subs]
        pT_out = [sem(f"f_pT_out{s}") for s in subs]
        o_ready = [sem(f"f_o{s}") for s in subs]
        gat_ready = [sem(f"f_gat{s}") for s in subs]
        h1_ready = [sem(f"f_h1{s}") for s in subs]
        gelu_ready = [sem(f"f_gelu{s}") for s in subs]
        eo_ready = [sem(f"f_eo{s}") for s in subs]
        gh_out = [sem(f"f_gh_out{s}") for s in subs]
        eo_out = [sem(f"f_eo_out{s}") for s in subs]
        gh_stored = [sem(f"f_gh_stored{s}") for s in subs]
        eo_stored = [sem(f"f_eo_stored{s}") for s in subs]
        h_done = sem("f_h_done")
        h_stored = sem("f_h_stored")
        pe_passed = sem("f_pe_passed")
        dve_passed = sem("f_dve_passed")
        block = ctx.enter_context(nc.Block())

        def bank(s, n):
            return psum[:, 4 * s + n, :]

        def tiles(r, s):
            return bass.ds((r * SUBS + s) * NT, NT)

        N_LOADS = 16 * (1 + 4 + EXPERTS)

        @block.sync
        def _(sync):
            sync.dma_start(H[:], fused.rearrange("(n p) d -> p n d", p=T)).then_inc(loaded, 16)
            sync.dma_start(wg[:], gat_w).then_inc(loaded, 16)
            sync.dma_start(w1[:], W1.rearrange("e k n -> k e n")).then_inc(loaded, 16)
            sync.dma_start(w2[:], W2.rearrange("e k n -> k e n")).then_inc(loaded, 16)
            for e in range(EXPERTS):
                sync.dma_start(b1c[:, e:e + 1], b1[e:e + 1, :].rearrange("e k -> k e")).then_inc(loaded, 16)
            sync.wait_ge(zeroed, 1)
            sync.dma_start(bias[0:1, :], b2.rearrange("(a e) d -> a (e d)", a=1)).then_inc(loaded, 16)
            gat_view = gat_h.rearrange("(n p) d -> p n d", p=T)
            eo_view = expert_out.rearrange("(n p) d -> p n d", p=T)
            with sync.Fori(0, ROUNDS) as r:
                for s in subs:
                    sync.wait_ge(gh_out[s], r + 1)
                    sync.dma_start(gat_view[:, tiles(r, s), :], gh[s][:]).then_inc(gh_stored[s], 16)
                    sync.wait_ge(eo_out[s], r + 1)
                    sync.dma_start(eo_view[:, tiles(r, s), :], eo[s][:]).then_inc(eo_stored[s], 16)
            sync.wait_ge(h_done, 1)
            sync.dma_start(hidden.rearrange("(n p) d -> p n d", p=T), H[:]).then_inc(h_stored, 16)
            sync.wait_ge(h_stored, 16)
            for s in subs:
                sync.wait_ge(gh_stored[s], 16 * (ROUNDS + 1))
                sync.wait_ge(eo_stored[s], 16 * (ROUNDS + 1))

        @block.gpsimd
        def _(pool):
            n = block_masks(pool, consts, IPT, NF, maskL[:], maskR[:])
            n = identity(pool, consts, n, ident[:])
            pool.memset(first[:], 0.0).then_inc(consts, 1)
            pool.wait_ge(consts, n + 1)
            pool.memset(first[0:1, :], 1.0).then_inc(consts, 1)
            pool.memset(half[:], -0.5).then_inc(consts, 1)
            pool.memset(bias[:], 0.0).then_inc(zeroed, 1)
            pool.wait_ge(consts, n + 3)
            with pool.Fori(0, ROUNDS * 2) as r:
                for s in subs:
                    pool.wait_ge(var_ready[s], r + 1)
                    pool.tensor_tensor(stat[s][:, 2, :], stat[s][:, 1, :], half[:], ALU.pow)\
                        .then_inc(rstd_ready[s], 1)

        N_CONSTS = 10 + 2 + 3

        @block.scalar
        def _(act):
            act.wait_ge(loaded, N_LOADS)
            with act.Fori(0, ROUNDS) as r:
                for s in subs:
                    act.wait_ge(t_ready[s], 2 * r + 1)
                    act.activation(hT[s][:], bank(s, 3)[0:D, 0:C], ACT.Copy).then_inc(hT_ready[s], 1)
                for s in subs:
                    act.wait_ge(shifted[s], r + 1)
                    act.activation(P[s][:], P[s][:], ACT.Exp).then_inc(exped[s], 1)
                for s in subs:
                    act.wait_ge(pT_ready[s], r + 1)
                    act.activation(pT[s][:], bank(s, 1)[0:T, 0:C], ACT.Copy).then_inc(pT_out[s], 1)
                for s in subs:
                    act.wait_ge(t_ready[s], 2 * r + 2)
                    act.activation(hT[s][:], bank(s, 3)[0:D, 0:C], ACT.Copy).then_inc(hT_ready[s], 1)
                for s in subs:
                    act.wait_ge(h1_ready[s], r + 1)
                    for e in range(EXPERTS):
                        last = act.activation(act1[s][:, e, :], bank(s, e // 2)[:, (e % 2) * C:(e % 2 + 1) * C],
                                              ACT.Gelu, bias=b1c[:, e:e + 1])
                    last.then_inc(gelu_ready[s], 1)

        @block.tensor
        def _(pe):
            pe.wait_ge(consts, N_CONSTS)
            pe.wait_ge(loaded, N_LOADS)
            with pe.Fori(0, ROUNDS) as r:
                def transposed(s, nth):
                    wait_apart(pe, xh_ready[s], 2 * r + nth, pe_passed)
                    for t in range(NT):
                        last = pe.transpose(bank(s, 3)[0:D, t * T:(t + 1) * T], xh[s][:, t, :], ident[:])
                    last.then_inc(t_ready[s], 1)

                for s in subs:
                    transposed(s, 1)
                for s in subs:
                    pe.wait_ge(hT_ready[s], 2 * r + 1)
                    pe.matmul(bank(s, 0)[0:T, 0:C], maskL[:, 0, :], maskR[:].rearrange("p n t -> p (n t)"),
                              start=True, stop=False, skip_group_check=True)
                    for t in range(NT):
                        at = slice(t * T, (t + 1) * T)
                        last = pe.matmul(bank(s, 0)[0:T, at], hT[s][:, at], hT[s][:, at],
                                         start=False, stop=(t == NT - 1), skip_group_check=True)
                    last.then_inc(s_ready[s], 1)
                for s in subs:
                    pe.wait_ge(p_ready[s], r + 1)
                    for t in range(NT):
                        last = pe.transpose(bank(s, 1)[0:T, t * T:(t + 1) * T], P[s][:, t, :], ident[:])
                    last.then_inc(pT_ready[s], 1)
                for s in subs:
                    pe.wait_ge(pT_out[s], r + 1)
                    for t in range(NT):
                        last = pe.matmul(bank(s, 2)[0:T, t * D:(t + 1) * D], pT[s][:, t * T:(t + 1) * T],
                                         xh[s][:, t, :], start=True, stop=True)
                    last.then_inc(o_ready[s], 1)
                for s in subs:
                    transposed(s, 2)
                for s in subs:
                    pe.wait_ge(hT_ready[s], 2 * r + 2)
                    for e in range(EXPERTS):
                        last = pe.matmul(bank(s, e // 2)[:, (e % 2) * C:(e % 2 + 1) * C], w1[:, e, :], hT[s][:],
                                         start=True, stop=True)
                    last.then_inc(h1_ready[s], 1)
                    for t in range(NT):
                        last = pe.matmul(bank(s, 3)[0:T, C + t * GF:C + (t + 1) * GF],
                                         hT[s][:, t * T:(t + 1) * T], wg[:], start=True, stop=True)
                    last.then_inc(gat_ready[s], 1)
                for s in subs:
                    pe.wait_ge(gelu_ready[s], r + 1)
                    for t in range(NT):
                        to = bank(s, 2)[0:T, t * EXPERTS * D:(t + 1) * EXPERTS * D]
                        pe.matmul(to, first[:], bias[:], start=True, stop=False, skip_group_check=True)
                        for e in range(EXPERTS):
                            last = pe.matmul(to[:, e * D:(e + 1) * D], act1[s][:, e, t * T:(t + 1) * T],
                                             w2[:, e, :], start=False, stop=(e == EXPERTS - 1),
                                             skip_group_check=True)
                    last.then_inc(eo_ready[s], 1)

        @block.vector
        def _(dve):
            dve.wait_ge(loaded, N_LOADS)
            for s in subs:
                dve.sem_inc(gh_stored[s], 16)
                dve.sem_inc(eo_stored[s], 16)
            with dve.Fori(0, ROUNDS) as r:
                ch = [Chain(dve, chain[s], STEPS, r) for s in subs]

                def normalise(nth):
                    total, var, rstd = (lambda s: stat[s][:, 0, :]), (lambda s: stat[s][:, 1, :]), \
                        (lambda s: stat[s][:, 2, :])
                    for s in subs:
                        ch[s].settle()
                        ch[s].step(dve.reduce_sum(total(s), xr[s][:], AX.X))
                    for s in subs:
                        ch[s].settle()
                        ch[s].step(dve.scalar_tensor_tensor(xc[s][:], spread(total(s), 2, D), -1.0 / D,
                                                            xr[s][:], ALU.mult, ALU.add))
                    for s in subs:
                        ch[s].settle()
                        ch[s].step(dve.tensor_tensor(sq[s][:], xc[s][:], xc[s][:], ALU.mult))
                    for s in subs:
                        ch[s].settle()
                        ch[s].step(dve.reduce_sum(total(s), sq[s][:], AX.X))
                    for s in subs:
                        ch[s].settle()
                        dve.tensor_scalar(var(s), total(s), 1.0 / D, EPS, ALU.mult, ALU.add)\
                            .then_inc(var_ready[s], 1)
                    for s in subs:
                        dve.wait_ge(rstd_ready[s], 2 * r + nth)
                        dve.tensor_tensor(xh[s][:], xc[s][:], spread(rstd(s), 2, D), ALU.mult)\
                            .then_inc(xh_ready[s], 1)

                for s in subs:
                    ch[s].step(dve.tensor_copy(xr[s][:], H[:, tiles(r, s), :]))
                normalise(1)
                for s in subs:
                    dve.wait_ge(s_ready[s], r + 1)
                    score = bank(s, 0)[0:T, 0:C].rearrange("p (n t) -> p n t", n=NT)
                    ch[s].step(dve.reduce_max(mx[s][:, 0, :], score, AX.X))
                for s in subs:
                    ch[s].settle()
                    score = bank(s, 0)[0:T, 0:C].rearrange("p (n t) -> p n t", n=NT)
                    dve.tensor_tensor(P[s][:], score, spread(mx[s][:, 0, :], 2, T), ALU.subtract)\
                        .then_inc(shifted[s], 1)
                for s in subs:
                    dve.wait_ge(exped[s], r + 1)
                    ch[s].step(dve.reduce_sum(mx[s][:, 0, :], P[s][:], AX.X))
                for s in subs:
                    ch[s].settle()
                    ch[s].step(dve.reciprocal(mx[s][:, 1, :], mx[s][:, 0, :]))
                for s in subs:
                    ch[s].settle()
                    dve.tensor_tensor(P[s][:], P[s][:], spread(mx[s][:, 1, :], 2, T), ALU.mult)\
                        .then_inc(p_ready[s], 1)
                for s in subs:
                    dve.wait_ge(o_ready[s], r + 1)
                    ch[s].step(dve.tensor_tensor(xr[s][:], xr[s][:],
                                                 bank(s, 2)[0:T, 0:NT * D].rearrange("p (n d) -> p n d", n=NT),
                                                 ALU.add))
                normalise(2)
                for s in subs:
                    ch[s].step(dve.tensor_copy(H[:, tiles(r, s), :], xr[s][:]))
                for s in subs:
                    dve.wait_ge(gat_ready[s], r + 1)
                    dve.wait_ge(gh_stored[s], 16 * (r + 1))
                    dve.tensor_copy(gh[s][:], bank(s, 3)[0:T, C:C + NT * GF].rearrange("p (n d) -> p n d", n=NT))\
                        .then_inc(gh_out[s], 1)
                for s in subs:
                    dve.wait_ge(eo_ready[s], r + 1)
                    dve.wait_ge(eo_stored[s], 16 * (r + 1))
                    dve.tensor_copy(eo[s][:], bank(s, 2)[0:T, :].rearrange("p (n d) -> p n d", n=NT))\
                        .then_inc(eo_out[s], 1)
                for s in subs:
                    ch[s].settle()
                    ch[s].close()
            dve.sem_inc(h_done, 1)


COLS = EDGES // 128
SRC_BITS = 13
KEY_TOP = 0x20000000
OUTER = 16
INNER = COLS // 8 // OUTER


def edge_rounds(eng, count, body):
    with eng.Fori(0, OUTER) as o:
        with eng.If(o * (INNER * 8) < count):
            with eng.Fori(0, INNER) as i:
                r = o * INNER + i
                with eng.If(r * 8 < count):
                    body(r)


def prepare_edges(nc, edge_index, keys_sorted, count_i, last_counts):
    HB = 8
    SUBS = 2
    STEPS = COLS // (HB * SUBS)
    subs = range(SUBS)
    with ExitStack() as ctx:
        sb, ps, sem = tools(nc, ctx)
        src = sb("src", [128, COLS], I32)
        dst = sb("dst", [128, COLS], I32)
        dst_ok = sb("dst_ok", [128, COLS])
        valid = sb("valid", [128, COLS])
        key = sb("key", [128, COLS], I32)
        keys = sb("keys", [128, COLS])
        img_i = sb("img_i", [128, COLS], I32)
        work = sb("work", [128, COLS])
        img_b = sb("img_b", [128, COLS], BF16)
        tok_b = sb("tok_b", [128, COLS], BF16)
        iota_f = sb("iota_p", [128, 128])
        iota_b = sb("iota_pb", [128, 128], BF16)
        count = sb("count", [128, 2])
        top8 = sb("top8", [128, 8])
        hot_img = [sb(f"hot_img_p{s}", [128, HB, 128], BF16) for s in subs]
        hot_tok = [sb(f"hot_tok_p{s}", [128, HB, NF], BF16) for s in subs]
        zeros = sb("zeros_p", [128, 128], BF16)
        hist = ps("hist", [128, NF])

        edges_in = sem("p_edges_in")
        iota_ready = sem("p_iota")
        zeros_ready = sem("p_zeros")
        prep = sem("p_prep")
        counted = sem("p_counted")
        count_max = sem("p_count_max")
        count_ready = sem("p_count_ready")
        sort_chain = sem("p_sort_chain")
        hot_ready = [sem(f"p_hot_ready{s}") for s in subs]
        hot_used = [sem(f"p_hot_used{s}") for s in subs]
        hist_ready = sem("p_hist_ready")
        passed = sem("p_passed")
        block = ctx.enter_context(nc.Block())

        @block.sync
        def _(sync):
            sync.dma_start(dst[:], edge_index[1].rearrange("(p n) -> p n", p=128)).then_inc(edges_in, 16)
            sync.dma_start(src[:], edge_index[0].rearrange("(p n) -> p n", p=128)).then_inc(edges_in, 16)

        @block.gpsimd
        def _(pool):
            pool.iota(iota_f[:], pattern=[[1, 128]], base=0, channel_multiplier=0,
                      allow_small_or_imprecise_dtypes=True).then_inc(iota_ready, 1)
            pool.memset(zeros[:], 0.0).then_inc(zeros_ready, 1)
            pool.wait_ge(counted, 1)
            pool.partition_all_reduce(count[:, 1:2], count[:, 0:1], 128, bass.bass_isa.ReduceOp.max)\
                .then_inc(count_max, 1)

        @block.tensor
        def _(pe):
            pe.wait_ge(zeros_ready, 1)
            pe.matmul(hist[:], zeros[:], zeros[:, 0:NF], start=True, stop=False, skip_group_check=True)
            with pe.Fori(0, STEPS) as n:
                for s in subs:
                    pe.wait_ge(hot_ready[s], n + 1)
                    for k in range(HB):
                        last = pe.matmul(hist[:], hot_img[s][:, k, :], hot_tok[s][:, k, :],
                                         start=False, stop=False, skip_group_check=True)
                    last.then_inc(hot_used[s], 1)
            pe.matmul(hist[:], zeros[:], zeros[:, 0:NF], start=False, stop=True, skip_group_check=True)\
                .then_inc(hist_ready, 1)

        @block.vector
        def _(dve):
            ch = Chain(dve, prep, 15, 0)
            dve.wait_ge(iota_ready, 1)
            ch.step(dve.tensor_copy(iota_b[:], iota_f[:]))
            dve.wait_ge(edges_in, 32)
            ch.step(dve.tensor_scalar(dst_ok[:], dst[:], float(NODES), None, ALU.is_lt))
            ch.step(dve.tensor_scalar(work[:], src[:], float(NODES - 1), None, ALU.is_lt))
            ch.step(dve.tensor_scalar(key[:], dst[:], SRC_BITS, KEY_TOP, ALU.logical_shift_left, ALU.bitwise_or))
            ch.step(dve.tensor_scalar(img_i[:], dst[:], -float(NF // 2), 1.0 / NF, ALU.add, ALU.mult))
            ch.step(dve.memset(keys_sorted[:], 0.0))
            ch.settle()
            ch.step(dve.tensor_tensor(valid[:], dst_ok[:], work[:], ALU.mult))
            ch.step(dve.tensor_tensor(key[:], key[:], src[:], ALU.bitwise_or))
            ch.step(dve.scalar_tensor_tensor(tok_b[:], img_i[:], -float(NF), dst[:], ALU.mult, ALU.add))
            ch.settle()
            dve.reduce_sum(count[:, 0:1], valid[:], AX.X).then_inc(counted, 1)
            ch.step(dve.tensor_tensor(keys[:], key[:].bitcast(F32), valid[:], ALU.mult))
            ch.step(dve.tensor_tensor(work[:], dst_ok[:], valid[:], ALU.subtract))
            ch.settle()
            ch.step(dve.scalar_tensor_tensor(valid[:], work[:], -256.0, img_i[:], ALU.mult, ALU.add))
            ch.settle()
            ch.step(dve.tensor_scalar(img_b[:], valid[:], 256.0, None, ALU.add))
            dve.wait_ge(count_max, 1)
            ch.step(dve.tensor_copy(count_i[:], count[:, 1:2]))
            ch.settle()
            ch.step(dve.memset(top8[:], 0.0))
            ch.settle()
            ch.close()
            for s in subs:
                dve.sem_inc(hot_used[s], 1)
            with dve.Fori(0, STEPS) as n:
                for s in subs:
                    at = bass.ds((n * SUBS + s) * HB, HB)
                    dve.wait_ge(hot_used[s], n + 1)
                    dve.tensor_tensor(hot_img[s][:], spread(img_b[:, at], 2, 128), spread(iota_b[:], 1, HB),
                                      ALU.is_equal)
                    dve.tensor_tensor(hot_tok[s][:], spread(tok_b[:, at], 2, NF), spread(iota_b[:, 0:NF], 1, HB),
                                      ALU.is_equal).then_inc(hot_ready[s], 1)
            edges_left = dve.value_load(count_i[0:1, 0:1], min_val=0, max_val=COLS)

            dve.sem_inc(sort_chain, 1)

            def sort_round(r):
                c = Chain(dve, sort_chain, 3, r, before=1)
                c.settle()
                dve.sem_inc(passed, 1)
                c.step(dve.max(top8[:], keys[:]))
                c.settle()
                c.step(dve.tensor_copy(keys_sorted[:, bass.ds(r * 8, 8)], top8[:]))
                c.step(dve.match_replace(keys[:], top8[:], keys[:], 0.0))
                c.close()

            edge_rounds(dve, edges_left, sort_round)
            dve.wait_ge(hist_ready, 1)
            dve.tensor_copy(last_counts[:], hist[:]).then_inc(count_ready, 1)
            dve.wait_ge(count_ready, 1)


def route_edges(nc, keys_sorted, count_i, last_counts, gat_h, att_src, att_dst, src_table, dst_table, agg):
    TF = GF + GH
    DF = 2 * GH
    BT = 4
    SUBS = 2
    HALF = (NF + 1) // 2
    SLOPE = 0.2
    subs = range(SUBS)
    with ExitStack() as ctx:
        sb, ps, sem = tools(nc, ctx)
        h_nodes = sb("h_nodes", [128, NF, GF])
        att = sb("att", [128, 2, GF])
        prod = sb("prod", [128, NF, GF])
        src_rows = sb("src_rows", [128, NF, TF])
        dst_rows = sb("dst_rows", [128, NF, DF])
        top = sb("top", [128, 2, GH])
        last_row = sb("last_row", [128, TF])
        z = sb("z_r", [128, 2, NF, GH])
        dense = sb("dense", [128, NF, TF])
        zeros = sb("zeros_r", [128, 512])
        img_i = sb("img_i_r", [128, COLS], I32)
        node_i = sb("node_i", [128, COLS, 2], I32)
        img = sb("img_r", [128, COLS])
        tok = sb("tok_r", [128, COLS])
        iota_f = sb("iota_r", [128, 128])
        node8 = [sb(f"node8_{s}", [128, BT, 2], I32) for s in subs]
        from_src = [sb(f"from_src{s}", [128, BT, TF]) for s in subs]
        from_dst = [sb(f"from_dst{s}", [128, BT, DF]) for s in subs]
        logit = [sb(f"logit{s}", [128, 2, BT, GH]) for s in subs]
        val = [sb(f"val{s}", [128, BT, TF]) for s in subs]
        hot_img = [sb(f"hot_img_r{s}", [128, BT, 128]) for s in subs]
        hot_tok = [sb(f"hot_tok_r{s}", [128, BT, NF]) for s in subs]
        spread_val = [sb(f"spread_val{s}", [128, BT, NF * TF]) for s in subs]
        acc = ps("acc_r", [128, 2, 512])

        nodes_in = sem("r_nodes_in")
        prep = sem("r_prep")
        top_ready = sem("r_top_ready")
        top_all = sem("r_top_all")
        rows_ready = sem("r_rows_ready")
        rows_stored = sem("r_rows_stored")
        last_in = sem("r_last_in")
        dense_logit = sem("r_dense_logit")
        dense_exp = sem("r_dense_exp")
        dense_ready = sem("r_dense_ready")
        iota_ready = sem("r_iota")
        decode = sem("r_decode")
        decoded = sem("r_decoded")
        copied = [sem(f"r_copied{s}") for s in subs]
        src_in = [sem(f"r_src_in{s}") for s in subs]
        dst_in = [sem(f"r_dst_in{s}") for s in subs]
        rows_used = [sem(f"r_rows_used{s}") for s in subs]
        chain = [sem(f"r_chain{s}") for s in subs]
        logit_ready = [sem(f"r_logit{s}") for s in subs]
        exp_ready = [sem(f"r_exp{s}") for s in subs]
        batch_ready = [sem(f"r_batch{s}") for s in subs]
        batch_used = [sem(f"r_batch_used{s}") for s in subs]
        sums_ready = sem("r_sums_ready")
        passed = sem("r_passed")
        sums_read = sem("r_sums_read")
        block = ctx.enter_context(nc.Block())

        by_node = lambda t: t.rearrange("(b t) f -> b t f", t=NF)

        @block.sync
        def _(sync):
            sync.dma_start(h_nodes[:], by_node(gat_h)).then_inc(nodes_in, 16)
            for n, a in enumerate((att_src, att_dst)):
                sync.dma_start(att[:, n, :], a.rearrange("h e -> (h e)").partition_broadcast(128))\
                    .then_inc(nodes_in, 16)
            sync.wait_ge(rows_ready, 1)
            sync.dma_start(by_node(src_table), src_rows[:]).then_inc(rows_stored, 16)
            sync.dma_start(by_node(dst_table), dst_rows[:]).then_inc(rows_stored, 16)
            sync.wait_ge(rows_stored, 32)
            sync.dma_start(last_row[:], src_table[NODES - 1].partition_broadcast(128)).then_inc(last_in, 16)

        @block.gpsimd
        def _(pool):
            pool.iota(iota_f[:], pattern=[[1, 128]], base=0, channel_multiplier=0,
                      allow_small_or_imprecise_dtypes=True).then_inc(iota_ready, 1)
            pool.wait_ge(top_ready, 1)
            pool.partition_all_reduce(top[:, 1, :], top[:, 0, :], 128, bass.bass_isa.ReduceOp.max)\
                .then_inc(top_all, 1)
            pool.wait_ge(rows_stored, 32)
            pool.wait_ge(decoded, 1)
            count = pool.value_load(count_i[0:1, 0:1], min_val=0, max_val=COLS)
            for s in subs:
                pool.sem_inc(rows_used[s], 1)

            def gather(r):
                for s in subs:
                    pool.wait_ge(rows_used[s], r + 1)
                    pool.sem_inc(passed, 1)
                    pool.tensor_copy(node8[s][:], node_i[:, bass.ds(r * (BT * SUBS) + s * BT, BT), :])\
                        .then_inc(copied[s], 1)
                    pool.wait_ge(copied[s], r + 1)
                    pool.sem_inc(passed, 1)
                    for k in range(BT):
                        pool.indirect_dma_start(
                            from_src[s][:, k, :], None, src_table,
                            bass.IndirectOffsetOnAxis(ap=node8[s][:, k, 0:1].bitcast(U32), axis=0))\
                            .then_inc(src_in[s], 16)
                        pool.indirect_dma_start(
                            from_dst[s][:, k, :], None, dst_table,
                            bass.IndirectOffsetOnAxis(ap=node8[s][:, k, 1:2].bitcast(U32), axis=0))\
                            .then_inc(dst_in[s], 16)
            edge_rounds(pool, count, gather)

        @block.scalar
        def _(act):
            act.wait_ge(dense_logit, 1)
            act.activation(z[:], z[:], ACT.Exp).then_inc(dense_exp, 1)
            act.wait_ge(decoded, 1)
            count = act.value_load(count_i[0:1, 0:1], min_val=0, max_val=COLS)

            def exps(r):
                for s in subs:
                    act.wait_ge(logit_ready[s], r + 1)
                    act.activation(val[s][:, :, GF:TF], logit[s][:, 1, :, :], ACT.Exp).then_inc(exp_ready[s], 1)
            edge_rounds(act, count, exps)

        @block.tensor
        def _(pe):
            pe.wait_ge(decoded, 1)
            for n, width in enumerate((HALF * TF, (NF - HALF) * TF)):
                pe.matmul(acc[:, n, 0:width], zeros[:, 0:128], zeros[:, 0:width],
                          start=True, stop=False, skip_group_check=True)
            count = pe.value_load(count_i[0:1, 0:1], min_val=0, max_val=COLS)

            def sums(r):
                for s in subs:
                    pe.wait_ge(batch_ready[s], r + 1)
                    for k in range(BT):
                        pe.matmul(acc[:, 0, 0:HALF * TF], hot_img[s][:, k, :],
                                  spread_val[s][:, k, 0:HALF * TF], start=False, stop=False, skip_group_check=True)
                        last = pe.matmul(acc[:, 1, 0:(NF - HALF) * TF], hot_img[s][:, k, :],
                                         spread_val[s][:, k, HALF * TF:NF * TF], start=False, stop=False,
                                         skip_group_check=True)
                    last.then_inc(batch_used[s], 1)
            edge_rounds(pe, count, sums)
            for n, width in enumerate((HALF * TF, (NF - HALF) * TF)):
                last = pe.matmul(acc[:, n, 0:width], zeros[:, 0:128], zeros[:, 0:width],
                                 start=False, stop=True, skip_group_check=True)
            last.then_inc(sums_ready, 1)

        @block.vector
        def _(dve):
            ch = Chain(dve, decode, 7, 0)
            keys_i = keys_sorted[:].bitcast(I32)
            low = (1 << SRC_BITS) - 1
            source, target = node_i[:, :, 0], node_i[:, :, 1]
            ch.step(dve.memset(zeros[:], 0.0))
            ch.step(dve.tensor_scalar(source, keys_i, low, None, ALU.bitwise_and))
            ch.step(dve.tensor_scalar(target, keys_i, SRC_BITS, low, ALU.logical_shift_right, ALU.bitwise_and))
            ch.step(dve.tensor_scalar(img[:], keys_sorted[:], 0.0, 256.0, ALU.is_equal, ALU.mult))
            ch.settle()
            ch.step(dve.tensor_scalar(img_i[:], target, -float(NF // 2), 1.0 / NF, ALU.add, ALU.mult))
            ch.settle()
            ch.step(dve.scalar_tensor_tensor(tok[:], img_i[:], -float(NF), target, ALU.mult, ALU.add))
            ch.step(dve.tensor_tensor(img[:], img[:], img_i[:], ALU.add))
            ch.settle()
            ch.close()
            dve.sem_inc(decoded, 1)

            ch = Chain(dve, prep, 12, 0)
            split = lambda t: t.rearrange("p t (h e) -> p t h e", e=EXPERTS)
            a_src, a_dst, bound = src_rows[:, :, GF:TF], dst_rows[:, :, 0:GH], dst_rows[:, :, GH:DF]
            dve.wait_ge(nodes_in, 48)
            ch.step(dve.tensor_copy(src_rows[:, :, 0:GF], h_nodes[:]))
            for n, to in enumerate((a_src, a_dst)):
                ch.settle()
                ch.step(dve.tensor_tensor(prod[:], h_nodes[:], spread(att[:, n, :], 1, NF), ALU.mult))
                ch.settle()
                ch.step(dve.reduce_sum(to, split(prod[:]), AX.X))
            ch.settle()
            dve.reduce_max(top[:, 0, :], a_src.rearrange("p t h -> p h t"), AX.X).then_inc(top_ready, 1)
            ch.step(dve.tensor_tensor(z[:, 0, :, :], a_src, a_dst, ALU.add))
            dve.wait_ge(top_all, 1)
            raw_bound = prod[:, :, 0:GH]
            ch.step(dve.tensor_tensor(raw_bound, a_dst, spread(top[:, 1, :], 1, NF), ALU.add))
            ch.settle()
            dve.scalar_tensor_tensor(bound, raw_bound, SLOPE, raw_bound, ALU.mult, ALU.max).then_inc(rows_ready, 1)
            dve.wait_ge(last_in, 16)
            ch.step(dve.tensor_tensor(z[:, 1, :, :], a_dst, spread(last_row[:, GF:TF], 1, NF), ALU.add))
            ch.settle()
            z_flat = z[:].rearrange("p n t h -> p (n t h)")
            ch.step(dve.scalar_tensor_tensor(z_flat, z_flat, SLOPE, z_flat, ALU.mult, ALU.max))
            dve.wait_ge(rows_ready, 1)
            ch.settle()
            dve.tensor_tensor(z[:], z[:], spread(bound, 1, 2), ALU.subtract).then_inc(dense_logit, 1)
            dve.wait_ge(dense_exp, 1)
            ch.step(dve.tensor_tensor(z[:, 1, :, :], z[:, 1, :, :], spread(last_counts[:], 2, GH), ALU.mult))
            ch.settle()
            ch.step(dve.tensor_tensor(split(dense[:, :, 0:GF]), split(h_nodes[:]),
                                      spread(z[:, 0, :, :], 3, EXPERTS), ALU.mult))
            ch.step(dve.tensor_tensor(split(prod[:]), spread(z[:, 1, :, :], 3, EXPERTS),
                                      spread(last_row[:, 0:GF].rearrange("p (h e) -> p h e", e=EXPERTS), 1, NF),
                                      ALU.mult))
            ch.close()
            ch.settle()
            dve.tensor_tensor(dense[:, :, 0:GF], dense[:, :, 0:GF], prod[:], ALU.add)
            dve.tensor_tensor(dense[:, :, GF:TF], z[:, 0, :, :], z[:, 1, :, :], ALU.add).then_inc(dense_ready, 1)

            dve.wait_ge(iota_ready, 1)
            count = dve.value_load(count_i[0:1, 0:1], min_val=0, max_val=COLS)
            for s in subs:
                dve.sem_inc(batch_used[s], 1)

            def batches(r):
                c = [Chain(dve, chain[s], 4, r) for s in subs]
                for s in subs:
                    dve.wait_ge(src_in[s], 16 * BT * (r + 1))
                    dve.wait_ge(dst_in[s], 16 * BT * (r + 1))
                    c[s].step(dve.tensor_tensor(logit[s][:, 0, :, :], from_src[s][:, :, GF:TF],
                                                from_dst[s][:, :, 0:GH], ALU.add))
                for s in subs:
                    c[s].settle()
                    c[s].step(dve.scalar_tensor_tensor(logit[s][:, 1, :, :], logit[s][:, 0, :, :], SLOPE,
                                                       logit[s][:, 0, :, :], ALU.mult, ALU.max))
                for s in subs:
                    c[s].settle()
                    dve.tensor_tensor(logit[s][:, 1, :, :], logit[s][:, 1, :, :], from_dst[s][:, :, GH:DF],
                                      ALU.subtract).then_inc(logit_ready[s], 1)
                for s in subs:
                    at = bass.ds(r * (BT * SUBS) + s * BT, BT)
                    dve.wait_ge(batch_used[s], r + 1)
                    c[s].step(dve.tensor_tensor(hot_img[s][:], spread(img[:, at], 2, 128),
                                                spread(iota_f[:], 1, BT), ALU.is_equal))
                    c[s].step(dve.tensor_tensor(hot_tok[s][:], spread(tok[:, at], 2, NF),
                                                spread(iota_f[:, 0:NF], 1, BT), ALU.is_equal))
                for s in subs:
                    dve.wait_ge(exp_ready[s], r + 1)
                    dve.tensor_tensor(split(val[s][:, :, 0:GF]), split(from_src[s][:, :, 0:GF]),
                                      spread(val[s][:, :, GF:TF], 3, EXPERTS), ALU.mult).then_inc(rows_used[s], 1)
                for s in subs:
                    dve.wait_ge(rows_used[s], r + 2)
                    c[s].settle()
                    dve.tensor_tensor(spread_val[s][:].rearrange("p k (t f) -> p k t f", f=TF),
                                      spread(hot_tok[s][:], 3, TF), spread(val[s][:], 2, NF), ALU.mult)\
                        .then_inc(batch_ready[s], 1)
                    c[s].close()
            edge_rounds(dve, count, batches)
            dve.wait_ge(dense_ready, 1)
            dve.wait_ge(sums_ready, 1)
            for n, at in enumerate((slice(0, HALF), slice(HALF, NF))):
                width = at.stop - at.start
                dve.tensor_tensor(agg[:, at, :], acc[:, n, 0:width * TF].rearrange("p (t f) -> p t f", f=TF),
                                  dense[:, at, :], ALU.add).then_inc(sums_read, 1)
            dve.wait_ge(sums_read, 2)


def mix_experts(nc, agg, hidden, expert_out, b_gat, gamma, beta, out):
    TF = GF + GH
    with ExitStack() as ctx:
        sb, ps, sem = tools(nc, ctx)
        hid = sb("hid", [128, NF, D])
        eo = sb("eo_m", [128, NF, EXPERTS * D])
        part = [sb(f"part{n}", [128, NF, D]) for n in range(2)]
        rows = sb("rows_m", [128, 3, GF])
        den = sb("den", [128, NF, GH])
        y = sb("y_m", [128, NF, GF])
        y2 = sb("y2_m", [128, NF, GF])
        stat = sb("stat_m", [128, 4, NF])
        half = sb("half_m", [128, NF])
        score = sb("score", [128, NF, EXPERTS])
        rank = sb("rank", [128, NF, EXPERTS])
        better = sb("better", [128, NF])
        gate = sb("gate", [128, NF, EXPERTS])
        rows_in = sem("m_rows_in")
        hid_in = sem("m_hid_in")
        eo_in = sem("m_eo_in")
        half_set = sem("m_half_set")
        var_ready = sem("m_var")
        rstd_ready = sem("m_rstd")
        shifted = sem("m_shifted")
        exped = sem("m_exped")
        chain = sem("m_chain")
        out_parts = sem("m_out_parts")
        out_ready = sem("m_out_ready")
        stored = sem("m_stored")
        block = ctx.enter_context(nc.Block())
        by_node = lambda t: t.rearrange("(b t) f -> b t f", t=NF)

        @block.sync
        def _(sync):
            for n, row in enumerate((b_gat, gamma, beta)):
                sync.dma_start(rows[:, n, :], row.partition_broadcast(128)).then_inc(rows_in, 16)
            sync.dma_start(hid[:], by_node(hidden)).then_inc(hid_in, 16)
            sync.dma_start(eo[:], by_node(expert_out)).then_inc(eo_in, 16)
            sync.wait_ge(out_ready, 1)
            sync.dma_start(out, hid[:]).then_inc(stored, 16)
            sync.wait_ge(stored, 16)

        @block.gpsimd
        def _(pool):
            pool.memset(half[:], -0.5).then_inc(half_set, 1)
            pool.wait_ge(half_set, 1)
            pool.wait_ge(var_ready, 1)
            pool.tensor_tensor(stat[:, 2, :], stat[:, 1, :], half[:], ALU.pow).then_inc(rstd_ready, 1)

        @block.scalar
        def _(act):
            act.wait_ge(shifted, 1)
            act.activation(gate[:], gate[:], ACT.Exp).then_inc(exped, 1)

        @block.vector
        def _(dve):
            ch = Chain(dve, chain, 41, 0)

            def then(ins):
                ch.step(ins)
                ch.settle()

            split = lambda t: t.rearrange("p t (h e) -> p t h e", e=EXPERTS)
            total, var, rstd, mean = (stat[:, n, :] for n in range(4))
            then(dve.tensor_scalar(den[:], agg[:, :, GF:TF], 1e-16, None, ALU.add))
            then(dve.reciprocal(den[:], den[:]))
            then(dve.tensor_tensor(split(y[:]), split(agg[:, :, 0:GF]), spread(den[:], 3, EXPERTS), ALU.mult))
            dve.wait_ge(rows_in, 48)
            then(dve.tensor_tensor(y[:], y[:], spread(rows[:, 0, :], 1, NF), ALU.add))
            then(dve.reduce_sum(total, y[:], AX.X))
            then(dve.scalar_tensor_tensor(y2[:], spread(total, 2, GF), -1.0 / GF, y[:], ALU.mult, ALU.add))
            then(dve.tensor_tensor(y[:], y2[:], y2[:], ALU.mult))
            then(dve.reduce_sum(total, y[:], AX.X))
            dve.tensor_scalar(var, total, 1.0 / GF, EPS, ALU.mult, ALU.add).then_inc(var_ready, 1)
            dve.wait_ge(rstd_ready, 1)
            then(dve.tensor_tensor(y[:], y2[:], spread(rstd, 2, GF), ALU.mult))
            then(dve.tensor_tensor(y2[:], y[:], spread(rows[:, 1, :], 1, NF), ALU.mult))
            then(dve.tensor_tensor(y[:], y2[:], spread(rows[:, 2, :], 1, NF), ALU.add))
            then(dve.reduce_sum(score[:], y[:].rearrange("p t (h e) -> p t e h", e=EXPERTS), AX.X))
            then(dve.tensor_scalar(score[:], score[:], 1.0 / GH, None, ALU.mult))
            for e in range(EXPERTS):
                then(dve.memset(rank[:, :, e], float(e)))
            for e in range(EXPERTS):
                for j in range(e):
                    then(dve.tensor_tensor(better[:], score[:, :, e], score[:, :, j], ALU.is_gt))
                    then(dve.tensor_tensor(rank[:, :, j], rank[:, :, j], better[:], ALU.add))
                    then(dve.tensor_tensor(rank[:, :, e], rank[:, :, e], better[:], ALU.subtract))
            then(dve.reduce_max(mean, score[:], AX.X))
            dve.tensor_tensor(gate[:], score[:], spread(mean, 2, EXPERTS), ALU.subtract).then_inc(shifted, 1)
            dve.wait_ge(exped, 1)
            then(dve.tensor_scalar(rank[:], rank[:], 1.5, None, ALU.is_lt))
            then(dve.tensor_tensor(gate[:], gate[:], rank[:], ALU.mult))
            then(dve.reduce_sum(total, gate[:], AX.X))
            then(dve.reciprocal(var, total))
            then(dve.tensor_tensor(gate[:], gate[:], spread(var, 2, EXPERTS), ALU.mult))
            dve.wait_ge(hid_in, 16)
            dve.wait_ge(eo_in, 16)
            ch.close()
            for e in range(EXPERTS):
                dve.tensor_tensor(part[e % 2][:], eo[:, :, e * D:(e + 1) * D], spread(gate[:, :, e], 2, D), ALU.mult)\
                    .then_inc(out_parts, 1)
                dve.wait_ge(out_parts, 2 * e + 1)
                dve.tensor_tensor(hid[:], hid[:], part[e % 2][:], ALU.add).then_inc(out_parts, 1)
                dve.wait_ge(out_parts, 2 * e + 2)
            dve.sem_inc(out_ready, 1)



def early_fusion(nc, x, txt, ln1_g, ln1_b, W_patch, b_patch, ln2_g, ln2_b, cls, pos, attn_g, attn_b, Wqkv, Wo, bo,
                 ff_g, ff_b, W1, b1, W2, b2, f_g, f_b, gat_w, att_src, att_dst, b_gat, gamma, beta, eW1, eb1, eW2,
                 eb2, edge_index, out):
    def scratch(name, shape):
        return nc.dram_tensor(name, shape, F32).ap()

    tokens = scratch("tokens", (B * NV, D))
    fused = scratch("fused", (NODES, D))
    hidden = scratch("hidden", (NODES, D))
    gat_h = scratch("gat_h", (NODES, GF))
    expert_out = scratch("expert_out", (NODES, EXPERTS * D))
    src_table = scratch("src_table", (NODES, GF + GH))
    dst_table = scratch("dst_table", (NODES, 2 * GH))
    with ExitStack() as ctx:
        sb, _, _ = tools(nc, ctx)
        keys_sorted = sb("keys_sorted", [128, COLS])
        count_i = sb("count_i", [128, 1], I32)
        last_counts = sb("last_counts", [128, NF])
        agg = sb("agg", [128, NF, GF + GH])
        prepare_edges(nc, edge_index, keys_sorted, count_i, last_counts)
        embed_patches(nc, x, ln1_g, ln1_b, W_patch, b_patch, ln2_g, ln2_b, cls, pos, tokens)
        run_vit(nc, tokens, attn_g, attn_b, Wqkv, Wo, bo, ff_g, ff_b, W1, b1, W2, b2, f_g, f_b, txt, fused)
        fuse_and_expert(nc, fused, gat_w, eW1, eb1, eW2, eb2, hidden, gat_h, expert_out)
        route_edges(nc, keys_sorted, count_i, last_counts, gat_h, att_src, att_dst, src_table, dst_table, agg)
        mix_experts(nc, agg, hidden, expert_out, b_gat, gamma, beta, out)


_INS = ['x', 'txt', 'L0_tok_ln_p1_g', 'L0_tok_ln_p1_b', 'L0_tok_W_patch', 'L0_tok_b_patch',
        'L0_tok_ln_p2_g', 'L0_tok_ln_p2_b', 'L0_tok_cls', 'L0_tok_pos', 'L0_tok_attn_ln_g',
        'L0_tok_attn_ln_b', 'L0_tok_Wqkv', 'L0_tok_Wo', 'L0_tok_bo', 'L0_tok_ff_ln_g', 'L0_tok_ff_ln_b',
        'L0_tok_W1', 'L0_tok_b1', 'L0_tok_W2', 'L0_tok_b2', 'L0_tok_ln_f_g', 'L0_tok_ln_f_b',
        'L0_ffn_W_gat', 'L0_ffn_att_src', 'L0_ffn_att_dst', 'L0_ffn_b_gat', 'L0_ffn_ln_gamma',
        'L0_ffn_ln_beta', 'L0_ffn_W1', 'L0_ffn_b1', 'L0_ffn_W2', 'L0_ffn_b2', 'L0_ffn_edge_index']
_OUTS = [((B, NF, D), 'float32')]


def kernel(**inputs):
    import numpy as _np
    import concourse.bacc as _bacc
    from concourse import mybir as _mybir
    from concourse.bass_utils import run_bass_kernel_spmd as _run

    nc = _bacc.Bacc("TRN2", target_bir_lowering=False, num_devices=1)
    arrays, args = {}, []
    for name in _INS:
        a = _np.ascontiguousarray(inputs[name])
        arrays[f"in_{name}_dram"] = a
        args.append(nc.dram_tensor(f"in_{name}_dram", a.shape, _mybir.dt.from_np(a.dtype), kind="ExternalInput").ap())
    for i, (shape, dtype) in enumerate(_OUTS):
        dt = _mybir.dt.from_np(_np.dtype(dtype))
        args.append(nc.dram_tensor(f"out_{i}_dram", shape, dt, kind="ExternalOutput").ap())
    early_fusion(nc, *args)
    r = _run(nc, [arrays], core_ids=[0])
    got = tuple(r.results[0][f"out_{i}_dram"] for i in range(len(_OUTS)))
    return got[0]
```

```python
from contextlib import ExitStack

import concourse.bass as bass
from concourse import mybir

F32 = mybir.dt.float32
I32 = mybir.dt.int32
U32 = mybir.dt.uint32
BF16 = mybir.dt.bfloat16
ALU = mybir.AluOpType
ACT = mybir.ActivationFunctionType
AX = mybir.AxisListType

B = 128
IMG = 128
PATCH = 32
GRID = IMG // PATCH
CH = 3
PD = CH * PATCH * PATCH
D = 64
NV = GRID * GRID + 1
NTXT = 32
NF = NV + NTXT
LAYERS = 4
HEADS = 4
DH = 64
MLP = 128
EXPERTS = 4
GH = 4
GF = GH * EXPERTS
NODES = B * NF
EDGES = 262144
EPS = 1e-5
MASK = 32768.0


class Chain:

    def __init__(self, eng, sem, per_round, round_no, before=0):
        self.eng, self.sem, self.per_round, self.round_no, self.n = eng, sem, per_round, round_no, 0
        self.before = before

    def step(self, ins):
        ins.then_inc(self.sem, 1)
        self.n += 1

    def settle(self):
        self.eng.wait_ge(self.sem, self.round_no * self.per_round + (self.before + self.n))

    def close(self):
        assert self.n == self.per_round, self.n


def wait_apart(eng, sem, value, passed):
    eng.wait_ge(sem, value)
    eng.sem_inc(passed, 1)


def spread(ap, at, count):
    shape = list(ap.shape)
    shape.insert(at, count)
    return ap.unsqueeze(at).to_broadcast(shape)


def tools(nc, ctx):
    sems = []

    def give_back():
        if sems:
            nc.clear_and_free_semaphores(sems)
            nc.all_engine_barrier()

    ctx.callback(give_back)

    def sb(name, shape, dt=F32):
        return ctx.enter_context(nc.sbuf_tensor(name, shape, dt))

    def ps(name, shape, dt=F32):
        return ctx.enter_context(nc.psum_tensor(name, shape, dt))

    def sem(name):
        sems.append(nc.alloc_semaphore(name))
        return sems[-1]

    return sb, ps, sem


def block_masks(pool, done, images, tokens, left, right):
    n = 0
    for mask, scale in ((left, 1.0), (right, MASK)):
        reps = mask.shape[1]
        pattern = [[0, reps], [1, images * tokens]]
        used = mask[0:images + 1]
        pool.memset(mask, 0.0).then_inc(done, 1)
        pool.wait_ge(done, n + 1)
        pool.memset(used, scale).then_inc(done, 1)
        pool.wait_ge(done, n + 2)
        pool.affine_select(out=used, in_=used, compare_op=ALU.is_ge, fill=0.0, base=tokens,
                           pattern=pattern, channel_multiplier=-tokens).then_inc(done, 1)
        pool.wait_ge(done, n + 3)
        pool.affine_select(out=used, in_=used, compare_op=ALU.is_ge, fill=0.0, base=-1,
                           pattern=[[0, reps], [-1, images * tokens]], channel_multiplier=tokens).then_inc(done, 1)
        pool.wait_ge(done, n + 4)
        pool.memset(mask[0:1], 1.0 if scale == 1.0 else -MASK).then_inc(done, 1)
        n += 5
    return n


def identity(pool, done, n, ident):
    pool.memset(ident, 0.0).then_inc(done, 1)
    pool.wait_ge(done, n + 1)
    pool.affine_select(out=ident, in_=ident, compare_op=ALU.not_equal, fill=1.0, base=0,
                       pattern=[[-1, ident.shape[1]]], channel_multiplier=1).then_inc(done, 1)
    return n + 2


COLS = EDGES // 128
SRC_BITS = 13
IMG_BITS = 7
KEY_TOP = 0x20000000
BLOCKS = 8
INNER = COLS // 8 // BLOCKS


def edge_block(eng, count, o, body):
    with eng.If(o * (INNER * 8) < count):
        with eng.Fori(0, INNER) as i:
            r = o * INNER + i
            with eng.If(r * 8 < count):
                body(r)


def edge_rounds(eng, count, body):
    with eng.Fori(0, BLOCKS) as o:
        edge_block(eng, count, o, body)


def embed_and_sort(nc, x, ln1_g, ln1_b, W, b_patch, ln2_g, ln2_b, cls, pos, tokens, edge_index, keys_sorted,
                   count_i, last_counts):
    GI = 16
    NG = B // GI
    K = CH * PATCH
    NP = GRID * GRID
    GP = GI * NP
    WN = D + 2
    PT = NG * GP // 128
    PREP = 4
    EPI = 12
    HB = 8
    HIST = COLS // HB // 2
    EDGE_PREP = 17
    two = range(2)
    with ExitStack() as ctx:
        sb, ps, sem = tools(nc, ctx)
        pix = [sb(f"pix{s}", [K, GP * PATCH]) for s in two]
        squares = sb("squares", [K, GP * PATCH])
        w_raw = sb("w_raw", [K, PATCH, D])
        w_ext = sb("w_ext", [K, PATCH, WN])
        w_bias = sb("w_bias", [K, PATCH, D])
        g_in = sb("g_in", [K, PATCH])
        b_in = sb("b_in", [K, PATCH])
        w_sum = sb("w_sum", [K, 2, D])
        pick_sq = sb("pick_sq", [K, WN])
        ones = sb("ones_e", [128, 128])
        ident = sb("ident_e", [WN, WN])
        col_sum = sb("col_sum", [128, D])
        const = sb("const", [128, D])
        rows = sb("rows_e", [128, 3, D])
        posP = sb("posP", [128, D])
        cls_t = sb("cls_t", [1, 2, D])
        cls_all = sb("cls_all", [128, D])
        stat = sb("stat_e", [128, 4, PT])
        half = sb("half_e", [128, PT])
        accT = sb("accT", [WN, NG * GP])
        y = sb("y_e", [128, PT, D])
        y2 = sb("y2_e", [128, PT, D])
        acc = [ps(f"acc_e{s}", [WN, 512]) for s in two]
        turned = ps("turned_e", [128, PT, 128])
        aux = ps("aux_e", [128, 3, D])
        src = sb("src", [128, COLS], I32)
        dst = sb("dst", [128, COLS], I32)
        dst_ok = sb("dst_ok", [128, COLS])
        keys = sb("keys", [128, COLS])
        img_i = sb("img_i", [128, COLS], I32)
        img_b = sb("img_b", [128, COLS], BF16)
        tok_b = sb("tok_b", [128, COLS], BF16)
        iota_i = sb("iota_i", [128, 128], I32)
        iota_b = sb("iota_pb", [128, 128, HB], BF16)
        count = sb("count", [128, 2])
        top8 = sb("top8", [128, 8])
        hot_img = [sb(f"hot_img_p{s}", [128, 128, HB], BF16) for s in two]
        hot_tok = [sb(f"hot_tok_p{s}", [128, NF, HB], BF16) for s in two]
        zeros = sb("zeros_p", [128, 128], BF16)
        hist = ps("hist", [128, NF])

        params_in = sem("e_params_in")
        pix_in = [sem(f"e_pix_in{s}") for s in two]
        pix_used = [sem(f"e_pix_used{s}") for s in two]
        squared = sem("e_squared")
        squares_used = sem("e_squares_used")
        consts_set = sem("e_consts_set")
        ident_set = sem("e_ident_set")
        pick_set = sem("e_pick_set")
        w_ready = sem("e_w_ready")
        w_here = sem("e_w_here")
        sums_ready = sem("e_sums_ready")
        cls_done = sem("e_cls_done")
        prep = sem("e_prep")
        acc_ready = [sem(f"e_acc_ready{s}") for s in two]
        acc_read = [sem(f"e_acc_read{s}") for s in two]
        turned_ready = sem("e_turned_ready")
        turned_read = sem("e_turned_read")
        var_ready = sem("e_var_ready")
        rstd_ready = sem("e_rstd_ready")
        chain_sem = sem("e_chain")
        y_ready = sem("e_y_ready")
        out_ready = sem("e_out_ready")
        stored = sem("e_stored")
        edges_in = sem("p_edges_in")
        iota_ready = sem("p_iota")
        zeros_ready = sem("p_zeros")
        edge_prep = sem("p_prep")
        counted = sem("p_counted")
        count_max = sem("p_count_max")
        count_ready = sem("p_count_ready")
        sort_chain = sem("p_sort_chain")
        hot_ready = [sem(f"p_hot_ready{s}") for s in two]
        hot_used = [sem(f"p_hot_used{s}") for s in two]
        hist_ready = sem("p_hist_ready")
        passed = sem("p_passed")
        block = ctx.enter_context(nc.Block())

        tok_view = tokens[0:B * NV, :].rearrange("(b t) d -> b t d", t=NV)
        per_patch = "(c i j) -> (c i) j"
        N_PARAMS = 16 * (3 + 3 + 128 // NP + 2)

        @block.sync
        def _(sync):
            sync.dma_start(dst[:], edge_index[1].rearrange("(p n) -> p n", p=128)).then_inc(edges_in, 16)
            sync.dma_start(src[:], edge_index[0].rearrange("(p n) -> p n", p=128)).then_inc(edges_in, 16)
            sync.dma_start(w_raw[:], W.rearrange("(c i j) d -> (c i) j d", c=CH, i=PATCH)).then_inc(params_in, 16)
            sync.dma_start(g_in[:], ln1_g.rearrange(per_patch, c=CH, i=PATCH)).then_inc(params_in, 16)
            sync.dma_start(b_in[:], ln1_b.rearrange(per_patch, c=CH, i=PATCH)).then_inc(params_in, 16)
            for n, row in enumerate((b_patch, ln2_g, ln2_b)):
                sync.dma_start(rows[:, n, :], row.partition_broadcast(128)).then_inc(params_in, 16)
            for b in range(128 // NP):
                sync.dma_start(posP[b * NP:(b + 1) * NP, :], pos[0, 1:NV, :]).then_inc(params_in, 16)
            sync.dma_start(cls_t[:, 0, :], cls[0]).then_inc(params_in, 16)
            sync.dma_start(cls_t[:, 1, :], pos[0, 0:1, :]).then_inc(params_in, 16)
            sync.wait_ge(cls_done, 1)
            sync.dma_start(tok_view[:, 0, :], cls_all[:]).then_inc(stored, 16)
            sync.wait_ge(out_ready, 1)
            for t in range(PT):
                images = slice(t * (128 // NP), (t + 1) * (128 // NP))
                sync.dma_start(tok_view[images, 1:NV, :], y2[:, t, :]).then_inc(stored, 16)
            sync.wait_ge(stored, 16 * (1 + PT))

        @block.gpsimd
        def _(pool):
            pool.iota(iota_i[:], pattern=[[1, 128]], base=0, channel_multiplier=0).then_inc(iota_ready, 1)
            pool.memset(zeros[:], 0.0).then_inc(zeros_ready, 1)
            pool.memset(ones[:], 1.0).then_inc(consts_set, 1)
            pool.memset(half[:], -0.5).then_inc(consts_set, 1)
            pool.memset(pick_sq[:], 0.0).then_inc(pick_set, 1)
            pool.wait_ge(pick_set, 1)
            pool.memset(pick_sq[:, D + 1:WN], 1.0).then_inc(pick_set, 1)
            identity(pool, ident_set, 0, ident[:])
            pool.wait_ge(consts_set, 2)
            pool.wait_ge(counted, 1)
            pool.partition_all_reduce(count[:, 1:2], count[:, 0:1], 128, bass.bass_isa.ReduceOp.max)\
                .then_inc(count_max, 1)
            with pool.Fori(0, 2) as n:
                pool.wait_ge(var_ready, n + 1)
                pool.tensor_tensor(stat[:, 2, :], stat[:, 1, :], half[:], ALU.pow).then_inc(rstd_ready, 1)

        @block.scalar
        def _(act):
            def load(g, s, nth):
                act.wait_ge(pix_used[s], 2 * nth)
                for c in range(CH):
                    for gy in range(GRID):
                        to = pix[s][c * PATCH:(c + 1) * PATCH, :].rearrange("i (b gy x) -> i b gy x", b=GI, gy=GRID)
                        act.dma_start(to[:, :, gy, :],
                                      x[bass.ds(g * GI, GI), c, gy * PATCH:(gy + 1) * PATCH, :]
                                      .rearrange("b i x -> i b x")).then_inc(pix_in[s], 16)

            for s in two:
                act.sem_inc(pix_used[s], 2)
            act.sem_inc(squares_used, 1)
            for s in two:
                load(s, s, 1)

            def pair(m, more):
                for s in two:
                    act.wait_ge(pix_in[s], 16 * CH * GRID * (m + 1))
                    act.wait_ge(squares_used, 2 * m + s + 1)
                    act.activation(squares[:], pix[s][:], ACT.Square).then_inc(squared, 1)
                    act.wait_ge(squared, 2 * m + s + 1)
                    act.sem_inc(pix_used[s], 1)
                    act.wait_ge(acc_ready[s], m + 1)
                    act.activation(accT[:, bass.ds((2 * m + s) * GP, GP)], acc[s][:, 0:GP], ACT.Copy).then_inc(acc_read[s], 1)
                    if more:
                        load(2 * m + s + 2, s, m + 2)

            with act.Fori(0, NG // 2 - 1) as m:
                pair(m, True)
            pair(NG // 2 - 1, False)

        @block.tensor
        def _(pe):
            pe.wait_ge(w_ready, 2)
            for n in range(2):
                pe.matmul(aux[:, n, :], ones[0:K, :], w_sum[:, n, :], start=True, stop=True)
            pe.matmul(aux[:, 2, :], ones[0:1, :], cls_t[0:1, 0, :], start=True, stop=False)
            pe.matmul(aux[:, 2, :], ones[0:1, :], cls_t[0:1, 1, :], start=False, stop=True).then_inc(sums_ready, 1)
            pe.wait_ge(zeros_ready, 1)
            pe.matmul(hist[:], zeros[:], zeros[:, 0:NF], start=True, stop=False, skip_group_check=True)
            pe.wait_ge(pick_set, 2)
            pe.wait_ge(ident_set, 2)
            for s in two:
                pe.sem_inc(acc_read[s], 1)
            with pe.Fori(0, NG // 2) as m:
                for s in two:
                    wait_apart(pe, pix_in[s], 16 * CH * GRID * (m + 1), passed)
                    wait_apart(pe, acc_read[s], m + 1, passed)
                    for j in range(PATCH):
                        last = pe.matmul(acc[s][:, 0:GP], w_ext[:, j, :], pix[s][:, j:GP * PATCH:PATCH],
                                         start=(j == 0), stop=False)
                    last.then_inc(pix_used[s], 1)
                    wait_apart(pe, squared, 2 * m + s + 1, passed)
                    for j in range(PATCH):
                        last = pe.matmul(acc[s][:, 0:GP], pick_sq[:], squares[:, j:GP * PATCH:PATCH],
                                         start=False, stop=(j == PATCH - 1))
                    last.then_inc(acc_ready[s], 1)
                    pe.wait_ge(acc_ready[s], m + 1)
                    pe.sem_inc(squares_used, 1)
            for s in two:
                pe.wait_ge(acc_read[s], NG // 2 + 1)
            for t in range(PT):
                last = pe.transpose(turned[:, t, 0:WN], accT[:, t * 128:(t + 1) * 128], ident[:])
            last.then_inc(turned_ready, 1)
            with pe.Fori(0, HIST) as n:
                for q in two:
                    pe.wait_ge(hot_ready[q], n + 1)
                    for k in range(HB):
                        last = pe.matmul(hist[:], hot_img[q][:, :, k], hot_tok[q][:, :, k],
                                         start=False, stop=False, skip_group_check=True)
                    last.then_inc(hot_used[q], 1)
            pe.matmul(hist[:], zeros[:], zeros[:, 0:NF], start=False, stop=True, skip_group_check=True)\
                .then_inc(hist_ready, 1)

        @block.vector
        def _(dve):
            ch = Chain(dve, prep, PREP, 0)
            dve.wait_ge(params_in, N_PARAMS)
            dve.wait_ge(consts_set, 2)
            ch.step(dve.tensor_tensor(w_bias[:], w_raw[:], spread(b_in[:], 2, D), ALU.mult))
            ch.step(dve.tensor_tensor(w_ext[:, :, 0:D], w_raw[:], spread(g_in[:], 2, D), ALU.mult))
            ch.step(dve.memset(w_ext[:, :, D:D + 1], 1.0))
            ch.step(dve.memset(w_ext[:, :, D + 1:WN], 0.0))
            ch.settle()
            ch.close()
            dve.reduce_sum(w_sum[:, 0, :], w_bias[:].rearrange("p n d -> p d n"), AX.X).then_inc(w_ready, 1)
            dve.reduce_sum(w_sum[:, 1, :], w_ext[:, :, 0:D].rearrange("p n d -> p d n"), AX.X).then_inc(w_ready, 1)
            ch = Chain(dve, edge_prep, EDGE_PREP, 0)
            dve.wait_ge(iota_ready, 1)
            ch.step(dve.tensor_copy(iota_b[:], spread(iota_i[:], 2, HB)))
            dve.wait_ge(edges_in, 32)
            work = keys
            ch.step(dve.tensor_scalar(dst_ok[:], dst[:], float(NODES), None, ALU.is_lt))
            ch.step(dve.tensor_scalar(img_i[:], dst[:], -float(NF // 2), 1.0 / NF, ALU.add, ALU.mult))
            ch.step(dve.memset(keys_sorted[:], 0.0))
            ch.step(dve.memset(top8[:], 0.0))
            ch.settle()
            ch.step(dve.scalar_tensor_tensor(tok_b[:], img_i[:], -float(NF), dst[:], ALU.mult, ALU.add))
            ch.step(dve.scalar_tensor_tensor(work[:], src[:], float(NODES - 1), dst_ok[:], ALU.is_lt, ALU.mult))
            ch.settle()
            ch.step(dve.tensor_copy(dst[:], tok_b[:]))
            dve.reduce_sum(count[:, 0:1], work[:], AX.X).then_inc(counted, 1)
            ch.step(dve.tensor_tensor(dst_ok[:], dst_ok[:], work[:], ALU.subtract))
            ch.settle()
            ch.step(dve.scalar_tensor_tensor(dst_ok[:], dst_ok[:], -256.0, img_i[:], ALU.mult, ALU.add))
            ch.step(dve.tensor_scalar(dst[:], dst[:], IMG_BITS, None, ALU.logical_shift_left))
            ch.settle()
            ch.step(dve.tensor_scalar(img_b[:], dst_ok[:], 256.0, None, ALU.add))
            ch.step(dve.tensor_tensor(dst[:], dst[:], img_i[:], ALU.bitwise_or))
            ch.settle()
            ch.step(dve.tensor_scalar(dst[:], dst[:], SRC_BITS, KEY_TOP, ALU.logical_shift_left, ALU.bitwise_or))
            ch.settle()
            ch.step(dve.tensor_tensor(dst[:], dst[:], src[:], ALU.bitwise_or))
            dve.wait_ge(counted, 1)
            ch.settle()
            ch.step(dve.tensor_tensor(keys[:], dst[:].bitcast(F32), work[:], ALU.mult))
            dve.wait_ge(count_max, 1)
            ch.step(dve.tensor_copy(count_i[:], count[:, 1:2]))
            ch.settle()
            ch.close()
            edges_left = dve.value_load(count_i[0:1, 0:1], min_val=0, max_val=COLS)

            dve.wait_ge(sums_ready, 1)
            dve.tensor_tensor(const[:], aux[:, 0, :], rows[:, 0, :], ALU.add).then_inc(w_here, 1)
            dve.tensor_copy(col_sum[:], aux[:, 1, :]).then_inc(w_here, 1)
            dve.tensor_copy(cls_all[:], aux[:, 2, :]).then_inc(cls_done, 1)
            dve.wait_ge(w_here, 2)
            for s in two:
                dve.sem_inc(hot_used[s], 1)
            dve.sem_inc(sort_chain, 1)

            def sort_round(r):
                c = Chain(dve, sort_chain, 3, r, before=1)
                c.settle()
                dve.sem_inc(passed, 1)
                c.step(dve.max(top8[:], keys[:]))
                c.settle()
                c.step(dve.tensor_copy(keys_sorted[:, bass.ds(r * 8, 8)], top8[:]))
                c.step(dve.match_replace(keys[:], top8[:], keys[:], 0.0))
                c.close()

            mean, var, rstd, tot = (stat[:, n, :] for n in range(4))
            edge_rounds(dve, edges_left, sort_round)
            ch = Chain(dve, chain_sem, EPI, 0)
            dve.wait_ge(turned_ready, 1)
            ch.step(dve.tensor_scalar(mean, turned[:, :, D], 1.0 / PD, None, ALU.mult))
            ch.step(dve.tensor_scalar(tot, turned[:, :, D + 1], 1.0 / PD, EPS, ALU.mult, ALU.add))
            ch.settle()
            ch.step(dve.tensor_tensor(var, mean, mean, ALU.mult))
            ch.step(dve.tensor_tensor(y2[:], spread(mean, 2, D), spread(col_sum[:], 1, PT), ALU.mult))
            ch.settle()
            dve.tensor_tensor(var, tot, var, ALU.subtract).then_inc(var_ready, 1)
            dve.tensor_tensor(y[:], turned[:, :, 0:D], y2[:], ALU.subtract).then_inc(turned_read, 1)
            dve.wait_ge(turned_read, 1)
            dve.wait_ge(rstd_ready, 1)
            ch.step(dve.tensor_tensor(y2[:], y[:], spread(rstd, 2, D), ALU.mult))
            ch.settle()
            ch.step(dve.tensor_tensor(y[:], y2[:], spread(const[:], 1, PT), ALU.add))
            ch.settle()
            ch.step(dve.reduce_sum(tot, y[:], AX.X))
            ch.settle()
            ch.step(dve.scalar_tensor_tensor(y2[:], spread(tot, 2, D), -1.0 / D, y[:], ALU.mult, ALU.add))
            ch.settle()
            ch.step(dve.tensor_tensor(y[:], y2[:], y2[:], ALU.mult))
            ch.settle()
            ch.step(dve.reduce_sum(tot, y[:], AX.X))
            ch.settle()
            dve.tensor_scalar(var, tot, 1.0 / D, EPS, ALU.mult, ALU.add).then_inc(var_ready, 1)
            dve.wait_ge(rstd_ready, 2)
            ch.step(dve.tensor_tensor(y[:], y2[:], spread(rstd, 2, D), ALU.mult))
            ch.settle()
            ch.step(dve.tensor_tensor(y2[:], y[:], spread(rows[:, 1, :], 1, PT), ALU.mult))
            ch.settle()
            dve.tensor_tensor(y[:], y2[:], spread(rows[:, 2, :], 1, PT), ALU.add).then_inc(y_ready, 1)
            dve.wait_ge(y_ready, 1)
            dve.tensor_tensor(y2[:], y[:], spread(posP[:], 1, PT), ALU.add).then_inc(out_ready, 1)
            ch.close()
            with dve.Fori(0, HIST) as n:
                for q in two:
                    at = bass.ds((n * 2 + q) * HB, HB)
                    dve.wait_ge(hot_used[q], n + 1)
                    dve.tensor_tensor(hot_img[q][:], spread(img_b[:, at], 1, 128), iota_b[:], ALU.is_equal)
                    dve.tensor_tensor(hot_tok[q][:], spread(tok_b[:, at], 1, NF), iota_b[:, 0:NF, :],
                                      ALU.is_equal).then_inc(hot_ready[q], 1)
            dve.wait_ge(hist_ready, 1)
            dve.tensor_copy(last_counts[:], hist[:]).then_inc(count_ready, 1)
            dve.wait_ge(count_ready, 1)


def run_vit(nc, tokens, ln_g, ln_b, Wqkv, Wo, bo, ff_g, ff_b, W1, b1, W2, b2, f_g, f_b, txt, fused):
    IPT = 7
    T = IPT * NV
    NT = 2
    C = NT * T
    SUBS = 2
    FULL = B // IPT
    PART = B - FULL * IPT
    CHUNKS = -(-B // (IPT * NT * SUBS))
    TILES = CHUNKS * NT * SUBS
    HD = HEADS * DH
    NW = 11
    STEPS = 15
    SCALE = DH ** -0.5
    subs = range(SUBS)
    with ExitStack() as ctx:
        sb, ps, sem = tools(nc, ctx)
        X = sb("X", [T, TILES, D])
        wqkv = sb("wqkv", [D, 3 * HD])
        wo = sb("wo", [128, HD // 128, D])
        w1 = sb("w1v", [D, MLP])
        w2 = sb("w2v", [MLP, D])
        b1c = sb("b1c", [MLP, 1])
        bias = sb("bias_v", [T, 2, D])
        gains = sb("gains_v", [D, 4])
        rows = sb("rows_v", [T, 2, D])
        ident = sb("ident_v", [T, T])
        maskL = sb("maskL_v", [128, 1, T])
        maskR = sb("maskR_v", [128, HEADS, T])
        mask_left = sb("mask_left_v", [128, T], BF16)
        mask_right = sb("mask_right_v", [128, HEADS * T], BF16)
        half = sb("half_v", [T, NT])
        xc = [sb(f"xc_v{s}", [T, NT, D]) for s in subs]
        xh = [sb(f"xh_v{s}", [T, NT, D]) for s in subs]
        stat = [sb(f"stat_v{s}", [T, 3, NT]) for s in subs]
        hT = [sb(f"hT_v{s}", [D, C]) for s in subs]
        qz = [sb(f"qz_v{s}", [128, HEADS, C]) for s in subs]
        kT = [sb(f"kT_v{s}", [128, 2, C]) for s in subs]
        v = [sb(f"v_v{s}", [T, NT, HD]) for s in subs]
        P = [sb(f"P_v{s}", [T, NT * HEADS, T]) for s in subs]
        mx = [sb(f"mx_v{s}", [T, 2, NT * HEADS]) for s in subs]
        pT = [sb(f"pT_v{s}", [T, NT, HEADS * T]) for s in subs]
        oT = [sb(f"oT_v{s}", [128, 2, C]) for s in subs]
        act1 = [sb(f"act1_v{s}", [MLP, C]) for s in subs]
        xf = sb("xf", [T, TILES, D])
        yf = sb("yf", [T, TILES, D])
        fstat = sb("fstat", [T, 3, TILES])
        fhalf = sb("fhalf", [T, TILES])
        psum = ps("psum_v", [128, 8, 512])

        tokens_in = sem("v_tokens_in")
        weights_in = sem("v_weights_in")
        layer_done = sem("v_layer_done")
        consts = sem("v_consts")
        masks_ready = sem("v_masks_ready")
        padded = sem("v_padded")
        zeroed = sem("v_zeroed")
        chain = [sem(f"v_chain{s}") for s in subs]
        var_ready = [sem(f"v_var{s}") for s in subs]
        rstd_ready = [sem(f"v_rstd{s}") for s in subs]
        xh_ready = [sem(f"v_xh{s}") for s in subs]
        t_ready = [sem(f"v_t{s}") for s in subs]
        hT_ready = [sem(f"v_hT{s}") for s in subs]
        qk_ready = [sem(f"v_qk{s}") for s in subs]
        v_ready = [sem(f"v_v{s}") for s in subs]
        qk_out = [sem(f"v_qk_out{s}") for s in subs]
        v_out = [sem(f"v_v_out{s}") for s in subs]
        s_ready = [sem(f"v_s{s}") for s in subs]
        shifted = [sem(f"v_shifted{s}") for s in subs]
        exped = [sem(f"v_exped{s}") for s in subs]
        p_ready = [sem(f"v_p{s}") for s in subs]
        pT_ready = [sem(f"v_pT{s}") for s in subs]
        pT_out = [sem(f"v_pT_out{s}") for s in subs]
        o_ready = [sem(f"v_o{s}") for s in subs]
        o_out = [sem(f"v_o_out{s}") for s in subs]
        wo_ready = [sem(f"v_wo{s}") for s in subs]
        h1_ready = [sem(f"v_h1{s}") for s in subs]
        gelu_ready = [sem(f"v_gelu{s}") for s in subs]
        w2_ready = [sem(f"v_w2{s}") for s in subs]
        final = sem("v_final")
        pe_passed = sem("v_pe_passed")
        dve_passed = sem("v_dve_passed")
        fvar = sem("v_fvar")
        frstd = sem("v_frstd")
        out_ready = sem("v_out_ready")
        stored = sem("v_stored")
        block = ctx.enter_context(nc.Block())

        def bank(s, n):
            return psum[:, SUBS * 2 * s + n, :]

        def banks(s, n):
            return psum[:, SUBS * 2 * s + n:SUBS * 2 * s + n + 2, :]

        def tiles(c, s):
            return bass.ds((c * SUBS + s) * NT, NT)

        @block.sync
        def _(sync):
            sync.dma_start(X[:, 0:FULL, :], tokens[0:FULL * T].rearrange("(n p) d -> p n d", p=T))\
                .then_inc(tokens_in, 16)
            sync.wait_ge(padded, 1)
            sync.dma_start(X[0:PART * NV, FULL, :], tokens[FULL * T:B * NV]).then_inc(tokens_in, 16)
            sync.dma_start(rows[:, 0, :], f_g.partition_broadcast(T)).then_inc(tokens_in, 16)
            sync.dma_start(rows[:, 1, :], f_b.partition_broadcast(T)).then_inc(tokens_in, 16)
            fused_view = fused.rearrange("(b t) d -> b t d", t=NF)
            sync.dma_start(fused_view[:, NV:NF, :], txt).then_inc(stored, 16)
            with sync.Fori(0, LAYERS) as l:
                sync.wait_ge(layer_done, l + 1)
                one = bass.ds(l, 1)
                sync.dma_start(wqkv[:], Wqkv[one].rearrange("l k n -> (l k) n")).then_inc(weights_in, 16)
                sync.dma_start(wo[:], Wo[one].rearrange("l (c k) n -> (l k) c n", k=128)).then_inc(weights_in, 16)
                sync.dma_start(w1[:], W1[one].rearrange("l k n -> (l k) n")).then_inc(weights_in, 16)
                sync.dma_start(w2[:], W2[one].rearrange("l k n -> (l k) n")).then_inc(weights_in, 16)
                sync.dma_start(b1c[:], b1[one].rearrange("l k -> k l")).then_inc(weights_in, 16)
                for n, row in enumerate((bo, b2)):
                    sync.dma_start(bias[:, n, :], row[one].rearrange("l k -> (l k)").partition_broadcast(T))\
                        .then_inc(weights_in, 16)
                for n, col in enumerate((ln_g, ln_b, ff_g, ff_b)):
                    sync.dma_start(gains[:, n:n + 1], col[one].rearrange("l k -> k l")).then_inc(weights_in, 16)
            sync.wait_ge(out_ready, 1)
            for i in range(IPT):
                sync.dma_start(fused_view[i:FULL * IPT:IPT, 0:NV, :].rearrange("n t d -> t n d"),
                               xf[i * NV:(i + 1) * NV, 0:FULL, :]).then_inc(stored, 16)
            for i in range(PART):
                sync.dma_start(fused_view[FULL * IPT + i, 0:NV, :],
                               xf[i * NV:(i + 1) * NV, FULL, :]).then_inc(stored, 16)
            sync.wait_ge(stored, 16 * (1 + IPT + PART))

        @block.gpsimd
        def _(pool):
            pool.memset(X[:, FULL:, :], 0.0).then_inc(padded, 1)
            n = block_masks(pool, consts, IPT, NV, maskL[:], maskR[:])
            n = identity(pool, consts, n, ident[:])
            pool.memset(half[:], -0.5).then_inc(consts, 1)
            pool.memset(fhalf[:], -0.5).then_inc(consts, 1)
            pool.wait_ge(consts, n + 2)
            with pool.Fori(0, LAYERS * CHUNKS * 2) as r:
                for s in subs:
                    pool.wait_ge(var_ready[s], r + 1)
                    pool.tensor_tensor(stat[s][:, 2, :], stat[s][:, 1, :], half[:], ALU.pow)\
                        .then_inc(rstd_ready[s], 1)
            pool.wait_ge(fvar, 1)
            pool.tensor_tensor(fstat[:, 2, :], fstat[:, 1, :], fhalf[:], ALU.pow).then_inc(frstd, 1)

        N_CONSTS = 10 + 2 + 2

        @block.scalar
        def _(act):
            with act.Fori(0, LAYERS) as l:
                act.wait_ge(weights_in, 16 * NW * (l + 1))
                with act.Fori(0, CHUNKS) as c:
                    r = l * CHUNKS + c
                    for s in subs:
                        act.wait_ge(t_ready[s], 2 * r + 1)
                        act.activation(hT[s][:], bank(s, 3)[0:D, 0:C], ACT.Identity,
                                       bias=gains[:, 1:2], scale=gains[:, 0:1]).then_inc(hT_ready[s], 1)
                    for s in subs:
                        act.wait_ge(qk_ready[s], r + 1)
                        q = bank(s, 0)[:, 0:2 * C].rearrange("p (h c) -> p h c", h=2)
                        act.activation(qz[s][0:DH, 0:HEADS:2, :], q[0:DH], ACT.Copy).then_inc(qk_out[s], 1)
                        act.activation(qz[s][DH:128, 1:HEADS:2, :], q[DH:128], ACT.Copy).then_inc(qk_out[s], 1)
                        act.activation(kT[s][:], bank(s, 1)[:, 0:2 * C].rearrange("p (h c) -> p h c", h=2),
                                       ACT.Copy).then_inc(qk_out[s], 1)
                    for s in subs:
                        act.wait_ge(shifted[s], r + 1)
                        act.activation(P[s][:], P[s][:], ACT.Exp, scale=SCALE).then_inc(exped[s], 1)
                    for s in subs:
                        act.wait_ge(pT_ready[s], r + 1)
                        act.activation(pT[s][:], banks(s, 2)[0:T, :, 0:HEADS * T], ACT.Copy).then_inc(pT_out[s], 1)
                    for s in subs:
                        act.wait_ge(o_ready[s], r + 1)
                        act.activation(oT[s][:], bank(s, 0)[:, 0:2 * C].rearrange("p (h c) -> p h c", h=2),
                                       ACT.Copy).then_inc(o_out[s], 1)
                    for s in subs:
                        act.wait_ge(t_ready[s], 2 * r + 2)
                        act.activation(hT[s][:], bank(s, 3)[0:D, 0:C], ACT.Identity,
                                       bias=gains[:, 3:4], scale=gains[:, 2:3]).then_inc(hT_ready[s], 1)
                    for s in subs:
                        act.wait_ge(h1_ready[s], r + 1)
                        act.activation(act1[s][:], bank(s, 2)[:, 0:C], ACT.Gelu, bias=b1c[:]).then_inc(gelu_ready[s], 1)

        @block.tensor
        def _(pe):
            pe.wait_ge(consts, N_CONSTS)
            pe.wait_ge(zeroed, 1)
            pe.wait_ge(masks_ready, 2)
            with pe.Fori(0, LAYERS) as l:
                wait_apart(pe, weights_in, 16 * NW * (l + 1), pe_passed)
                with pe.Fori(0, CHUNKS) as c:
                    r = l * CHUNKS + c

                    def transposed(s, nth):
                        wait_apart(pe, xh_ready[s], 2 * r + nth, pe_passed)
                        for t in range(NT):
                            last = pe.transpose(bank(s, 3)[0:D, t * T:(t + 1) * T], xh[s][:, t, :], ident[:])
                        last.then_inc(t_ready[s], 1)

                    for s in subs:
                        transposed(s, 1)
                    for s in subs:
                        pe.wait_ge(hT_ready[s], 2 * r + 1)
                        for m in range(4):
                            last = pe.matmul(bank(s, m // 2)[:, (m % 2) * C:(m % 2 + 1) * C],
                                             wqkv[:, m * 128:(m + 1) * 128], hT[s][:], start=True, stop=True)
                        last.then_inc(qk_ready[s], 1)
                        for t in range(NT):
                            last = pe.matmul(bank(s, 2)[0:T, t * HD:(t + 1) * HD], hT[s][:, t * T:(t + 1) * T],
                                             wqkv[:, 2 * HD:3 * HD], start=True, stop=True)
                        last.then_inc(v_ready[s], 1)
                    for s in subs:
                        pe.wait_ge(qk_out[s], 3 * (r + 1))
                        for t in range(NT):
                            at = slice(t * T, (t + 1) * T)
                            pe.matmul(bank(s, t)[0:T, 0:HEADS * T], mask_left[:], mask_right[:],
                                      start=True, stop=False, skip_group_check=True)
                            for h in range(HEADS):
                                last = pe.matmul(bank(s, t)[0:T, h * T:(h + 1) * T], qz[s][:, h, at],
                                                 kT[s][:, h // 2, at], start=False, stop=(h == HEADS - 1),
                                                 skip_group_check=True)
                        last.then_inc(s_ready[s], 1)
                    for s in subs:
                        pe.wait_ge(p_ready[s], r + 1)
                        pe.wait_ge(v_out[s], r + 1)
                        for t in range(NT):
                            for h in range(HEADS):
                                last = pe.transpose(bank(s, 2 + t)[0:T, h * T:(h + 1) * T],
                                                    P[s][:, t * HEADS + h, :], ident[:])
                        last.then_inc(pT_ready[s], 1)
                    for s in subs:
                        pe.wait_ge(pT_out[s], r + 1)
                        for t in range(NT):
                            for h in range(HEADS):
                                to = bank(s, 0)[DH * (h % 2):DH * (h % 2) + DH,
                                                (h // 2) * C + t * T:(h // 2) * C + (t + 1) * T]
                                last = pe.matmul(to, v[s][:, t, h * DH:(h + 1) * DH],
                                                 pT[s][:, t, h * T:(h + 1) * T], start=True, stop=True)
                        last.then_inc(o_ready[s], 1)
                    for s in subs:
                        pe.wait_ge(o_out[s], r + 1)
                        for t in range(NT):
                            to = bank(s, 1)[0:T, t * D:(t + 1) * D]
                            for m in range(2):
                                last = pe.matmul(to, oT[s][:, m, t * T:(t + 1) * T], wo[:, m, :],
                                                 start=(m == 0), stop=(m == 1))
                        last.then_inc(wo_ready[s], 1)
                    for s in subs:
                        transposed(s, 2)
                    for s in subs:
                        pe.wait_ge(hT_ready[s], 2 * r + 2)
                        pe.matmul(bank(s, 2)[:, 0:C], w1[:], hT[s][:], start=True, stop=True)\
                            .then_inc(h1_ready[s], 1)
                    for s in subs:
                        pe.wait_ge(gelu_ready[s], r + 1)
                        for t in range(NT):
                            to = bank(s, 1)[0:T, (NT + t) * D:(NT + t + 1) * D]
                            last = pe.matmul(to, act1[s][:, t * T:(t + 1) * T], w2[:], start=True, stop=True)
                        last.then_inc(w2_ready[s], 1)

        @block.vector
        def _(dve):
            for s in subs:
                last = dve.memset(qz[s][:], 0.0)
            last.then_inc(zeroed, 1)
            dve.wait_ge(consts, N_CONSTS)
            dve.tensor_copy(mask_left[:], maskL[:, 0, :]).then_inc(masks_ready, 1)
            dve.tensor_copy(mask_right[:], maskR[:].rearrange("p h t -> p (h t)")).then_inc(masks_ready, 1)
            dve.wait_ge(tokens_in, 64)
            dve.sem_inc(layer_done, 1)
            with dve.Fori(0, LAYERS) as l:
                dve.wait_ge(weights_in, 16 * NW * (l + 1))
                dve.sem_inc(dve_passed, 1)
                with dve.Fori(0, CHUNKS) as c:
                    r = l * CHUNKS + c
                    ch = [Chain(dve, chain[s], STEPS, r) for s in subs]

                    def normalise(nth):
                        total, var, rstd = (lambda s: stat[s][:, 0, :]), (lambda s: stat[s][:, 1, :]), \
                            (lambda s: stat[s][:, 2, :])
                        for s in subs:
                            if nth == 2:
                                ch[s].settle()
                                dve.sem_inc(dve_passed, 1)
                            ch[s].step(dve.reduce_sum(total(s), X[:, tiles(c, s), :], AX.X))
                        for s in subs:
                            ch[s].settle()
                            ch[s].step(dve.scalar_tensor_tensor(xc[s][:], spread(total(s), 2, D), -1.0 / D,
                                                                X[:, tiles(c, s), :], ALU.mult, ALU.add))
                        for s in subs:
                            ch[s].settle()
                            ch[s].step(dve.tensor_tensor(xh[s][:], xc[s][:], xc[s][:], ALU.mult))
                        for s in subs:
                            ch[s].settle()
                            ch[s].step(dve.reduce_sum(total(s), xh[s][:], AX.X))
                        for s in subs:
                            ch[s].settle()
                            dve.tensor_scalar(var(s), total(s), 1.0 / D, EPS, ALU.mult, ALU.add)\
                                .then_inc(var_ready[s], 1)
                        for s in subs:
                            dve.wait_ge(rstd_ready[s], 2 * r + nth)
                            dve.tensor_tensor(xh[s][:], xc[s][:], spread(rstd(s), 2, D), ALU.mult)\
                                .then_inc(xh_ready[s], 1)
                        for s in subs:
                            x = X[:, tiles(c, s), :]
                            ch[s].step(dve.tensor_tensor(x, x, spread(bias[:, nth - 1, :], 1, NT), ALU.add))

                    normalise(1)
                    for s in subs:
                        dve.wait_ge(v_ready[s], r + 1)
                        dve.tensor_copy(v[s][:].rearrange("p t n -> p (t n)"), bank(s, 2)[0:T, :])\
                            .then_inc(v_out[s], 1)
                    scores = [banks(s, 0)[0:T, :, 0:HEADS * T].rearrange("p t (h k) -> p t h k", h=HEADS)
                              for s in subs]
                    for s in subs:
                        dve.wait_ge(s_ready[s], r + 1)
                        ch[s].step(dve.reduce_max(mx[s][:, 0, :].rearrange("p (t h) -> p t h", t=NT),
                                                  scores[s], AX.X))
                    for s in subs:
                        ch[s].settle()
                        dve.tensor_tensor(P[s][:].rearrange("p (t h) k -> p t h k", t=NT), scores[s],
                                          spread(mx[s][:, 0, :].rearrange("p (t h) -> p t h", t=NT), 3, T),
                                          ALU.subtract).then_inc(shifted[s], 1)
                    for s in subs:
                        dve.wait_ge(exped[s], r + 1)
                        ch[s].step(dve.reduce_sum(mx[s][:, 0, :], P[s][:], AX.X))
                    for s in subs:
                        ch[s].settle()
                        ch[s].step(dve.reciprocal(mx[s][:, 1, :], mx[s][:, 0, :]))
                    for s in subs:
                        ch[s].settle()
                        dve.tensor_tensor(P[s][:], P[s][:], spread(mx[s][:, 1, :], 2, T), ALU.mult)\
                            .then_inc(p_ready[s], 1)
                    for s in subs:
                        ch[s].settle()
                        dve.wait_ge(wo_ready[s], r + 1)
                        ch[s].step(dve.tensor_tensor(
                            X[:, tiles(c, s), :], X[:, tiles(c, s), :],
                            bank(s, 1)[0:T, 0:NT * D].rearrange("p (t d) -> p t d", t=NT), ALU.add))
                    normalise(2)
                    for s in subs:
                        ch[s].settle()
                        dve.wait_ge(w2_ready[s], r + 1)
                        ch[s].step(dve.tensor_tensor(
                            X[:, tiles(c, s), :], X[:, tiles(c, s), :],
                            bank(s, 1)[0:T, NT * D:2 * NT * D].rearrange("p (t d) -> p t d", t=NT), ALU.add))
                    for s in subs:
                        ch[s].settle()
                    ch[0].close()
                    ch[1].close()
                dve.sem_inc(layer_done, 1)
            total, var, rstd = fstat[:, 0, :], fstat[:, 1, :], fstat[:, 2, :]
            ch = Chain(dve, final, 6, 0)
            ch.step(dve.reduce_sum(total, X[:], AX.X))
            ch.settle()
            ch.step(dve.scalar_tensor_tensor(yf[:], spread(total, 2, D), -1.0 / D, X[:], ALU.mult, ALU.add))
            ch.settle()
            ch.step(dve.tensor_tensor(xf[:], yf[:], yf[:], ALU.mult))
            ch.settle()
            ch.step(dve.reduce_sum(total, xf[:], AX.X))
            ch.settle()
            dve.tensor_scalar(var, total, 1.0 / D, EPS, ALU.mult, ALU.add).then_inc(fvar, 1)
            dve.wait_ge(frstd, 1)
            ch.step(dve.tensor_tensor(xf[:], yf[:], spread(rstd, 2, D), ALU.mult))
            ch.settle()
            ch.step(dve.tensor_tensor(yf[:], xf[:], spread(rows[:, 0, :], 1, TILES), ALU.mult))
            ch.settle()
            ch.close()
            dve.tensor_tensor(xf[:], yf[:], spread(rows[:, 1, :], 1, TILES), ALU.add).then_inc(out_ready, 1)


def fuse_and_expert(nc, fused, gat_w, W1, b1, W2, b2, hidden, gat_h, expert_out):
    IPT = 2
    T = IPT * NF
    NT = 2
    C = NT * T
    TILES = B // IPT
    SUBS = 2
    ROUNDS = TILES // (NT * SUBS)
    EH = 2 * D
    STEPS = 14
    subs = range(SUBS)
    with ExitStack() as ctx:
        sb, ps, sem = tools(nc, ctx)
        H = sb("H", [T, TILES, D])
        wg = sb("wg", [D, GF])
        w1 = sb("w1f", [D, EXPERTS, EH])
        w2 = sb("w2f", [EH, EXPERTS, D])
        b1c = sb("b1f", [EH, EXPERTS])
        bias = sb("bias_f", [T, EXPERTS * D])
        mask_left = sb("mask_left_f", [128, T], BF16)
        mask_right = sb("mask_right_f", [128, C], BF16)
        ident = sb("ident_f", [T, T])
        maskL = sb("maskL_f", [128, 1, T])
        maskR = sb("maskR_f", [128, NT, T])
        half = sb("half_f", [T, NT])
        xr = [sb(f"xr_f{s}", [T, NT, D]) for s in subs]
        xc = [sb(f"xc_f{s}", [T, NT, D]) for s in subs]
        sq = [sb(f"sq_f{s}", [T, NT, D]) for s in subs]
        xh = [sb(f"xh_f{s}", [T, NT, D]) for s in subs]
        stat = [sb(f"stat_f{s}", [T, 3, NT]) for s in subs]
        hT = [sb(f"hT_f{s}", [D, C]) for s in subs]
        P = [sb(f"P_f{s}", [T, NT, T]) for s in subs]
        mx = [sb(f"mx_f{s}", [T, 2, NT]) for s in subs]
        pT = [sb(f"pT_f{s}", [T, C]) for s in subs]
        act1 = [sb(f"act1_f{s}", [EH, EXPERTS, C]) for s in subs]
        gh = [sb(f"gh_f{s}", [T, NT, GF]) for s in subs]
        eo = [sb(f"eo_f{s}", [T, NT, EXPERTS * D]) for s in subs]
        psum = ps("psum_f", [128, 8, 512])

        loaded = sem("f_loaded")
        consts = sem("f_consts")
        masks_ready = sem("f_masks_ready")
        chain = [sem(f"f_chain{s}") for s in subs]
        var_ready = [sem(f"f_var{s}") for s in subs]
        rstd_ready = [sem(f"f_rstd{s}") for s in subs]
        xh_ready = [sem(f"f_xh{s}") for s in subs]
        t_ready = [sem(f"f_t{s}") for s in subs]
        hT_ready = [sem(f"f_hT{s}") for s in subs]
        s_ready = [sem(f"f_s{s}") for s in subs]
        shifted = [sem(f"f_shifted{s}") for s in subs]
        exped = [sem(f"f_exped{s}") for s in subs]
        p_ready = [sem(f"f_p{s}") for s in subs]
        pT_ready = [sem(f"f_pT{s}") for s in subs]
        pT_out = [sem(f"f_pT_out{s}") for s in subs]
        o_ready = [sem(f"f_o{s}") for s in subs]
        gat_ready = [sem(f"f_gat{s}") for s in subs]
        h1_ready = [sem(f"f_h1{s}") for s in subs]
        gelu_ready = [sem(f"f_gelu{s}") for s in subs]
        eo_ready = [sem(f"f_eo{s}") for s in subs]
        gh_out = [sem(f"f_gh_out{s}") for s in subs]
        eo_out = [sem(f"f_eo_out{s}") for s in subs]
        gh_stored = [sem(f"f_gh_stored{s}") for s in subs]
        eo_stored = [sem(f"f_eo_stored{s}") for s in subs]
        h_done = sem("f_h_done")
        h_stored = sem("f_h_stored")
        pe_passed = sem("f_pe_passed")
        dve_passed = sem("f_dve_passed")
        block = ctx.enter_context(nc.Block())

        def bank(s, n):
            return psum[:, 4 * s + n, :]

        def tiles(r, s):
            return bass.ds((r * SUBS + s) * NT, NT)

        N_LOADS = 16 * (1 + 4 + EXPERTS)

        @block.sync
        def _(sync):
            sync.dma_start(H[:], fused.rearrange("(n p) d -> p n d", p=T)).then_inc(loaded, 16)
            sync.dma_start(wg[:], gat_w).then_inc(loaded, 16)
            sync.dma_start(w1[:], W1.rearrange("e k n -> k e n")).then_inc(loaded, 16)
            sync.dma_start(w2[:], W2.rearrange("e k n -> k e n")).then_inc(loaded, 16)
            for e in range(EXPERTS):
                sync.dma_start(b1c[:, e:e + 1], b1[e:e + 1, :].rearrange("e k -> k e")).then_inc(loaded, 16)
            sync.dma_start(bias[:], b2.rearrange("e d -> (e d)").partition_broadcast(T)).then_inc(loaded, 16)
            gat_view = gat_h.rearrange("(n p) d -> p n d", p=T)
            eo_view = expert_out.rearrange("(n p) d -> p n d", p=T)
            with sync.Fori(0, ROUNDS) as r:
                for s in subs:
                    sync.wait_ge(gh_out[s], r + 1)
                    sync.dma_start(gat_view[:, tiles(r, s), :], gh[s][:]).then_inc(gh_stored[s], 16)
                    sync.wait_ge(eo_out[s], r + 1)
                    sync.dma_start(eo_view[:, tiles(r, s), :], eo[s][:]).then_inc(eo_stored[s], 16)
            sync.wait_ge(h_done, 1)
            sync.dma_start(hidden.rearrange("(n p) d -> p n d", p=T), H[:]).then_inc(h_stored, 16)
            sync.wait_ge(h_stored, 16)
            for s in subs:
                sync.wait_ge(gh_stored[s], 16 * (ROUNDS + 1))
                sync.wait_ge(eo_stored[s], 16 * (ROUNDS + 1))

        @block.gpsimd
        def _(pool):
            n = block_masks(pool, consts, IPT, NF, maskL[:], maskR[:])
            n = identity(pool, consts, n, ident[:])
            pool.memset(half[:], -0.5).then_inc(consts, 1)
            pool.wait_ge(consts, n + 1)
            with pool.Fori(0, ROUNDS * 2) as r:
                for s in subs:
                    pool.wait_ge(var_ready[s], r + 1)
                    pool.tensor_tensor(stat[s][:, 2, :], stat[s][:, 1, :], half[:], ALU.pow)\
                        .then_inc(rstd_ready[s], 1)

        N_CONSTS = 10 + 2 + 1

        @block.scalar
        def _(act):
            act.wait_ge(loaded, N_LOADS)
            with act.Fori(0, ROUNDS) as r:
                for s in subs:
                    act.wait_ge(t_ready[s], 2 * r + 1)
                    act.activation(hT[s][:], bank(s, 3)[0:D, 0:C], ACT.Copy).then_inc(hT_ready[s], 1)
                for s in subs:
                    act.wait_ge(shifted[s], r + 1)
                    act.activation(P[s][:], P[s][:], ACT.Exp).then_inc(exped[s], 1)
                for s in subs:
                    act.wait_ge(pT_ready[s], r + 1)
                    act.activation(pT[s][:], bank(s, 1)[0:T, 0:C], ACT.Copy).then_inc(pT_out[s], 1)
                for s in subs:
                    act.wait_ge(t_ready[s], 2 * r + 2)
                    act.activation(hT[s][:], bank(s, 3)[0:D, 0:C], ACT.Copy).then_inc(hT_ready[s], 1)
                for s in subs:
                    act.wait_ge(h1_ready[s], r + 1)
                    for e in range(EXPERTS):
                        last = act.activation(act1[s][:, e, :], bank(s, e // 2)[:, (e % 2) * C:(e % 2 + 1) * C],
                                              ACT.Gelu, bias=b1c[:, e:e + 1])
                    last.then_inc(gelu_ready[s], 1)

        @block.tensor
        def _(pe):
            pe.wait_ge(consts, N_CONSTS)
            pe.wait_ge(masks_ready, 2)
            pe.wait_ge(loaded, N_LOADS)
            with pe.Fori(0, ROUNDS) as r:
                def transposed(s, nth):
                    wait_apart(pe, xh_ready[s], 2 * r + nth, pe_passed)
                    for t in range(NT):
                        last = pe.transpose(bank(s, 3)[0:D, t * T:(t + 1) * T], xh[s][:, t, :], ident[:])
                    last.then_inc(t_ready[s], 1)

                for s in subs:
                    transposed(s, 1)
                for s in subs:
                    pe.wait_ge(hT_ready[s], 2 * r + 1)
                    pe.matmul(bank(s, 0)[0:T, 0:C], mask_left[:], mask_right[:],
                              start=True, stop=False, skip_group_check=True)
                    for t in range(NT):
                        at = slice(t * T, (t + 1) * T)
                        last = pe.matmul(bank(s, 0)[0:T, at], hT[s][:, at], hT[s][:, at],
                                         start=False, stop=(t == NT - 1), skip_group_check=True)
                    last.then_inc(s_ready[s], 1)
                for s in subs:
                    pe.wait_ge(p_ready[s], r + 1)
                    for t in range(NT):
                        last = pe.transpose(bank(s, 1)[0:T, t * T:(t + 1) * T], P[s][:, t, :], ident[:])
                    last.then_inc(pT_ready[s], 1)
                for s in subs:
                    pe.wait_ge(pT_out[s], r + 1)
                    for t in range(NT):
                        last = pe.matmul(bank(s, 2)[0:T, t * D:(t + 1) * D], pT[s][:, t * T:(t + 1) * T],
                                         xh[s][:, t, :], start=True, stop=True)
                    last.then_inc(o_ready[s], 1)
                for s in subs:
                    transposed(s, 2)
                for s in subs:
                    pe.wait_ge(hT_ready[s], 2 * r + 2)
                    for e in range(EXPERTS):
                        last = pe.matmul(bank(s, e // 2)[:, (e % 2) * C:(e % 2 + 1) * C], w1[:, e, :], hT[s][:],
                                         start=True, stop=True)
                    last.then_inc(h1_ready[s], 1)
                    for t in range(NT):
                        last = pe.matmul(bank(s, 3)[0:T, C + t * GF:C + (t + 1) * GF],
                                         hT[s][:, t * T:(t + 1) * T], wg[:], start=True, stop=True)
                    last.then_inc(gat_ready[s], 1)
                for s in subs:
                    pe.wait_ge(gelu_ready[s], r + 1)
                    for t in range(NT):
                        to = bank(s, 2)[0:T, t * EXPERTS * D:(t + 1) * EXPERTS * D]
                        for e in range(EXPERTS):
                            last = pe.matmul(to[:, e * D:(e + 1) * D], act1[s][:, e, t * T:(t + 1) * T],
                                             w2[:, e, :], start=True, stop=True)
                    last.then_inc(eo_ready[s], 1)

        @block.vector
        def _(dve):
            dve.wait_ge(consts, N_CONSTS)
            dve.tensor_copy(mask_left[:], maskL[:, 0, :]).then_inc(masks_ready, 1)
            dve.tensor_copy(mask_right[:], maskR[:].rearrange("p n t -> p (n t)")).then_inc(masks_ready, 1)
            dve.wait_ge(loaded, N_LOADS)
            for s in subs:
                dve.sem_inc(gh_stored[s], 16)
                dve.sem_inc(eo_stored[s], 16)
            with dve.Fori(0, ROUNDS) as r:
                ch = [Chain(dve, chain[s], STEPS, r) for s in subs]

                def normalise(nth):
                    total, var, rstd = (lambda s: stat[s][:, 0, :]), (lambda s: stat[s][:, 1, :]), \
                        (lambda s: stat[s][:, 2, :])
                    for s in subs:
                        ch[s].settle()
                        ch[s].step(dve.reduce_sum(total(s), xr[s][:], AX.X))
                    for s in subs:
                        ch[s].settle()
                        ch[s].step(dve.scalar_tensor_tensor(xc[s][:], spread(total(s), 2, D), -1.0 / D,
                                                            xr[s][:], ALU.mult, ALU.add))
                    for s in subs:
                        ch[s].settle()
                        ch[s].step(dve.tensor_tensor(sq[s][:], xc[s][:], xc[s][:], ALU.mult))
                    for s in subs:
                        ch[s].settle()
                        ch[s].step(dve.reduce_sum(total(s), sq[s][:], AX.X))
                    for s in subs:
                        ch[s].settle()
                        dve.tensor_scalar(var(s), total(s), 1.0 / D, EPS, ALU.mult, ALU.add)\
                            .then_inc(var_ready[s], 1)
                    for s in subs:
                        dve.wait_ge(rstd_ready[s], 2 * r + nth)
                        dve.tensor_tensor(xh[s][:], xc[s][:], spread(rstd(s), 2, D), ALU.mult)\
                            .then_inc(xh_ready[s], 1)

                for s in subs:
                    ch[s].step(dve.tensor_copy(xr[s][:], H[:, tiles(r, s), :]))
                normalise(1)
                for s in subs:
                    dve.wait_ge(s_ready[s], r + 1)
                    score = bank(s, 0)[0:T, 0:C].rearrange("p (n t) -> p n t", n=NT)
                    ch[s].step(dve.reduce_max(mx[s][:, 0, :], score, AX.X))
                for s in subs:
                    ch[s].settle()
                    score = bank(s, 0)[0:T, 0:C].rearrange("p (n t) -> p n t", n=NT)
                    dve.tensor_tensor(P[s][:], score, spread(mx[s][:, 0, :], 2, T), ALU.subtract)\
                        .then_inc(shifted[s], 1)
                for s in subs:
                    dve.wait_ge(exped[s], r + 1)
                    ch[s].step(dve.reduce_sum(mx[s][:, 0, :], P[s][:], AX.X))
                for s in subs:
                    ch[s].settle()
                    ch[s].step(dve.reciprocal(mx[s][:, 1, :], mx[s][:, 0, :]))
                for s in subs:
                    ch[s].settle()
                    dve.tensor_tensor(P[s][:], P[s][:], spread(mx[s][:, 1, :], 2, T), ALU.mult)\
                        .then_inc(p_ready[s], 1)
                for s in subs:
                    dve.wait_ge(o_ready[s], r + 1)
                    ch[s].step(dve.tensor_tensor(xr[s][:], xr[s][:],
                                                 bank(s, 2)[0:T, 0:NT * D].rearrange("p (n d) -> p n d", n=NT),
                                                 ALU.add))
                normalise(2)
                for s in subs:
                    ch[s].step(dve.tensor_copy(H[:, tiles(r, s), :], xr[s][:]))
                for s in subs:
                    dve.wait_ge(gat_ready[s], r + 1)
                    dve.wait_ge(gh_stored[s], 16 * (r + 1))
                    dve.tensor_copy(gh[s][:], bank(s, 3)[0:T, C:C + NT * GF].rearrange("p (n d) -> p n d", n=NT))\
                        .then_inc(gh_out[s], 1)
                for s in subs:
                    dve.wait_ge(eo_ready[s], r + 1)
                    dve.wait_ge(eo_stored[s], 16 * (r + 1))
                    dve.tensor_tensor(eo[s][:], bank(s, 2)[0:T, :].rearrange("p (n d) -> p n d", n=NT),
                                      spread(bias[:], 1, NT), ALU.add).then_inc(eo_out[s], 1)
                for s in subs:
                    ch[s].settle()
                    ch[s].close()
            dve.sem_inc(h_done, 1)


def route_edges(nc, keys_sorted, count_i, last_counts, gat_h, att_src, att_dst, src_table, agg):
    TF = GF + GH
    BT = 4
    SUBS = 2
    ROUNDS = COLS // (BT * SUBS)
    STRIDE = 7
    WIN = 3 * STRIDE
    STARTS = NF // STRIDE - 2
    HALF = (NF + 1) // 2
    NO_TOKEN = 64.0
    SLOPE = 0.2
    PARTS = 3
    DECODE = 14
    PREP = 24
    subs = range(SUBS)
    with ExitStack() as ctx:
        sb, ps, sem = tools(nc, ctx)
        h_nodes = sb("h_nodes", [128, NF, GF])
        att = sb("att", [128, 2, GF])
        prod = sb("prod", [128, NF, GF])
        src_rows = sb("src_rows", [128, NF, TF])
        a_dst = sb("a_dst", [128, NF, GH])
        bound = sb("bound", [128, NF, GH])
        rest = sb("rest", [128, NF, GH])
        dst_parts = sb("dst_parts", [128, PARTS, NF * GH], BF16)
        top = sb("top", [128, 2, GH])
        last_row = sb("last_row", [128, TF])
        z = sb("z_r", [128, 2, NF, GH])
        dense = sb("dense", [128, NF, TF])
        zeros = sb("zeros_r", [128, 512])
        source = sb("source", [128, COLS], I32)
        tok_i = sb("tok_i_r", [128, COLS], I32)
        img_i = sb("img_i_r", [128, COLS], I32)
        empty = sb("empty", [128, COLS])
        img = sb("img_r", [128, COLS + BT * SUBS], BF16)
        tok = sb("tok_r", [128, COLS + BT * SUBS])
        ends = sb("ends", [128, 2, 2, ROUNDS])
        start_i = sb("start_i", [128, ROUNDS + 1], I32)
        start_f = sb("start_f", [128, ROUNDS])
        wide_f = sb("wide_f", [128, 1])
        wide_i = sb("wide_i", [128, 1], I32)
        iota_f = sb("iota_r", [128, 128])
        iota_b = sb("iota_rb", [128, 128, BT], BF16)
        ident_f = sb("ident_rf", [128, 128])
        ident = sb("ident_r", [128, 128], BF16)
        node4 = [sb(f"node4_{s}", [128, BT], I32) for s in subs]
        gathered = [sb(f"gathered{s}", [128, BT, TF]) for s in subs]
        from_src = [sb(f"from_src{s}", [128, BT, TF]) for s in subs]
        logit = [sb(f"logit{s}", [128, 3, BT, GH]) for s in subs]
        from_dst = [sb(f"from_dst{s}", [128, BT, GH]) for s in subs]
        val = [sb(f"val{s}", [128, BT, TF]) for s in subs]
        hot_b = [sb(f"hot_b{s}", [128, 128, BT], BF16) for s in subs]
        hot_T = [sb(f"hot_T{s}", [128, BT * 128], BF16) for s in subs]
        hot_f = [sb(f"hot_f{s}", [128, BT, 128]) for s in subs]
        hot_tok = [sb(f"hot_tok_r{s}", [128, BT * NF]) for s in subs]
        picked = [sb(f"picked{s}", [128, BT * NF * GH]) for s in subs]
        spread_val = [sb(f"spread_val{s}", [128, BT * NF * TF]) for s in subs]
        psum = ps("psum_r", [128, 8 * 512])

        nodes_in = sem("r_nodes_in")
        prep = sem("r_prep")
        top_ready = sem("r_top_ready")
        top_all = sem("r_top_all")
        rows_ready = sem("r_rows_ready")
        rows_stored = sem("r_rows_stored")
        last_in = sem("r_last_in")
        dense_logit = sem("r_dense_logit")
        dense_exp = sem("r_dense_exp")
        dense_ready = sem("r_dense_ready")
        iota_ready = sem("r_iota")
        ident_set = sem("r_ident")
        decode = sem("r_decode")
        decoded = sem("r_decoded")
        ends_ready = sem("r_ends_ready")
        ends_all = sem("r_ends_all")
        opened = sem("r_opened")
        copied = [sem(f"r_copied{s}") for s in subs]
        src_in = [sem(f"r_src_in{s}") for s in subs]
        src_taken = [sem(f"r_src_taken{s}") for s in subs]
        chain = [sem(f"r_chain{s}") for s in subs]
        hot_ready = [sem(f"r_hot_ready{s}") for s in subs]
        turned = [sem(f"r_turned{s}") for s in subs]
        turned_out = [sem(f"r_turned_out{s}") for s in subs]
        cast = [sem(f"r_cast{s}") for s in subs]
        dst_ready = [sem(f"r_dst_ready{s}") for s in subs]
        logit_ready = [sem(f"r_logit{s}") for s in subs]
        exp_ready = [sem(f"r_exp{s}") for s in subs]
        batch_ready = [sem(f"r_batch{s}") for s in subs]
        batch_used = [sem(f"r_batch_used{s}") for s in subs]
        sums_ready = sem("r_sums_ready")
        sums_read = sem("r_sums_read")
        passed = sem("r_passed")
        pe_passed = sem("r_pe_passed")
        block = ctx.enter_context(nc.Block())

        def columns(r, s):
            return bass.ds(r * (BT * SUBS) + s * BT, BT)

        def dst_psum(s, wide, k):
            if wide:
                at = (3 + 2 * s + k // 2) * 512 + (k % 2) * NF * GH
                return psum[:, at:at + NF * GH]
            return psum[:, (6 + s) * 512 + k * WIN * GH:(6 + s) * 512 + (k + 1) * WIN * GH]

        def turned_psum(s, wide):
            bank = (2 if wide else 5) * 512
            return psum[:, bank:bank + 512].bitcast(BF16)[:, s * BT * 128:(s + 1) * BT * 128]

        def start_of(eng, r):
            return eng.value_load(start_i[0:1, bass.ds(r, 1)], min_val=0, max_val=STARTS - 1)

        def both_paths(eng, path):
            wide = eng.value_load(wide_i[0:1, 0:1], min_val=0, max_val=1)
            with eng.If(wide < 1):
                path(False)
            with eng.If(wide > 0):
                path(True)

        @block.sync
        def _(sync):
            by_node = lambda t: t.rearrange("(b t) f -> b t f", t=NF)
            sync.dma_start(h_nodes[:], by_node(gat_h)).then_inc(nodes_in, 16)
            for n, a in enumerate((att_src, att_dst)):
                sync.dma_start(att[:, n, :], a.rearrange("h e -> (h e)").partition_broadcast(128))\
                    .then_inc(nodes_in, 16)
            sync.wait_ge(rows_ready, 1)
            sync.dma_start(by_node(src_table), src_rows[:]).then_inc(rows_stored, 16)
            sync.wait_ge(rows_stored, 16)
            sync.dma_start(last_row[:], src_table[NODES - 1].partition_broadcast(128)).then_inc(last_in, 16)

        @block.gpsimd
        def _(pool):
            pool.iota(iota_f[:], pattern=[[1, 128]], base=0, channel_multiplier=0,
                      allow_small_or_imprecise_dtypes=True).then_inc(iota_ready, 1)
            identity(pool, ident_set, 0, ident_f[:])
            pool.wait_ge(top_ready, 1)
            pool.partition_all_reduce(top[:, 1, :], top[:, 0, :], 128, bass.bass_isa.ReduceOp.max)\
                .then_inc(top_all, 1)
            pool.wait_ge(ends_ready, 2)
            pool.partition_all_reduce(ends[:, 1, :, :].rearrange("p n r -> p (n r)"),
                                      ends[:, 0, :, :].rearrange("p n r -> p (n r)"), 128,
                                      bass.bass_isa.ReduceOp.max).then_inc(ends_all, 1)
            pool.wait_ge(rows_stored, 16)
            count = pool.value_load(count_i[0:1, 0:1], min_val=0, max_val=COLS)
            for s in subs:
                pool.sem_inc(src_taken[s], 1)

            def gather(r):
                for s in subs:
                    pool.wait_ge(src_taken[s], r + 1)
                    pool.sem_inc(passed, 1)
                    pool.tensor_copy(node4[s][:], source[:, columns(r, s)]).then_inc(copied[s], 1)
                    pool.wait_ge(copied[s], r + 1)
                    pool.sem_inc(passed, 1)
                    for k in range(BT):
                        pool.indirect_dma_start(
                            gathered[s][:, k, :], None, src_table,
                            bass.IndirectOffsetOnAxis(ap=node4[s][:, k:k + 1].bitcast(U32), axis=0))\
                            .then_inc(src_in[s], 16)
            edge_rounds(pool, count, gather)

        @block.scalar
        def _(act):
            act.wait_ge(dense_logit, 1)
            act.activation(z[:], z[:], ACT.Exp).then_inc(dense_exp, 1)
            act.wait_ge(decoded, 1)
            count = act.value_load(count_i[0:1, 0:1], min_val=0, max_val=COLS)
            for s in subs:
                act.sem_inc(batch_used[s], 1)

            def path(wide):
                def out_of_psum(s, r):
                    act.wait_ge(turned[s], r + 1)
                    act.activation(hot_T[s][:], turned_psum(s, wide), ACT.Copy).then_inc(turned_out[s], 1)

                def batches(r):
                    for s in subs:
                        act.wait_ge(batch_used[s], r + 1)
                        act.activation(hot_f[s][:], hot_b[s][:].rearrange("p i k -> p k i"), ACT.Copy)\
                            .then_inc(cast[s], 1)
                    for s in subs:
                        act.wait_ge(logit_ready[s], r + 1)
                        act.activation(val[s][:, :, GF:TF], logit[s][:, 2, :, :], ACT.Exp).then_inc(exp_ready[s], 1)
                    for s in subs:
                        out_of_psum(s, r + 1)

                for s in subs:
                    out_of_psum(s, 0)
                edge_rounds(act, count, batches)
            both_paths(act, path)

        @block.tensor
        def _(pe):
            pe.wait_ge(decoded, 1)
            count = pe.value_load(count_i[0:1, 0:1], min_val=0, max_val=COLS)

            def path(wide):
                sums = [(0, HALF * TF), (1, (NF - HALF) * TF)] if wide else [(n, WIN * TF) for n in range(STARTS)]
                width = NF if wide else WIN
                for n, size in sums:
                    pe.matmul(psum[:, n * 512:n * 512 + size], zeros[:, 0:128], zeros[:, 0:size],
                              start=True, stop=False, skip_group_check=True)

                def targets(s, r):
                    pe.wait_ge(hot_ready[s], r + 1)
                    for k in range(BT):
                        last = pe.transpose(turned_psum(s, wide)[:, k * 128:(k + 1) * 128], hot_b[s][:, :, k], ident[:])
                    last.then_inc(turned[s], 1)

                def target_rows(s, r, start):
                    pe.wait_ge(turned_out[s], r + 1)
                    for k in range(BT):
                        for n in range(PARTS):
                            rows = dst_parts[:, n, :] if wide else dst_parts[:, n, bass.ds(start * (STRIDE * GH), WIN * GH)]
                            last = pe.matmul(dst_psum(s, wide, k), hot_T[s][:, k * 128:(k + 1) * 128], rows,
                                             start=(n == 0), stop=(n == PARTS - 1), skip_group_check=True)
                    last.then_inc(dst_ready[s], 1)

                def batches(r):
                    after = None if wide else start_of(pe, r + 1)
                    for s in subs:
                        targets(s, r + 1)
                        target_rows(s, r + 1, after)
                    start = None if wide else start_of(pe, r)
                    for s in subs:
                        wait_apart(pe, cast[s], r + 1, pe_passed)
                        wait_apart(pe, batch_ready[s], r + 2, pe_passed)
                        for k in range(BT):
                            base = k * width * TF
                            if wide:
                                for n, size in sums:
                                    at = base + n * HALF * TF
                                    last = pe.matmul(psum[:, n * 512:n * 512 + size], hot_f[s][:, k, :],
                                                     spread_val[s][:, at:at + size],
                                                     start=False, stop=False, skip_group_check=True)
                            else:
                                last = pe.matmul(psum[:, bass.ds(start * 512, WIN * TF)], hot_f[s][:, k, :],
                                                 spread_val[s][:, base:base + WIN * TF],
                                                 start=False, stop=False, skip_group_check=True)
                        last.then_inc(batch_used[s], 1)

                first = None if wide else start_of(pe, 0)
                for s in subs:
                    targets(s, 0)
                    target_rows(s, 0, first)
                edge_rounds(pe, count, batches)
                for n, size in sums:
                    last = pe.matmul(psum[:, n * 512:n * 512 + size], zeros[:, 0:128], zeros[:, 0:size],
                                     start=False, stop=True, skip_group_check=True)
                last.then_inc(sums_ready, 1)
            both_paths(pe, path)

        @block.vector
        def _(dve):
            ch = Chain(dve, decode, DECODE, 0)
            keys_i = keys_sorted[:].bitcast(I32)
            ch.step(dve.memset(zeros[:], 0.0))
            ch.step(dve.tensor_scalar(source[:], keys_i, (1 << SRC_BITS) - 1, None, ALU.bitwise_and))
            ch.step(dve.tensor_scalar(img_i[:], keys_i, SRC_BITS, (1 << IMG_BITS) - 1,
                                      ALU.logical_shift_right, ALU.bitwise_and))
            ch.step(dve.tensor_scalar(tok_i[:], keys_i, SRC_BITS + IMG_BITS, 63,
                                      ALU.logical_shift_right, ALU.bitwise_and))
            ch.step(dve.tensor_scalar(empty[:], keys_sorted[:], 0.0, NO_TOKEN, ALU.is_equal, ALU.mult))
            ch.step(dve.memset(img[:, COLS:], 0.0))
            ch.step(dve.memset(tok[:, COLS:], NO_TOKEN))
            ch.step(dve.memset(start_i[:, ROUNDS:], 0))
            dve.wait_ge(iota_ready, 1)
            ch.step(dve.tensor_copy(iota_b[:], spread(iota_f[:], 2, BT)))
            dve.wait_ge(ident_set, 2)
            ch.step(dve.tensor_copy(ident[:], ident_f[:]))
            ch.settle()
            ch.step(dve.tensor_copy(img[:, 0:COLS], img_i[:]))
            ch.step(dve.tensor_tensor(tok[:, 0:COLS], tok_i[:], empty[:], ALU.add))
            ch.step(dve.tensor_tensor(empty[:], tok_i[:], empty[:], ALU.subtract))
            ch.settle()
            per_round = "p (r k) -> p r k"
            dve.reduce_max(ends[:, 0, 0, :], empty[:].rearrange(per_round, r=ROUNDS), AX.X).then_inc(ends_ready, 1)
            dve.wait_ge(ends_ready, 1)
            ch.step(dve.tensor_scalar(empty[:], tok[:, 0:COLS], -1.0, None, ALU.mult))
            ch.settle()
            dve.reduce_max(ends[:, 0, 1, :], empty[:].rearrange(per_round, r=ROUNDS), AX.X).then_inc(ends_ready, 1)
            ch.close()

            ch = Chain(dve, prep, PREP, 0)
            split = lambda t: t.rearrange("p t (h e) -> p t h e", e=EXPERTS)
            a_src = src_rows[:, :, GF:TF]
            dve.wait_ge(nodes_in, 48)
            ch.step(dve.tensor_tensor(prod[:], h_nodes[:], spread(att[:, 0, :], 1, NF), ALU.mult))
            dve.tensor_copy(src_rows[:, :, 0:GF], h_nodes[:])
            ch.settle()
            dve.reduce_sum(a_src, split(prod[:]), AX.X).then_inc(rows_ready, 1)
            dve.wait_ge(rows_ready, 1)
            dve.reduce_max(top[:, 0, :], a_src.rearrange("p t h -> p h t"), AX.X).then_inc(top_ready, 1)
            ch.step(dve.tensor_tensor(prod[:], h_nodes[:], spread(att[:, 1, :], 1, NF), ALU.mult))
            ch.settle()
            ch.step(dve.reduce_sum(a_dst[:], split(prod[:]), AX.X))
            ch.settle()
            left = a_dst
            for n in range(PARTS):
                part = dst_parts[:, n, :].rearrange("p (t h) -> p t h", h=GH)
                ch.step(dve.tensor_copy(part, left[:]))
                ch.settle()
                if n < PARTS - 1:
                    ch.step(dve.tensor_tensor(rest[:], left[:], part, ALU.subtract))
                    ch.settle()
                    left = rest

            dve.wait_ge(ends_all, 1)
            below = ends[:, 1, 1, :]
            ch.step(dve.tensor_scalar(start_f[:], below, -float(STRIDE), None, ALU.is_le))
            for n in range(2, STARTS):
                ch.settle()
                ch.step(dve.scalar_tensor_tensor(start_f[:], below, -float(n * STRIDE), start_f[:],
                                                 ALU.is_le, ALU.add))
            ch.settle()
            ch.step(dve.tensor_copy(start_i[:, 0:ROUNDS], start_f[:]))
            ch.settle()
            ch.step(dve.scalar_tensor_tensor(start_f[:], start_f[:], -float(STRIDE), ends[:, 1, 0, :],
                                             ALU.mult, ALU.add))
            ch.settle()
            ch.step(dve.reduce_max(wide_f[:], start_f[:], AX.X))
            ch.settle()
            ch.step(dve.tensor_scalar(wide_i[:], wide_f[:], float(WIN), None, ALU.is_ge))
            ch.settle()
            dve.sem_inc(decoded, 1)

            dve.wait_ge(top_all, 1)
            ch.step(dve.tensor_tensor(z[:, 0, :, :], a_src, a_dst[:], ALU.add))
            raw_bound = prod[:, :, 0:GH]
            ch.step(dve.tensor_tensor(raw_bound, a_dst[:], spread(top[:, 1, :], 1, NF), ALU.add))
            ch.settle()
            ch.step(dve.scalar_tensor_tensor(bound[:], raw_bound, SLOPE, raw_bound, ALU.mult, ALU.max))
            dve.wait_ge(last_in, 16)
            ch.step(dve.tensor_tensor(z[:, 1, :, :], a_dst[:], spread(last_row[:, GF:TF], 1, NF), ALU.add))
            ch.settle()
            z_flat = z[:].rearrange("p n t h -> p (n t h)")
            ch.step(dve.scalar_tensor_tensor(z_flat, z_flat, SLOPE, z_flat, ALU.mult, ALU.max))
            ch.settle()
            dve.tensor_tensor(z[:], z[:], spread(bound[:], 1, 2), ALU.subtract).then_inc(dense_logit, 1)
            dve.wait_ge(dense_exp, 1)
            ch.step(dve.tensor_tensor(z[:, 1, :, :], z[:, 1, :, :], spread(last_counts[:], 2, GH), ALU.mult))
            ch.settle()
            ch.step(dve.tensor_tensor(split(dense[:, :, 0:GF]), split(h_nodes[:]),
                                      spread(z[:, 0, :, :], 3, EXPERTS), ALU.mult))
            ch.step(dve.tensor_tensor(split(prod[:]), spread(z[:, 1, :, :], 3, EXPERTS),
                                      spread(last_row[:, 0:GF].rearrange("p (h e) -> p h e", e=EXPERTS), 1, NF),
                                      ALU.mult))
            ch.close()
            ch.settle()
            dve.tensor_tensor(dense[:, :, 0:GF], dense[:, :, 0:GF], prod[:], ALU.add).then_inc(dense_ready, 1)
            dve.tensor_tensor(dense[:, :, GF:TF], z[:, 0, :, :], z[:, 1, :, :], ALU.add).then_inc(dense_ready, 1)
            dve.wait_ge(dense_ready, 2)

            count = dve.value_load(count_i[0:1, 0:1], min_val=0, max_val=COLS)

            def path(wide):
                width = NF if wide else WIN

                def one_hot(s, r):
                    dve.tensor_tensor(hot_b[s][:], spread(img[:, columns(r, s)], 1, 128), iota_b[:], ALU.is_equal)\
                        .then_inc(hot_ready[s], 1)

                def batches(r):
                    start = None if wide else start_of(dve, r)
                    c = [Chain(dve, chain[s], 6, r) for s in subs]
                    tokens = iota_f[:, 0:NF] if wide else iota_f[:, bass.ds(start * STRIDE, WIN)]
                    hots = [hot_tok[s][:, 0:BT * width].rearrange("p (k t) -> p k t", k=BT) for s in subs]
                    picks = [picked[s][:, 0:BT * width * GH].rearrange("p (k t h) -> p k t h", k=BT, h=GH)
                             for s in subs]
                    for s in subs:
                        dve.wait_ge(batch_ready[s], r + 1)
                        c[s].step(dve.tensor_tensor(hots[s], spread(tok[:, columns(r, s)], 2, width),
                                                    spread(tokens, 1, BT), ALU.is_equal))
                    for s in subs:
                        dve.wait_ge(src_in[s], 16 * BT * (r + 1))
                        dve.tensor_copy(from_src[s][:], gathered[s][:]).then_inc(src_taken[s], 1)
                    for s in subs:
                        dve.wait_ge(dst_ready[s], r + 1)
                        c[s].settle()
                        if wide:
                            for n in range(2):
                                at = (3 + 2 * s + n) * 512
                                got = psum[:, at:at + 2 * NF * GH].rearrange("p (k t h) -> p k t h", k=2, h=GH)
                                last = dve.tensor_tensor(picks[s][:, 2 * n:2 * n + 2], got,
                                                         spread(hots[s][:, 2 * n:2 * n + 2, :], 3, GH), ALU.mult)
                            c[s].step(last)
                        else:
                            at = (6 + s) * 512
                            got = psum[:, at:at + BT * WIN * GH].rearrange("p (k t h) -> p k t h", k=BT, h=GH)
                            c[s].step(dve.tensor_tensor(picks[s], got, spread(hots[s], 3, GH), ALU.mult))
                    for s in subs:
                        c[s].settle()
                        c[s].step(dve.reduce_sum(from_dst[s][:], picks[s].rearrange("p k t h -> p k h t"), AX.X))
                    for s in subs:
                        c[s].settle()
                        dve.wait_ge(src_taken[s], r + 2)
                        dve.tensor_tensor(logit[s][:, 0, :, :], from_src[s][:, :, GF:TF], from_dst[s][:], ALU.add)
                        c[s].step(dve.tensor_tensor(logit[s][:, 1, :, :], from_dst[s][:], spread(top[:, 1, :], 1, BT),
                                                    ALU.add))
                    for s in subs:
                        c[s].settle()
                        both = logit[s][:, 0:2, :, :].rearrange("p n k h -> p (n k h)")
                        c[s].step(dve.scalar_tensor_tensor(both, both, SLOPE, both, ALU.mult, ALU.max))
                    for s in subs:
                        c[s].settle()
                        dve.tensor_tensor(logit[s][:, 2, :, :], logit[s][:, 0, :, :], logit[s][:, 1, :, :],
                                          ALU.subtract).then_inc(logit_ready[s], 1)
                    for s in subs:
                        dve.wait_ge(cast[s], r + 1)
                        one_hot(s, r + 1)
                    for s in subs:
                        dve.wait_ge(exp_ready[s], r + 1)
                        c[s].step(dve.tensor_tensor(split(val[s][:, :, 0:GF]), split(from_src[s][:, :, 0:GF]),
                                                    spread(val[s][:, :, GF:TF], 3, EXPERTS), ALU.mult))
                    for s in subs:
                        c[s].settle()
                        dve.tensor_tensor(spread_val[s][:, 0:BT * width * TF]
                                          .rearrange("p (k t f) -> p k t f", k=BT, f=TF),
                                          spread(hots[s], 3, TF), spread(val[s][:], 2, width), ALU.mult)\
                            .then_inc(batch_ready[s], 1)
                        c[s].close()

                for s in subs:
                    one_hot(s, 0)
                    dve.sem_inc(batch_ready[s], 1)
                edge_rounds(dve, count, batches)
                dve.wait_ge(sums_ready, 1)
                if wide:
                    for n, at in enumerate((slice(0, HALF), slice(HALF, NF))):
                        size = (at.stop - at.start) * TF
                        dve.tensor_tensor(agg[:, at, :],
                                          psum[:, n * 512:n * 512 + size].rearrange("p (t f) -> p t f", f=TF),
                                          dense[:, at, :], ALU.add).then_inc(sums_read, 1)
                    dve.wait_ge(sums_read, 2)
                else:
                    dve.tensor_copy(agg[:], dense[:]).then_inc(sums_read, 1)
                    for n in range(STARTS):
                        at = slice(n * STRIDE, n * STRIDE + WIN)
                        dve.wait_ge(sums_read, n + 1)
                        dve.tensor_tensor(agg[:, at, :], agg[:, at, :],
                                          psum[:, n * 512:n * 512 + WIN * TF].rearrange("p (t f) -> p t f", f=TF),
                                          ALU.add).then_inc(sums_read, 1)
                    dve.wait_ge(sums_read, STARTS + 1)
            both_paths(dve, path)


def mix_experts(nc, agg, hidden, expert_out, b_gat, gamma, beta, out):
    TF = GF + GH
    with ExitStack() as ctx:
        sb, ps, sem = tools(nc, ctx)
        hid = sb("hid", [128, NF, D])
        eo = sb("eo_m", [128, NF, EXPERTS * D])
        part = [sb(f"part{n}", [128, NF, D]) for n in range(2)]
        rows = sb("rows_m", [128, 3, GF])
        den = sb("den", [128, NF, GH])
        y = sb("y_m", [128, NF, GF])
        y2 = sb("y2_m", [128, NF, GF])
        stat = sb("stat_m", [128, 4, NF])
        half = sb("half_m", [128, NF])
        score = sb("score", [128, NF, EXPERTS])
        rank = sb("rank", [128, NF, EXPERTS])
        better = sb("better", [128, NF])
        gate = sb("gate", [128, NF, EXPERTS])
        rows_in = sem("m_rows_in")
        hid_in = sem("m_hid_in")
        eo_in = sem("m_eo_in")
        half_set = sem("m_half_set")
        var_ready = sem("m_var")
        rstd_ready = sem("m_rstd")
        shifted = sem("m_shifted")
        exped = sem("m_exped")
        chain = sem("m_chain")
        out_parts = sem("m_out_parts")
        out_ready = sem("m_out_ready")
        stored = sem("m_stored")
        block = ctx.enter_context(nc.Block())
        by_node = lambda t: t.rearrange("(b t) f -> b t f", t=NF)

        @block.sync
        def _(sync):
            for n, row in enumerate((b_gat, gamma, beta)):
                sync.dma_start(rows[:, n, :], row.partition_broadcast(128)).then_inc(rows_in, 16)
            sync.dma_start(hid[:], by_node(hidden)).then_inc(hid_in, 16)
            sync.dma_start(eo[:], by_node(expert_out)).then_inc(eo_in, 16)
            sync.wait_ge(out_ready, 1)
            sync.dma_start(out, hid[:]).then_inc(stored, 16)
            sync.wait_ge(stored, 16)

        @block.gpsimd
        def _(pool):
            pool.memset(half[:], -0.5).then_inc(half_set, 1)
            pool.wait_ge(half_set, 1)
            pool.wait_ge(var_ready, 1)
            pool.tensor_tensor(stat[:, 2, :], stat[:, 1, :], half[:], ALU.pow).then_inc(rstd_ready, 1)

        @block.scalar
        def _(act):
            act.wait_ge(shifted, 1)
            act.activation(gate[:], gate[:], ACT.Exp).then_inc(exped, 1)

        @block.vector
        def _(dve):
            ch = Chain(dve, chain, 41, 0)

            def then(ins):
                ch.step(ins)
                ch.settle()

            split = lambda t: t.rearrange("p t (h e) -> p t h e", e=EXPERTS)
            total, var, rstd, mean = (stat[:, n, :] for n in range(4))
            then(dve.tensor_scalar(den[:], agg[:, :, GF:TF], 1e-16, None, ALU.add))
            then(dve.reciprocal(den[:], den[:]))
            then(dve.tensor_tensor(split(y[:]), split(agg[:, :, 0:GF]), spread(den[:], 3, EXPERTS), ALU.mult))
            dve.wait_ge(rows_in, 48)
            then(dve.tensor_tensor(y[:], y[:], spread(rows[:, 0, :], 1, NF), ALU.add))
            then(dve.reduce_sum(total, y[:], AX.X))
            then(dve.scalar_tensor_tensor(y2[:], spread(total, 2, GF), -1.0 / GF, y[:], ALU.mult, ALU.add))
            then(dve.tensor_tensor(y[:], y2[:], y2[:], ALU.mult))
            then(dve.reduce_sum(total, y[:], AX.X))
            dve.tensor_scalar(var, total, 1.0 / GF, EPS, ALU.mult, ALU.add).then_inc(var_ready, 1)
            dve.wait_ge(rstd_ready, 1)
            then(dve.tensor_tensor(y[:], y2[:], spread(rstd, 2, GF), ALU.mult))
            then(dve.tensor_tensor(y2[:], y[:], spread(rows[:, 1, :], 1, NF), ALU.mult))
            then(dve.tensor_tensor(y[:], y2[:], spread(rows[:, 2, :], 1, NF), ALU.add))
            then(dve.reduce_sum(score[:], y[:].rearrange("p t (h e) -> p t e h", e=EXPERTS), AX.X))
            then(dve.tensor_scalar(score[:], score[:], 1.0 / GH, None, ALU.mult))
            for e in range(EXPERTS):
                then(dve.memset(rank[:, :, e], float(e)))
            for e in range(EXPERTS):
                for j in range(e):
                    then(dve.tensor_tensor(better[:], score[:, :, e], score[:, :, j], ALU.is_gt))
                    then(dve.tensor_tensor(rank[:, :, j], rank[:, :, j], better[:], ALU.add))
                    then(dve.tensor_tensor(rank[:, :, e], rank[:, :, e], better[:], ALU.subtract))
            then(dve.reduce_max(mean, score[:], AX.X))
            dve.tensor_tensor(gate[:], score[:], spread(mean, 2, EXPERTS), ALU.subtract).then_inc(shifted, 1)
            dve.wait_ge(exped, 1)
            then(dve.tensor_scalar(rank[:], rank[:], 1.5, None, ALU.is_lt))
            then(dve.tensor_tensor(gate[:], gate[:], rank[:], ALU.mult))
            then(dve.reduce_sum(total, gate[:], AX.X))
            then(dve.reciprocal(var, total))
            then(dve.tensor_tensor(gate[:], gate[:], spread(var, 2, EXPERTS), ALU.mult))
            dve.wait_ge(hid_in, 16)
            dve.wait_ge(eo_in, 16)
            ch.close()
            for e in range(EXPERTS):
                dve.tensor_tensor(part[e % 2][:], eo[:, :, e * D:(e + 1) * D], spread(gate[:, :, e], 2, D), ALU.mult)\
                    .then_inc(out_parts, 1)
                dve.wait_ge(out_parts, 2 * e + 1)
                dve.tensor_tensor(hid[:], hid[:], part[e % 2][:], ALU.add).then_inc(out_parts, 1)
                dve.wait_ge(out_parts, 2 * e + 2)
            dve.sem_inc(out_ready, 1)



def early_fusion(nc, x, txt, ln1_g, ln1_b, W_patch, b_patch, ln2_g, ln2_b, cls, pos, attn_g, attn_b, Wqkv, Wo, bo,
                 ff_g, ff_b, W1, b1, W2, b2, f_g, f_b, gat_w, att_src, att_dst, b_gat, gamma, beta, eW1, eb1, eW2,
                 eb2, edge_index, out):
    def scratch(name, shape):
        return nc.dram_tensor(name, shape, F32).ap()

    tokens = scratch("tokens", (B * NV, D))
    fused = scratch("fused", (NODES, D))
    hidden = scratch("hidden", (NODES, D))
    gat_h = scratch("gat_h", (NODES, GF))
    expert_out = scratch("expert_out", (NODES, EXPERTS * D))
    src_table = scratch("src_table", (NODES, GF + GH))
    with ExitStack() as ctx:
        sb, _, _ = tools(nc, ctx)
        keys_sorted = sb("keys_sorted", [128, COLS])
        count_i = sb("count_i", [128, 1], I32)
        last_counts = sb("last_counts", [128, NF])
        embed_and_sort(nc, x, ln1_g, ln1_b, W_patch, b_patch, ln2_g, ln2_b, cls, pos, tokens, edge_index,
                       keys_sorted, count_i, last_counts)
        agg = sb("agg", [128, NF, GF + GH])
        run_vit(nc, tokens, attn_g, attn_b, Wqkv, Wo, bo, ff_g, ff_b, W1, b1, W2, b2, f_g, f_b, txt, fused)
        fuse_and_expert(nc, fused, gat_w, eW1, eb1, eW2, eb2, hidden, gat_h, expert_out)
        route_edges(nc, keys_sorted, count_i, last_counts, gat_h, att_src, att_dst, src_table, agg)
        mix_experts(nc, agg, hidden, expert_out, b_gat, gamma, beta, out)


_INS = ['x', 'txt', 'L0_tok_ln_p1_g', 'L0_tok_ln_p1_b', 'L0_tok_W_patch', 'L0_tok_b_patch',
        'L0_tok_ln_p2_g', 'L0_tok_ln_p2_b', 'L0_tok_cls', 'L0_tok_pos', 'L0_tok_attn_ln_g',
        'L0_tok_attn_ln_b', 'L0_tok_Wqkv', 'L0_tok_Wo', 'L0_tok_bo', 'L0_tok_ff_ln_g', 'L0_tok_ff_ln_b',
        'L0_tok_W1', 'L0_tok_b1', 'L0_tok_W2', 'L0_tok_b2', 'L0_tok_ln_f_g', 'L0_tok_ln_f_b',
        'L0_ffn_W_gat', 'L0_ffn_att_src', 'L0_ffn_att_dst', 'L0_ffn_b_gat', 'L0_ffn_ln_gamma',
        'L0_ffn_ln_beta', 'L0_ffn_W1', 'L0_ffn_b1', 'L0_ffn_W2', 'L0_ffn_b2', 'L0_ffn_edge_index']
_OUTS = [((B, NF, D), 'float32')]


def kernel(**inputs):
    import numpy as _np
    import concourse.bacc as _bacc
    from concourse import mybir as _mybir
    from concourse.bass_utils import run_bass_kernel_spmd as _run

    nc = _bacc.Bacc("TRN2", target_bir_lowering=False, num_devices=1)
    arrays, args = {}, []
    for name in _INS:
        a = _np.ascontiguousarray(inputs[name])
        arrays[f"in_{name}_dram"] = a
        args.append(nc.dram_tensor(f"in_{name}_dram", a.shape, _mybir.dt.from_np(a.dtype), kind="ExternalInput").ap())
    for i, (shape, dtype) in enumerate(_OUTS):
        dt = _mybir.dt.from_np(_np.dtype(dtype))
        args.append(nc.dram_tensor(f"out_{i}_dram", shape, dt, kind="ExternalOutput").ap())
    early_fusion(nc, *args)
    r = _run(nc, [arrays], core_ids=[0])
    got = tuple(r.results[0][f"out_{i}_dram"] for i in range(len(_OUTS)))
    return got[0]
```

```python
from contextlib import ExitStack

import concourse.bass as bass
from concourse import mybir

F32 = mybir.dt.float32
I32 = mybir.dt.int32
U32 = mybir.dt.uint32
BF16 = mybir.dt.bfloat16
ALU = mybir.AluOpType
ACT = mybir.ActivationFunctionType
AX = mybir.AxisListType

B = 128
IMG = 128
PATCH = 32
GRID = IMG // PATCH
CH = 3
PD = CH * PATCH * PATCH
D = 64
NV = GRID * GRID + 1
NTXT = 32
NF = NV + NTXT
LAYERS = 4
HEADS = 4
DH = 64
MLP = 128
EXPERTS = 4
GH = 4
GF = GH * EXPERTS
NODES = B * NF
EDGES = 262144
EPS = 1e-5
MASK = 32768.0


class Chain:

    def __init__(self, eng, sem, per_round, round_no, before=0):
        self.eng, self.sem, self.per_round, self.round_no, self.n = eng, sem, per_round, round_no, 0
        self.before = before

    def step(self, ins):
        ins.then_inc(self.sem, 1)
        self.n += 1

    def settle(self):
        self.eng.wait_ge(self.sem, self.round_no * self.per_round + (self.before + self.n))

    def close(self):
        assert self.n == self.per_round, self.n


def wait_apart(eng, sem, value, passed):
    eng.wait_ge(sem, value)
    eng.sem_inc(passed, 1)


def spread(ap, at, count):
    shape = list(ap.shape)
    shape.insert(at, count)
    return ap.unsqueeze(at).to_broadcast(shape)


def tools(nc, ctx):
    sems = []

    def give_back():
        if sems:
            nc.clear_and_free_semaphores(sems)
            nc.all_engine_barrier()

    ctx.callback(give_back)

    def sb(name, shape, dt=F32):
        return ctx.enter_context(nc.sbuf_tensor(name, shape, dt))

    def ps(name, shape, dt=F32):
        return ctx.enter_context(nc.psum_tensor(name, shape, dt))

    def sem(name):
        sems.append(nc.alloc_semaphore(name))
        return sems[-1]

    return sb, ps, sem


def block_masks(pool, done, images, tokens, left, right):
    n = 0
    for mask, scale in ((left, 1.0), (right, MASK)):
        reps = mask.shape[1]
        pattern = [[0, reps], [1, images * tokens]]
        used = mask[0:images + 1]
        pool.memset(mask, 0.0).then_inc(done, 1)
        pool.wait_ge(done, n + 1)
        pool.memset(used, scale).then_inc(done, 1)
        pool.wait_ge(done, n + 2)
        pool.affine_select(out=used, in_=used, compare_op=ALU.is_ge, fill=0.0, base=tokens,
                           pattern=pattern, channel_multiplier=-tokens).then_inc(done, 1)
        pool.wait_ge(done, n + 3)
        pool.affine_select(out=used, in_=used, compare_op=ALU.is_ge, fill=0.0, base=-1,
                           pattern=[[0, reps], [-1, images * tokens]], channel_multiplier=tokens).then_inc(done, 1)
        pool.wait_ge(done, n + 4)
        pool.memset(mask[0:1], 1.0 if scale == 1.0 else -MASK).then_inc(done, 1)
        n += 5
    return n


def identity(pool, done, n, ident):
    pool.memset(ident, 0.0).then_inc(done, 1)
    pool.wait_ge(done, n + 1)
    pool.affine_select(out=ident, in_=ident, compare_op=ALU.not_equal, fill=1.0, base=0,
                       pattern=[[-1, ident.shape[1]]], channel_multiplier=1).then_inc(done, 1)
    return n + 2


COLS = EDGES // 128
SRC_BITS = 13
IMG_BITS = 7
KEY_TOP = 0x20000000


def edge_rounds(eng, count, body, first=0, rounds=COLS // 8, together=1):
    with eng.Fori(0, 4) as i:
        at = first + i * (rounds // 4)
        with eng.If(at * 8 < count):
            if rounds == 4 * together:
                body(at)
            else:
                edge_rounds(eng, count, body, at, rounds // 4, together)


def embed_and_sort(nc, x, ln1_g, ln1_b, W, b_patch, ln2_g, ln2_b, cls, pos, tokens, edge_index, keys_sorted,
                   count_i, last_counts):
    GI = 16
    NG = B // GI
    K = CH * PATCH
    NP = GRID * GRID
    GP = GI * NP
    WN = D + 2
    PT = NG * GP // 128
    PREP = 4
    EPI = 12
    HB = 8
    HIST = COLS // HB // 2
    EDGE_PREP = 19
    PURE = 6
    PER_GROUP = (2 * HIST // (NG - PURE)) // 2 * 2
    SEGS = 8
    WIDTH = COLS // SEGS
    TOGETHER = 4
    SLOTS = 72
    two = range(2)
    with ExitStack() as ctx:
        sb, ps, sem = tools(nc, ctx)
        pix = [sb(f"pix{s}", [K, GP * PATCH]) for s in two]
        squares = sb("squares", [K, GP * PATCH])
        w_raw = sb("w_raw", [K, PATCH, D])
        w_ext = sb("w_ext", [K, PATCH, WN])
        w_bias = sb("w_bias", [K, PATCH, D])
        g_in = sb("g_in", [K, PATCH])
        b_in = sb("b_in", [K, PATCH])
        w_sum = sb("w_sum", [K, 2, D])
        pick_sq = sb("pick_sq", [K, WN])
        ones = sb("ones_e", [128, 128])
        ident = sb("ident_e", [WN, WN])
        col_sum = sb("col_sum", [128, D])
        const = sb("const", [128, D])
        rows = sb("rows_e", [128, 3, D])
        posP = sb("posP", [128, D])
        cls_t = sb("cls_t", [1, 2, D])
        cls_all = sb("cls_all", [128, D])
        stat = sb("stat_e", [128, 4, PT])
        half = sb("half_e", [128, PT])
        accT = sb("accT", [WN, NG * GP])
        y = sb("y_e", [128, PT, D])
        y2 = sb("y2_e", [128, PT, D])
        acc = [ps(f"acc_e{s}", [WN, 512]) for s in two]
        turned = ps("turned_e", [128, PT, 128])
        aux = ps("aux_e", [128, 3, D])
        src = sb("src", [128, COLS], I32)
        dst = sb("dst", [128, COLS], I32)
        dst_ok = sb("dst_ok", [128, COLS])
        keys = sb("keys", [128, COLS])
        img_i = sb("img_i", [128, COLS], I32)
        img_b = sb("img_b", [128, COLS], BF16)
        tok_b = sb("tok_b", [128, COLS], BF16)
        iota_i = sb("iota_i", [128, 128], I32)
        iota_b = sb("iota_pb", [128, 128, HB], BF16)
        count = sb("count", [128, 4])
        seg = sb("seg", [128, SEGS])
        seg_i = sb("seg_i", [128, 1], I32)
        top8 = sb("top8", [128, 8])
        hot_img = [sb(f"hot_img_p{s}", [128, 128, HB], BF16) for s in two]
        hot_tok = [sb(f"hot_tok_p{s}", [128, NF, HB], BF16) for s in two]
        zeros = sb("zeros_p", [128, 128], BF16)
        hist = ps("hist", [128, NF])

        params_in = sem("e_params_in")
        pix_in = [sem(f"e_pix_in{s}") for s in two]
        pix_used = [sem(f"e_pix_used{s}") for s in two]
        squared = sem("e_squared")
        squares_used = sem("e_squares_used")
        consts_set = sem("e_consts_set")
        ident_set = sem("e_ident_set")
        pick_set = sem("e_pick_set")
        w_ready = sem("e_w_ready")
        w_here = sem("e_w_here")
        sums_ready = sem("e_sums_ready")
        cls_done = sem("e_cls_done")
        prep = sem("e_prep")
        acc_ready = [sem(f"e_acc_ready{s}") for s in two]
        acc_read = [sem(f"e_acc_read{s}") for s in two]
        turned_ready = sem("e_turned_ready")
        turned_read = sem("e_turned_read")
        var_ready = sem("e_var_ready")
        rstd_ready = sem("e_rstd_ready")
        chain_sem = sem("e_chain")
        y_ready = sem("e_y_ready")
        out_ready = sem("e_out_ready")
        stored = sem("e_stored")
        edges_in = sem("p_edges_in")
        iota_ready = sem("p_iota")
        zeros_ready = sem("p_zeros")
        edge_prep = sem("p_prep")
        counted = sem("p_counted")
        count_max = sem("p_count_max")
        picked = [sem(f"p_picked{q}") for q in two]
        count_ready = sem("p_count_ready")
        sort_chain = sem("p_sort_chain")
        hot_ready = [sem(f"p_hot_ready{s}") for s in two]
        hot_used = [sem(f"p_hot_used{s}") for s in two]
        hist_ready = sem("p_hist_ready")
        passed = sem("p_passed")
        block = ctx.enter_context(nc.Block())

        tok_view = tokens[0:B * NV, :].rearrange("(b t) d -> b t d", t=NV)
        per_patch = "(c i j) -> (c i) j"
        N_PARAMS = 16 * (3 + 3 + 128 // NP + 2)

        @block.sync
        def _(sync):
            sync.dma_start(dst[:], edge_index[1].rearrange("(p n) -> p n", p=128)).then_inc(edges_in, 16)
            sync.dma_start(src[:], edge_index[0].rearrange("(p n) -> p n", p=128)).then_inc(edges_in, 16)
            sync.dma_start(w_raw[:], W.rearrange("(c i j) d -> (c i) j d", c=CH, i=PATCH)).then_inc(params_in, 16)
            sync.dma_start(g_in[:], ln1_g.rearrange(per_patch, c=CH, i=PATCH)).then_inc(params_in, 16)
            sync.dma_start(b_in[:], ln1_b.rearrange(per_patch, c=CH, i=PATCH)).then_inc(params_in, 16)
            for n, row in enumerate((b_patch, ln2_g, ln2_b)):
                sync.dma_start(rows[:, n, :], row.partition_broadcast(128)).then_inc(params_in, 16)
            for b in range(128 // NP):
                sync.dma_start(posP[b * NP:(b + 1) * NP, :], pos[0, 1:NV, :]).then_inc(params_in, 16)
            sync.dma_start(cls_t[:, 0, :], cls[0]).then_inc(params_in, 16)
            sync.dma_start(cls_t[:, 1, :], pos[0, 0:1, :]).then_inc(params_in, 16)
            sync.wait_ge(cls_done, 1)
            sync.dma_start(tok_view[:, 0, :], cls_all[:]).then_inc(stored, 16)
            sync.wait_ge(out_ready, 1)
            for t in range(PT):
                images = slice(t * (128 // NP), (t + 1) * (128 // NP))
                sync.dma_start(tok_view[images, 1:NV, :], y2[:, t, :]).then_inc(stored, 16)
            sync.wait_ge(stored, 16 * (1 + PT))

        @block.gpsimd
        def _(pool):
            pool.iota(iota_i[:], pattern=[[1, 128]], base=0, channel_multiplier=0).then_inc(iota_ready, 1)
            pool.memset(zeros[:], 0.0).then_inc(zeros_ready, 1)
            pool.memset(ones[:], 1.0).then_inc(consts_set, 1)
            pool.memset(half[:], -0.5).then_inc(consts_set, 1)
            pool.memset(pick_sq[:], 0.0).then_inc(pick_set, 1)
            pool.wait_ge(pick_set, 1)
            pool.memset(pick_sq[:, D + 1:WN], 1.0).then_inc(pick_set, 1)
            identity(pool, ident_set, 0, ident[:])
            pool.wait_ge(consts_set, 2)
            pool.wait_ge(counted, 2)
            pool.partition_all_reduce(count[:, 2:4], count[:, 0:2], 128, bass.bass_isa.ReduceOp.max)\
                .then_inc(count_max, 1)
            with pool.Fori(0, 2) as n:
                pool.wait_ge(var_ready, n + 1)
                pool.tensor_tensor(stat[:, 2, :], stat[:, 1, :], half[:], ALU.pow).then_inc(rstd_ready, 1)

        @block.scalar
        def _(act):
            def load(g, s, nth):
                act.wait_ge(pix_used[s], 2 * nth)
                for c in range(CH):
                    for gy in range(GRID):
                        to = pix[s][c * PATCH:(c + 1) * PATCH, :].rearrange("i (b gy x) -> i b gy x", b=GI, gy=GRID)
                        act.dma_start(to[:, :, gy, :],
                                      x[bass.ds(g * GI, GI), c, gy * PATCH:(gy + 1) * PATCH, :]
                                      .rearrange("b i x -> i b x")).then_inc(pix_in[s], 16)

            for s in two:
                act.sem_inc(pix_used[s], 2)
            act.sem_inc(squares_used, 1)
            for s in two:
                load(s, s, 1)

            def pair(m, more):
                for s in two:
                    act.wait_ge(pix_in[s], 16 * CH * GRID * (m + 1))
                    act.wait_ge(squares_used, 2 * m + s + 1)
                    act.activation(squares[:], pix[s][:], ACT.Square).then_inc(squared, 1)
                    act.wait_ge(squared, 2 * m + s + 1)
                    act.sem_inc(pix_used[s], 1)
                    act.wait_ge(acc_ready[s], m + 1)
                    act.activation(accT[:, bass.ds((2 * m + s) * GP, GP)], acc[s][:, 0:GP], ACT.Copy).then_inc(acc_read[s], 1)
                    if more:
                        load(2 * m + s + 2, s, m + 2)

            with act.Fori(0, NG // 2 - 1) as m:
                pair(m, True)
            pair(NG // 2 - 1, False)

        @block.tensor
        def _(pe):
            pe.wait_ge(w_ready, 2)
            for n in range(2):
                pe.matmul(aux[:, n, :], ones[0:K, :], w_sum[:, n, :], start=True, stop=True)
            pe.matmul(aux[:, 2, :], ones[0:1, :], cls_t[0:1, 0, :], start=True, stop=False)
            pe.matmul(aux[:, 2, :], ones[0:1, :], cls_t[0:1, 1, :], start=False, stop=True).then_inc(sums_ready, 1)
            pe.wait_ge(zeros_ready, 1)
            pe.matmul(hist[:], zeros[:], zeros[:, 0:NF], start=True, stop=False, skip_group_check=True)
            pe.wait_ge(pick_set, 2)
            pe.wait_ge(ident_set, 2)
            for s in two:
                pe.sem_inc(acc_read[s], 1)

            def count_edges(q, n):
                pe.wait_ge(hot_ready[q], n + 1)
                for k in range(HB):
                    last = pe.matmul(hist[:], hot_img[q][:, :, k], hot_tok[q][:, :, k],
                                     start=False, stop=False, skip_group_check=True)
                last.then_inc(hot_used[q], 1)

            def group(m, s, first_count=None):
                wait_apart(pe, pix_in[s], 16 * CH * GRID * (m + 1), passed)
                wait_apart(pe, acc_read[s], m + 1, passed)
                counts = 0
                for n in range(2 * PATCH):
                    j = n % PATCH
                    if n == PATCH:
                        last.then_inc(pix_used[s], 1)
                        wait_apart(pe, squared, 2 * m + s + 1, passed)
                    if n < PATCH:
                        last = pe.matmul(acc[s][:, 0:GP], w_ext[:, j, :], pix[s][:, j:GP * PATCH:PATCH],
                                         start=(j == 0), stop=False)
                    else:
                        last = pe.matmul(acc[s][:, 0:GP], pick_sq[:], squares[:, j:GP * PATCH:PATCH],
                                         start=False, stop=(j == PATCH - 1))
                    if n == 2 * PATCH - 1:
                        last.then_inc(acc_ready[s], 1)
                    while first_count is not None and counts * 2 * PATCH < PER_GROUP * (n + 1) and n != PATCH - 1:
                        count_edges(counts % 2, first_count + counts // 2)
                        counts += 1
                pe.wait_ge(acc_ready[s], m + 1)
                pe.sem_inc(squares_used, 1)

            with pe.Fori(0, PURE // 2) as m:
                for s in two:
                    group(m, s)
            for g in range(PURE, NG):
                group(g // 2, g % 2, (g - PURE) * (PER_GROUP // 2))
            for s in two:
                pe.wait_ge(acc_read[s], NG // 2 + 1)
            for t in range(PT):
                last = pe.transpose(turned[:, t, 0:WN], accT[:, t * 128:(t + 1) * 128], ident[:])
            last.then_inc(turned_ready, 1)
            for n in range((NG - PURE) * PER_GROUP // 2, HIST):
                for q in two:
                    count_edges(q, n)
            pe.matmul(hist[:], zeros[:], zeros[:, 0:NF], start=False, stop=True, skip_group_check=True)\
                .then_inc(hist_ready, 1)

        @block.vector
        def _(dve):
            ch = Chain(dve, prep, PREP, 0)
            dve.wait_ge(params_in, N_PARAMS)
            dve.wait_ge(consts_set, 2)
            ch.step(dve.tensor_tensor(w_bias[:], w_raw[:], spread(b_in[:], 2, D), ALU.mult))
            ch.step(dve.tensor_tensor(w_ext[:, :, 0:D], w_raw[:], spread(g_in[:], 2, D), ALU.mult))
            ch.step(dve.memset(w_ext[:, :, D:D + 1], 1.0))
            ch.step(dve.memset(w_ext[:, :, D + 1:WN], 0.0))
            ch.settle()
            ch.close()
            dve.reduce_sum(w_sum[:, 0, :], w_bias[:].rearrange("p n d -> p d n"), AX.X).then_inc(w_ready, 1)
            dve.reduce_sum(w_sum[:, 1, :], w_ext[:, :, 0:D].rearrange("p n d -> p d n"), AX.X).then_inc(w_ready, 1)
            ch = Chain(dve, edge_prep, EDGE_PREP, 0)
            dve.wait_ge(iota_ready, 1)
            ch.step(dve.tensor_copy(iota_b[:], spread(iota_i[:], 2, HB)))
            dve.wait_ge(edges_in, 32)
            work = keys
            ch.step(dve.tensor_scalar(dst_ok[:], dst[:], float(NODES), None, ALU.is_lt))
            ch.step(dve.tensor_scalar(img_i[:], dst[:], -float(NF // 2), 1.0 / NF, ALU.add, ALU.mult))
            ch.step(dve.memset(keys_sorted[:], 0.0))
            ch.step(dve.memset(top8[:], 0.0))
            ch.settle()
            ch.step(dve.scalar_tensor_tensor(tok_b[:], img_i[:], -float(NF), dst[:], ALU.mult, ALU.add))
            ch.step(dve.scalar_tensor_tensor(work[:], src[:], float(NODES - 1), dst_ok[:], ALU.is_lt, ALU.mult))
            ch.settle()
            ch.step(dve.tensor_copy(dst[:], tok_b[:]))
            ch.step(dve.reduce_sum(seg[:], work[:].rearrange("p (g n) -> p g n", g=SEGS), AX.X))
            ch.step(dve.tensor_tensor(dst_ok[:], dst_ok[:], work[:], ALU.subtract))
            ch.settle()
            dve.reduce_sum(count[:, 0:1], seg[:], AX.X).then_inc(counted, 1)
            dve.reduce_max(count[:, 1:2], seg[:], AX.X).then_inc(counted, 1)
            ch.step(dve.scalar_tensor_tensor(dst_ok[:], dst_ok[:], -256.0, img_i[:], ALU.mult, ALU.add))
            ch.step(dve.tensor_scalar(dst[:], dst[:], IMG_BITS, None, ALU.logical_shift_left))
            ch.settle()
            ch.step(dve.tensor_scalar(img_b[:], dst_ok[:], 256.0, None, ALU.add))
            ch.step(dve.tensor_tensor(dst[:], dst[:], img_i[:], ALU.bitwise_or))
            ch.settle()
            ch.step(dve.tensor_scalar(dst[:], dst[:], SRC_BITS, KEY_TOP, ALU.logical_shift_left, ALU.bitwise_or))
            ch.settle()
            ch.step(dve.tensor_tensor(dst[:], dst[:], src[:], ALU.bitwise_or))
            ch.settle()
            ch.step(dve.tensor_tensor(keys[:], dst[:].bitcast(F32), work[:], ALU.mult))
            dve.wait_ge(count_max, 1)
            ch.step(dve.tensor_copy(count_i[:], count[:, 2:3]))
            ch.step(dve.tensor_copy(seg_i[:], count[:, 3:4]))
            ch.settle()
            ch.close()
            edges_left = dve.value_load(count_i[0:1, 0:1], min_val=0, max_val=COLS)
            most = dve.value_load(seg_i[0:1, 0:1], min_val=0, max_val=COLS // SEGS)

            dve.wait_ge(sums_ready, 1)
            dve.tensor_tensor(const[:], aux[:, 0, :], rows[:, 0, :], ALU.add).then_inc(w_here, 1)
            dve.tensor_copy(col_sum[:], aux[:, 1, :]).then_inc(w_here, 1)
            dve.tensor_copy(cls_all[:], aux[:, 2, :]).then_inc(cls_done, 1)
            dve.wait_ge(w_here, 2)
            for s in two:
                dve.sem_inc(hot_used[s], 1)
            dve.sem_inc(sort_chain, 1)

            few = dst[:, 0:SEGS * SLOTS].bitcast(F32)

            def sort_rounds(source):
                def body(r):
                    c = Chain(dve, sort_chain, 3, r, before=1)
                    for n in range(TOGETHER):
                        c.settle()
                        dve.sem_inc(passed, 1)
                        c.step(dve.max(top8[:], source))
                        c.settle()
                        c.step(dve.tensor_copy(keys_sorted[:, bass.ds((r + n) * 8, 8)], top8[:]))
                        c.step(dve.match_replace(source, top8[:], source, 0.0))
                return body

            with dve.If(most < SLOTS + 1):
                for g in range(0, SEGS, 2):
                    pairs = [Chain(dve, picked[q], SLOTS // 8 * 2, g // 2) for q in two]
                    segments = [keys[:, (g + q) * WIDTH:(g + q + 1) * WIDTH] for q in two]
                    for n in range(SLOTS // 8):
                        eights = [few[:, (g + q) * SLOTS + n * 8:(g + q) * SLOTS + (n + 1) * 8] for q in two]
                        for q in two:
                            if n:
                                pairs[q].settle()
                            pairs[q].step(dve.max(eights[q], segments[q]))
                        for q in two:
                            pairs[q].settle()
                            pairs[q].step(dve.match_replace(segments[q], eights[q], segments[q], 0.0))
                    for q in two:
                        pairs[q].close()
                for q in two:
                    dve.wait_ge(picked[q], SEGS * (SLOTS // 8))
                dve.sem_inc(passed, 1)
                edge_rounds(dve, edges_left, sort_rounds(few), together=TOGETHER)
            with dve.If(most > SLOTS):
                edge_rounds(dve, edges_left, sort_rounds(keys[:]), together=TOGETHER)

            with dve.Fori(0, HIST) as n:
                for q in two:
                    at = bass.ds((n * 2 + q) * HB, HB)
                    dve.wait_ge(hot_used[q], n + 1)
                    dve.tensor_tensor(hot_img[q][:], spread(img_b[:, at], 1, 128), iota_b[:], ALU.is_equal)
                    dve.tensor_tensor(hot_tok[q][:], spread(tok_b[:, at], 1, NF), iota_b[:, 0:NF, :],
                                      ALU.is_equal).then_inc(hot_ready[q], 1)

            mean, var, rstd, tot = (stat[:, n, :] for n in range(4))
            ch = Chain(dve, chain_sem, EPI, 0)
            dve.wait_ge(turned_ready, 1)
            ch.step(dve.tensor_scalar(mean, turned[:, :, D], 1.0 / PD, None, ALU.mult))
            ch.step(dve.tensor_scalar(tot, turned[:, :, D + 1], 1.0 / PD, EPS, ALU.mult, ALU.add))
            ch.settle()
            ch.step(dve.tensor_tensor(var, mean, mean, ALU.mult))
            ch.step(dve.tensor_tensor(y2[:], spread(mean, 2, D), spread(col_sum[:], 1, PT), ALU.mult))
            ch.settle()
            dve.tensor_tensor(var, tot, var, ALU.subtract).then_inc(var_ready, 1)
            dve.tensor_tensor(y[:], turned[:, :, 0:D], y2[:], ALU.subtract).then_inc(turned_read, 1)
            dve.wait_ge(turned_read, 1)
            dve.wait_ge(rstd_ready, 1)
            ch.step(dve.tensor_tensor(y2[:], y[:], spread(rstd, 2, D), ALU.mult))
            ch.settle()
            ch.step(dve.tensor_tensor(y[:], y2[:], spread(const[:], 1, PT), ALU.add))
            ch.settle()
            ch.step(dve.reduce_sum(tot, y[:], AX.X))
            ch.settle()
            ch.step(dve.scalar_tensor_tensor(y2[:], spread(tot, 2, D), -1.0 / D, y[:], ALU.mult, ALU.add))
            ch.settle()
            ch.step(dve.tensor_tensor(y[:], y2[:], y2[:], ALU.mult))
            ch.settle()
            ch.step(dve.reduce_sum(tot, y[:], AX.X))
            ch.settle()
            dve.tensor_scalar(var, tot, 1.0 / D, EPS, ALU.mult, ALU.add).then_inc(var_ready, 1)
            dve.wait_ge(rstd_ready, 2)
            ch.step(dve.tensor_tensor(y[:], y2[:], spread(rstd, 2, D), ALU.mult))
            ch.settle()
            ch.step(dve.tensor_tensor(y2[:], y[:], spread(rows[:, 1, :], 1, PT), ALU.mult))
            ch.settle()
            dve.tensor_tensor(y[:], y2[:], spread(rows[:, 2, :], 1, PT), ALU.add).then_inc(y_ready, 1)
            dve.wait_ge(y_ready, 1)
            dve.tensor_tensor(y2[:], y[:], spread(posP[:], 1, PT), ALU.add).then_inc(out_ready, 1)
            ch.close()
            dve.wait_ge(hist_ready, 1)
            dve.tensor_copy(last_counts[:], hist[:]).then_inc(count_ready, 1)
            dve.wait_ge(count_ready, 1)


def run_vit(nc, tokens, ln_g, ln_b, Wqkv, Wo, bo, ff_g, ff_b, W1, b1, W2, b2, f_g, f_b, txt, fused):
    IPT = 7
    T = IPT * NV
    NT = 2
    C = NT * T
    SUBS = 2
    FULL = B // IPT
    PART = B - FULL * IPT
    CHUNKS = -(-B // (IPT * NT * SUBS))
    TILES = CHUNKS * NT * SUBS
    HD = HEADS * DH
    ROUNDS = LAYERS * CHUNKS
    FRONT = 7
    BACK = 11
    SCALE = DH ** -0.5
    subs = range(SUBS)
    with ExitStack() as ctx:
        sb, ps, sem = tools(nc, ctx)
        X = sb("X", [T, TILES, D])
        all_wqkv = sb("all_wqkv", [D, LAYERS, 3 * HD])
        all_wo = sb("all_wo", [128, LAYERS, (HD // 128) * D])
        all_w1 = sb("all_w1", [D, LAYERS, MLP])
        all_w2 = sb("all_w2", [MLP, LAYERS, D])
        all_b1 = sb("all_b1", [MLP, LAYERS])
        all_bias = sb("all_bias", [T, 2, LAYERS * D])
        all_gains = sb("all_gains", [D, 4, LAYERS])
        wqkv = sb("wqkv", [D, 3 * HD])
        wo = sb("wo", [128, HD // 128, D])
        w1 = sb("w1v", [D, MLP])
        w2 = sb("w2v", [MLP, D])
        b1c = sb("b1c", [MLP, 1])
        bias = [sb(f"bias_v{n}", [T, D]) for n in range(2)]
        gains = [sb(f"gains_v{n}", [D, 2]) for n in range(2)]
        rows = sb("rows_v", [T, 2, D])
        ident = sb("ident_v", [T, T])
        maskL = sb("maskL_v", [128, 1, T])
        maskR = sb("maskR_v", [128, HEADS, T])
        mask_left = sb("mask_left_v", [128, T], BF16)
        mask_right = sb("mask_right_v", [128, HEADS * T], BF16)
        half = sb("half_v", [T, NT])
        xc = [sb(f"xc_v{s}", [T, NT, D]) for s in subs]
        xh = [sb(f"xh_v{s}", [T, NT, D]) for s in subs]
        stat = [sb(f"stat_v{s}", [T, 3, NT]) for s in subs]
        hT = [sb(f"hT_v{s}", [D, C]) for s in subs]
        qz = [sb(f"qz_v{s}", [128, HEADS, C]) for s in subs]
        kT = [sb(f"kT_v{s}", [128, 2, C]) for s in subs]
        v = [sb(f"v_v{s}", [T, NT, HD]) for s in subs]
        P = [sb(f"P_v{s}", [T, NT * HEADS, T]) for s in subs]
        mx = [sb(f"mx_v{s}", [T, 2, NT * HEADS]) for s in subs]
        pT = [sb(f"pT_v{s}", [T, NT, HEADS * T]) for s in subs]
        oT = [sb(f"oT_v{s}", [128, 2, C]) for s in subs]
        act1 = [sb(f"act1_v{s}", [MLP, C]) for s in subs]
        xf = sb("xf", [T, TILES, D])
        yf = sb("yf", [T, TILES, D])
        fstat = sb("fstat", [T, 3, TILES])
        fhalf = sb("fhalf", [T, TILES])
        psum = ps("psum_v", [128, 8, 512])

        tokens_in = sem("v_tokens_in")
        weights_in = sem("v_weights_in")
        front_loaded = sem("v_front_loaded")
        back_loaded = sem("v_back_loaded")
        consts = sem("v_consts")
        masks_ready = sem("v_masks_ready")
        padded = sem("v_padded")
        zeroed = sem("v_zeroed")
        front = [sem(f"v_front{s}") for s in subs]
        back = [sem(f"v_back{s}") for s in subs]
        var_ready = [sem(f"v_var{s}") for s in subs]
        rstd_ready = [sem(f"v_rstd{s}") for s in subs]
        xh_ready = [sem(f"v_xh{s}") for s in subs]
        t_ready = [sem(f"v_t{s}") for s in subs]
        hT_ready = [sem(f"v_hT{s}") for s in subs]
        qk_ready = [sem(f"v_qk{s}") for s in subs]
        v_ready = [sem(f"v_v{s}") for s in subs]
        qk_out = [sem(f"v_qk_out{s}") for s in subs]
        v_out = [sem(f"v_v_out{s}") for s in subs]
        s_ready = [sem(f"v_s{s}") for s in subs]
        shifted = [sem(f"v_shifted{s}") for s in subs]
        exped = [sem(f"v_exped{s}") for s in subs]
        p_ready = [sem(f"v_p{s}") for s in subs]
        pT_ready = [sem(f"v_pT{s}") for s in subs]
        pT_out = [sem(f"v_pT_out{s}") for s in subs]
        o_ready = [sem(f"v_o{s}") for s in subs]
        o_out = [sem(f"v_o_out{s}") for s in subs]
        wo_ready = [sem(f"v_wo{s}") for s in subs]
        h1_ready = [sem(f"v_h1{s}") for s in subs]
        gelu_ready = [sem(f"v_gelu{s}") for s in subs]
        w2_ready = [sem(f"v_w2{s}") for s in subs]
        final = sem("v_final")
        pe_passed = sem("v_pe_passed")
        pool_passed = sem("v_pool_passed")
        dve_passed = sem("v_dve_passed")
        fvar = sem("v_fvar")
        frstd = sem("v_frstd")
        out_ready = sem("v_out_ready")
        stored = sem("v_stored")
        block = ctx.enter_context(nc.Block())

        def bank(s, n):
            return psum[:, SUBS * 2 * s + n, :]

        def tiles(c, s):
            return bass.ds((c * SUBS + s) * NT, NT)

        @block.sync
        def _(sync):
            sync.dma_start(X[:, 0:FULL, :], tokens[0:FULL * T].rearrange("(n p) d -> p n d", p=T))\
                .then_inc(tokens_in, 16)
            sync.wait_ge(padded, 1)
            sync.dma_start(X[0:PART * NV, FULL, :], tokens[FULL * T:B * NV]).then_inc(tokens_in, 16)
            sync.dma_start(rows[:, 0, :], f_g.partition_broadcast(T)).then_inc(tokens_in, 16)
            sync.dma_start(rows[:, 1, :], f_b.partition_broadcast(T)).then_inc(tokens_in, 16)
            fused_view = fused.rearrange("(b t) d -> b t d", t=NF)
            sync.dma_start(fused_view[:, NV:NF, :], txt).then_inc(stored, 16)
            for to, source in ((all_wqkv[:], Wqkv.rearrange("l k n -> k l n")),
                               (all_wo[:].rearrange("k l (c n) -> k (l c) n", n=D),
                                Wo.rearrange("l (c k) n -> k (l c) n", k=128)),
                               (all_w1[:], W1.rearrange("l k n -> k l n")),
                               (all_w2[:], W2.rearrange("l k n -> k l n")),
                               (all_bias[:, 0, :], bo.rearrange("l k -> (l k)").partition_broadcast(T)),
                               (all_bias[:, 1, :], b2.rearrange("l k -> (l k)").partition_broadcast(T))):
                sync.dma_start(to, source).then_inc(weights_in, 16)
            for l in range(LAYERS):
                sync.dma_start(all_b1[:, l:l + 1], b1[l:l + 1].rearrange("l k -> k l")).then_inc(weights_in, 16)
                for n, col in enumerate((ln_g, ln_b, ff_g, ff_b)):
                    sync.dma_start(all_gains[:, n, l:l + 1], col[l:l + 1].rearrange("l k -> k l"))\
                        .then_inc(weights_in, 16)
            sync.wait_ge(out_ready, 1)
            for i in range(IPT):
                sync.dma_start(fused_view[i:FULL * IPT:IPT, 0:NV, :].rearrange("n t d -> t n d"),
                               xf[i * NV:(i + 1) * NV, 0:FULL, :]).then_inc(stored, 16)
            for i in range(PART):
                sync.dma_start(fused_view[FULL * IPT + i, 0:NV, :],
                               xf[i * NV:(i + 1) * NV, FULL, :]).then_inc(stored, 16)
            sync.wait_ge(stored, 16 * (1 + IPT + PART))

        @block.gpsimd
        def _(pool):
            pool.memset(X[:, FULL:, :], 0.0).then_inc(padded, 1)
            n = block_masks(pool, consts, IPT, NV, maskL[:], maskR[:])
            n = identity(pool, consts, n, ident[:])
            pool.memset(half[:], -0.5).then_inc(consts, 1)
            pool.memset(fhalf[:], -0.5).then_inc(consts, 1)
            pool.wait_ge(consts, n + 2)

            def front_weights(l):
                one = bass.ds(l, 1)
                pool.tensor_copy(wqkv[:].unsqueeze(1), all_wqkv[:, one, :])
                pool.tensor_copy(gains[0][:].unsqueeze(2), all_gains[:, 0:2, one])
                pool.tensor_copy(bias[0][:], all_bias[:, 0, bass.ds(l * D, D)]).then_inc(front_loaded, CHUNKS)

            def back_weights(l):
                one = bass.ds(l, 1)
                pool.tensor_copy(wo[:].rearrange("k (l c) n -> k l (c n)", l=1), all_wo[:, one, :])
                pool.tensor_copy(w1[:].unsqueeze(1), all_w1[:, one, :])
                pool.tensor_copy(w2[:].unsqueeze(1), all_w2[:, one, :])
                pool.tensor_copy(b1c[:], all_b1[:, one])
                pool.tensor_copy(gains[1][:].unsqueeze(2), all_gains[:, 2:4, one])
                pool.tensor_copy(bias[1][:], all_bias[:, 1, bass.ds(l * D, D)]).then_inc(back_loaded, CHUNKS)

            def rstd(s, n):
                pool.wait_ge(var_ready[s], n)
                pool.tensor_tensor(stat[s][:, 2, :], stat[s][:, 1, :], half[:], ALU.pow).then_inc(rstd_ready[s], 1)

            def body(r, l=None, more=True):
                rstd(1, 2 * r + 1)
                rstd(0, 2 * r + 2)
                if l is not None:
                    pool.wait_ge(v_out[1], r + 1)
                    pool.sem_inc(pool_passed, 1)
                    front_weights(l + 1)
                if more:
                    rstd(0, 2 * r + 3)
                rstd(1, 2 * r + 2)
                if l is not None:
                    pool.wait_ge(back[1], BACK * r + (BACK + 1))
                    pool.sem_inc(pool_passed, 1)
                    back_weights(l + 1)

            pool.wait_ge(weights_in, 16 * (6 + 5 * LAYERS))
            front_weights(0)
            back_weights(0)
            rstd(0, 1)
            with pool.Fori(0, LAYERS - 1) as l:
                with pool.Fori(0, CHUNKS - 1) as c:
                    body(l * CHUNKS + c)
                body(l * CHUNKS + (CHUNKS - 1), l)
            with pool.Fori(ROUNDS - CHUNKS, ROUNDS - 1) as r:
                body(r)
            body(ROUNDS - 1, more=False)
            pool.wait_ge(fvar, 1)
            pool.tensor_tensor(fstat[:, 2, :], fstat[:, 1, :], fhalf[:], ALU.pow).then_inc(frstd, 1)

        N_CONSTS = 10 + 2 + 2

        @block.scalar
        def _(act):
            def normalised(s, r, nth):
                act.wait_ge((front_loaded, back_loaded)[nth - 1], r + 1)
                act.wait_ge(t_ready[s], 2 * r + nth)
                act.activation(hT[s][:], bank(s, 3)[0:D, 0:C], ACT.Identity, bias=gains[nth - 1][:, 1:2],
                               scale=gains[nth - 1][:, 0:1]).then_inc(hT_ready[s], 1)

            def queries_keys(s, r):
                act.wait_ge(qk_ready[s], r + 1)
                q = bank(s, 0)[:, 0:2 * C].rearrange("p (h c) -> p h c", h=2)
                act.activation(qz[s][0:DH, 0:HEADS:2, :], q[0:DH], ACT.Copy).then_inc(qk_out[s], 1)
                act.activation(qz[s][DH:128, 1:HEADS:2, :], q[DH:128], ACT.Copy).then_inc(qk_out[s], 1)
                act.activation(kT[s][:], bank(s, 1)[:, 0:2 * C].rearrange("p (h c) -> p h c", h=2),
                               ACT.Copy).then_inc(qk_out[s], 1)

            def exps(s, r):
                for t in range(NT):
                    p = P[s][:, t * HEADS:(t + 1) * HEADS, :]
                    act.wait_ge(shifted[s], NT * r + (t + 1))
                    act.activation(p, p, ACT.Exp, scale=SCALE).then_inc(exped[s], 1)

            def half_round(a, ra, b, rb):
                for t in range(NT):
                    act.wait_ge(pT_ready[b], NT * rb + (t + 1))
                    act.activation(pT[b][:, t, :], bank(b, 2 + t)[0:T, 0:HEADS * T], ACT.Copy).then_inc(pT_out[b], 1)
                if ra is not None:
                    normalised(a, ra, 1)
                act.wait_ge(o_ready[b], rb + 1)
                act.activation(oT[b][:], bank(b, 0)[:, 0:2 * C].rearrange("p (h c) -> p h c", h=2),
                               ACT.Copy).then_inc(o_out[b], 1)
                if ra is not None:
                    queries_keys(a, ra)
                normalised(b, rb, 2)
                act.wait_ge(h1_ready[b], rb + 1)
                act.activation(act1[b][:], bank(b, 2)[:, 0:C], ACT.Gelu, bias=b1c[:]).then_inc(gelu_ready[b], 1)
                if ra is not None:
                    exps(a, ra)

            normalised(0, 0, 1)
            queries_keys(0, 0)
            exps(0, 0)
            with act.Fori(0, ROUNDS - 1) as r:
                half_round(1, r, 0, r)
                half_round(0, r + 1, 1, r)
            half_round(1, ROUNDS - 1, 0, ROUNDS - 1)
            half_round(None, None, 1, ROUNDS - 1)

        @block.tensor
        def _(pe):
            pe.wait_ge(consts, N_CONSTS)
            pe.wait_ge(zeroed, 1)
            pe.wait_ge(masks_ready, 2)

            def keep_busy(s, n, count):
                for _ in range(count):
                    pe.matmul(bank(s, n)[0:T, 0:HEADS * T], mask_left[:], mask_right[:], start=True, stop=True,
                              skip_group_check=True)

            def transposed(s, n):
                wait_apart(pe, xh_ready[s], n, pe_passed)
                for t in range(NT):
                    last = pe.transpose(bank(s, 3)[0:D, t * T:(t + 1) * T], xh[s][:, t, :], ident[:])
                last.then_inc(t_ready[s], 1)

            def queries_keys(s, r):
                pe.wait_ge(front_loaded, r + 1)
                pe.wait_ge(hT_ready[s], 2 * r + 1)
                for m in range(4):
                    last = pe.matmul(bank(s, m // 2)[:, (m % 2) * C:(m % 2 + 1) * C],
                                     wqkv[:, m * 128:(m + 1) * 128], hT[s][:], start=True, stop=True)
                last.then_inc(qk_ready[s], 1)

            def values(s, r):
                for t in range(NT):
                    last = pe.matmul(bank(s, 2)[0:T, t * HD:(t + 1) * HD], hT[s][:, t * T:(t + 1) * T],
                                     wqkv[:, 2 * HD:3 * HD], start=True, stop=True)
                last.then_inc(v_ready[s], 1)

            def scores(s, r, t):
                pe.wait_ge(qk_out[s], 3 * r + 3)
                at = slice(t * T, (t + 1) * T)
                pe.matmul(bank(s, t)[0:T, 0:HEADS * T], mask_left[:], mask_right[:],
                          start=True, stop=False, skip_group_check=True)
                for h in range(HEADS):
                    last = pe.matmul(bank(s, t)[0:T, h * T:(h + 1) * T], qz[s][:, h, at],
                                     kT[s][:, h // 2, at], start=False, stop=(h == HEADS - 1),
                                     skip_group_check=True)
                last.then_inc(s_ready[s], 1)

            def turn_weights(s, r):
                pe.wait_ge(v_out[s], r + 1)
                for t in range(NT):
                    keep_busy(s, 3, (13, 4)[t])
                    pe.wait_ge(p_ready[s], NT * r + (t + 1))
                    for h in range(HEADS):
                        last = pe.transpose(bank(s, 2 + t)[0:T, h * T:(h + 1) * T],
                                            P[s][:, t * HEADS + h, :], ident[:])
                    last.then_inc(pT_ready[s], 1)

            def weighted_values(s, r):
                for t in range(NT):
                    pe.wait_ge(pT_out[s], NT * r + (t + 1))
                    for h in range(HEADS):
                        to = bank(s, 0)[DH * (h % 2):DH * (h % 2) + DH,
                                        (h // 2) * C + t * T:(h // 2) * C + (t + 1) * T]
                        last = pe.matmul(to, v[s][:, t, h * DH:(h + 1) * DH],
                                         pT[s][:, t, h * T:(h + 1) * T], start=True, stop=True)
                last.then_inc(o_ready[s], 1)

            def project(s, r):
                pe.wait_ge(back_loaded, r + 1)
                pe.wait_ge(o_out[s], r + 1)
                for t in range(NT):
                    to = bank(s, 1)[0:T, t * D:(t + 1) * D]
                    for m in range(2):
                        last = pe.matmul(to, oT[s][:, m, t * T:(t + 1) * T], wo[:, m, :],
                                         start=(m == 0), stop=(m == 1))
                last.then_inc(wo_ready[s], 1)

            def mlp_up(s, r):
                pe.wait_ge(hT_ready[s], 2 * r + 2)
                pe.matmul(bank(s, 2)[:, 0:C], w1[:], hT[s][:], start=True, stop=True).then_inc(h1_ready[s], 1)

            def mlp_down(s, r):
                keep_busy(s, 0, 4)
                pe.wait_ge(gelu_ready[s], r + 1)
                for t in range(NT):
                    to = bank(s, 1)[0:T, (NT + t) * D:(NT + t + 1) * D]
                    last = pe.matmul(to, act1[s][:, t * T:(t + 1) * T], w2[:], start=True, stop=True)
                last.then_inc(w2_ready[s], 1)

            def half_round(a, ra, b, rb):
                more = ra is not None
                turn_weights(b, rb)
                if more:
                    transposed(a, 2 * ra + 1)
                weighted_values(b, rb)
                if more:
                    queries_keys(a, ra)
                project(b, rb)
                if more:
                    values(a, ra)
                    scores(a, ra, 0)
                keep_busy(b, 3, 3)
                transposed(b, 2 * rb + 2)
                if more:
                    scores(a, ra, 1)
                mlp_up(b, rb)
                mlp_down(b, rb)

            transposed(0, 1)
            queries_keys(0, 0)
            values(0, 0)
            scores(0, 0, 0)
            scores(0, 0, 1)
            with pe.Fori(0, ROUNDS - 1) as r:
                half_round(1, r, 0, r)
                half_round(0, r + 1, 1, r)
            half_round(1, ROUNDS - 1, 0, ROUNDS - 1)
            half_round(None, None, 1, ROUNDS - 1)

        @block.vector
        def _(dve):
            for s in subs:
                last = dve.memset(qz[s][:], 0.0)
            last.then_inc(zeroed, 1)
            dve.wait_ge(consts, N_CONSTS)
            dve.tensor_copy(mask_left[:], maskL[:, 0, :]).then_inc(masks_ready, 1)
            dve.tensor_copy(mask_right[:], maskR[:].rearrange("p h t -> p (h t)")).then_inc(masks_ready, 1)
            dve.wait_ge(tokens_in, 64)
            for s in subs:
                dve.sem_inc(back[s], 1)

            total, var, rstd = (lambda s: stat[s][:, 0, :]), (lambda s: stat[s][:, 1, :]), (lambda s: stat[s][:, 2, :])

            def statistics(s, c, ch):
                ch.step(dve.reduce_sum(total(s), X[:, tiles(c, s), :], AX.X))
                yield
                ch.settle()
                ch.step(dve.scalar_tensor_tensor(xc[s][:], spread(total(s), 2, D), -1.0 / D,
                                                 X[:, tiles(c, s), :], ALU.mult, ALU.add))
                yield
                ch.settle()
                ch.step(dve.tensor_tensor(xh[s][:], xc[s][:], xc[s][:], ALU.mult))
                yield
                ch.settle()
                ch.step(dve.reduce_sum(total(s), xh[s][:], AX.X))
                yield
                ch.settle()
                dve.tensor_scalar(var(s), total(s), 1.0 / D, EPS, ALU.mult, ALU.add).then_inc(var_ready[s], 1)
                yield

            def normalised(s, r, c, nth, ch):
                dve.wait_ge(rstd_ready[s], 2 * r + nth)
                dve.tensor_tensor(xh[s][:], xc[s][:], spread(rstd(s), 2, D), ALU.mult).then_inc(xh_ready[s], 1)
                dve.wait_ge((front_loaded, back_loaded)[nth - 1], r + 1)
                x = X[:, tiles(c, s), :]
                ch.step(dve.tensor_tensor(x, x, spread(bias[nth - 1][:], 1, NT), ALU.add))

            def add_product(s, c, ch, at):
                x = X[:, tiles(c, s), :]
                ch.step(dve.tensor_tensor(x, x, bank(s, 1)[0:T, at * NT * D:(at + 1) * NT * D]
                                          .rearrange("p (t d) -> p t d", t=NT), ALU.add))

            def softmax(s, r, ch):
                for t in range(NT):
                    heads = slice(t * HEADS, (t + 1) * HEADS)
                    dve.wait_ge(exped[s], NT * r + (t + 1))
                    ch.step(dve.reduce_sum(mx[s][:, 0, heads], P[s][:, heads, :], AX.X))
                    yield
                    ch.settle()
                    ch.step(dve.reciprocal(mx[s][:, 1, heads], mx[s][:, 0, heads]))
                    yield
                    ch.settle()
                    dve.tensor_tensor(P[s][:, heads, :], P[s][:, heads, :],
                                      spread(mx[s][:, 1, heads], 2, T), ALU.mult).then_inc(p_ready[s], 1)
                    yield

            def values(s, r):
                dve.wait_ge(v_ready[s], r + 1)
                dve.tensor_copy(v[s][:].rearrange("p t n -> p (t n)"), bank(s, 2)[0:T, :]).then_inc(v_out[s], 1)

            def shift(s, r, ch):
                for t in range(NT):
                    heads = slice(t * HEADS, (t + 1) * HEADS)
                    scores = bank(s, t)[0:T, 0:HEADS * T].rearrange("p (h k) -> p h k", h=HEADS)
                    dve.wait_ge(s_ready[s], NT * r + (t + 1))
                    ch.step(dve.reduce_max(mx[s][:, 0, heads], scores, AX.X))
                    ch.settle()
                    dve.tensor_tensor(P[s][:, heads, :], scores, spread(mx[s][:, 0, heads], 2, T),
                                      ALU.subtract).then_inc(shifted[s], 1)

            def half_round(a, ra, ca, b, rb, cb):
                more = ra is not None
                soft = Chain(dve, back[b], BACK, rb, before=1)
                if more:
                    norm = Chain(dve, front[a], FRONT, ra)
                    dve.wait_ge(back[a], BACK * ra + 1)
                    dve.sem_inc(dve_passed, 1)
                    one, other = statistics(a, ca, norm), softmax(b, rb, soft)
                    for turn in (one, one, other, one, other, one, other, one, other, other):
                        next(turn)
                    normalised(a, ra, ca, 1, norm)
                    next(other)
                else:
                    for _ in softmax(b, rb, soft):
                        pass
                dve.wait_ge(front[b], FRONT * rb + FRONT)
                dve.wait_ge(wo_ready[b], rb + 1)
                add_product(b, cb, soft, 0)
                soft.settle()
                dve.sem_inc(dve_passed, 1)
                for _ in statistics(b, cb, soft):
                    pass
                if more:
                    values(a, ra)
                normalised(b, rb, cb, 2, soft)
                if more:
                    shift(a, ra, norm)
                    norm.close()
                soft.settle()
                dve.wait_ge(w2_ready[b], rb + 1)
                add_product(b, cb, soft, 1)
                soft.close()

            def body(r, c, after):
                half_round(1, r, c, 0, r, c)
                half_round(0, r + 1, after, 1, r, c)

            norm = Chain(dve, front[0], FRONT, 0)
            for _ in statistics(0, 0, norm):
                pass
            normalised(0, 0, 0, 1, norm)
            values(0, 0)
            shift(0, 0, norm)
            norm.close()
            with dve.Fori(0, LAYERS - 1) as l:
                with dve.Fori(0, CHUNKS - 1) as c:
                    body(l * CHUNKS + c, c, c + 1)
                body(l * CHUNKS + (CHUNKS - 1), CHUNKS - 1, 0)
            with dve.Fori(0, CHUNKS - 1) as c:
                body(c + (ROUNDS - CHUNKS), c, c + 1)
            half_round(1, ROUNDS - 1, CHUNKS - 1, 0, ROUNDS - 1, CHUNKS - 1)
            half_round(None, None, None, 1, ROUNDS - 1, CHUNKS - 1)
            for s in subs:
                dve.wait_ge(back[s], BACK * ROUNDS + 1)
            total, var, rstd = fstat[:, 0, :], fstat[:, 1, :], fstat[:, 2, :]
            ch = Chain(dve, final, 6, 0)
            ch.step(dve.reduce_sum(total, X[:], AX.X))
            ch.settle()
            ch.step(dve.scalar_tensor_tensor(yf[:], spread(total, 2, D), -1.0 / D, X[:], ALU.mult, ALU.add))
            ch.settle()
            ch.step(dve.tensor_tensor(xf[:], yf[:], yf[:], ALU.mult))
            ch.settle()
            ch.step(dve.reduce_sum(total, xf[:], AX.X))
            ch.settle()
            dve.tensor_scalar(var, total, 1.0 / D, EPS, ALU.mult, ALU.add).then_inc(fvar, 1)
            dve.wait_ge(frstd, 1)
            ch.step(dve.tensor_tensor(xf[:], yf[:], spread(rstd, 2, D), ALU.mult))
            ch.settle()
            ch.step(dve.tensor_tensor(yf[:], xf[:], spread(rows[:, 0, :], 1, TILES), ALU.mult))
            ch.settle()
            ch.close()
            dve.tensor_tensor(xf[:], yf[:], spread(rows[:, 1, :], 1, TILES), ALU.add).then_inc(out_ready, 1)


def fuse_and_expert(nc, fused, gat_w, W1, b1, W2, b2, hidden, gat_h, expert_out):
    IPT = 2
    T = IPT * NF
    NT = 2
    C = NT * T
    TILES = B // IPT
    SUBS = 2
    ROUNDS = TILES // (NT * SUBS)
    EH = 2 * D
    FRONT = 9
    BACK = 5
    subs = range(SUBS)
    with ExitStack() as ctx:
        sb, ps, sem = tools(nc, ctx)
        H = sb("H", [T, TILES, D])
        wg = sb("wg", [D, GF])
        w1 = sb("w1f", [D, EXPERTS, EH])
        w2 = sb("w2f", [EH, EXPERTS, D])
        b1c = sb("b1f", [EH, EXPERTS])
        bias = sb("bias_f", [T, EXPERTS * D])
        mask_left = sb("mask_left_f", [128, T], BF16)
        mask_right = sb("mask_right_f", [128, C], BF16)
        ident = sb("ident_f", [T, T])
        maskL = sb("maskL_f", [128, 1, T])
        maskR = sb("maskR_f", [128, NT, T])
        half = sb("half_f", [T, NT])
        xr = [sb(f"xr_f{s}", [T, NT, D]) for s in subs]
        xc = [sb(f"xc_f{s}", [T, NT, D]) for s in subs]
        sq = [sb(f"sq_f{s}", [T, NT, D]) for s in subs]
        xh = [sb(f"xh_f{s}", [T, NT, D]) for s in subs]
        stat = [sb(f"stat_f{s}", [T, 3, NT]) for s in subs]
        hT = [sb(f"hT_f{s}", [D, C]) for s in subs]
        P = [sb(f"P_f{s}", [T, NT, T]) for s in subs]
        mx = [sb(f"mx_f{s}", [T, 2, NT]) for s in subs]
        pT = [sb(f"pT_f{s}", [T, C]) for s in subs]
        act1 = [sb(f"act1_f{s}", [EH, EXPERTS, C]) for s in subs]
        gh = [sb(f"gh_f{s}", [T, NT, GF]) for s in subs]
        eo = [sb(f"eo_f{s}", [T, NT, EXPERTS * D]) for s in subs]
        psum = ps("psum_f", [128, 8, 512])

        loaded = sem("f_loaded")
        consts = sem("f_consts")
        masks_ready = sem("f_masks_ready")
        front = [sem(f"f_front{s}") for s in subs]
        back = [sem(f"f_back{s}") for s in subs]
        var_ready = [sem(f"f_var{s}") for s in subs]
        rstd_ready = [sem(f"f_rstd{s}") for s in subs]
        xh_ready = [sem(f"f_xh{s}") for s in subs]
        t_ready = [sem(f"f_t{s}") for s in subs]
        hT_ready = [sem(f"f_hT{s}") for s in subs]
        s_ready = [sem(f"f_s{s}") for s in subs]
        shifted = [sem(f"f_shifted{s}") for s in subs]
        exped = [sem(f"f_exped{s}") for s in subs]
        p_ready = [sem(f"f_p{s}") for s in subs]
        pT_ready = [sem(f"f_pT{s}") for s in subs]
        pT_out = [sem(f"f_pT_out{s}") for s in subs]
        o_ready = [sem(f"f_o{s}") for s in subs]
        gat_ready = [sem(f"f_gat{s}") for s in subs]
        h1_ready = [sem(f"f_h1{s}") for s in subs]
        gelu_ready = [sem(f"f_gelu{s}") for s in subs]
        eo_ready = [sem(f"f_eo{s}") for s in subs]
        gh_out = [sem(f"f_gh_out{s}") for s in subs]
        eo_out = [sem(f"f_eo_out{s}") for s in subs]
        gh_stored = [sem(f"f_gh_stored{s}") for s in subs]
        eo_stored = [sem(f"f_eo_stored{s}") for s in subs]
        h_done = sem("f_h_done")
        h_stored = sem("f_h_stored")
        pe_passed = sem("f_pe_passed")
        dve_passed = sem("f_dve_passed")
        block = ctx.enter_context(nc.Block())

        def bank(s, n):
            return psum[:, 4 * s + n, :]

        def tiles(r, s):
            return bass.ds((r * SUBS + s) * NT, NT)

        N_LOADS = 16 * (1 + 4 + EXPERTS)

        @block.sync
        def _(sync):
            sync.dma_start(H[:], fused.rearrange("(n p) d -> p n d", p=T)).then_inc(loaded, 16)
            sync.dma_start(wg[:], gat_w).then_inc(loaded, 16)
            sync.dma_start(w1[:], W1.rearrange("e k n -> k e n")).then_inc(loaded, 16)
            sync.dma_start(w2[:], W2.rearrange("e k n -> k e n")).then_inc(loaded, 16)
            for e in range(EXPERTS):
                sync.dma_start(b1c[:, e:e + 1], b1[e:e + 1, :].rearrange("e k -> k e")).then_inc(loaded, 16)
            sync.dma_start(bias[:], b2.rearrange("e d -> (e d)").partition_broadcast(T)).then_inc(loaded, 16)
            gat_view = gat_h.rearrange("(n p) d -> p n d", p=T)
            eo_view = expert_out.rearrange("(n p) d -> p n d", p=T)
            with sync.Fori(0, ROUNDS) as r:
                for s in subs:
                    sync.wait_ge(gh_out[s], r + 1)
                    sync.dma_start(gat_view[:, tiles(r, s), :], gh[s][:]).then_inc(gh_stored[s], 16)
                    sync.wait_ge(eo_out[s], r + 1)
                    sync.dma_start(eo_view[:, tiles(r, s), :], eo[s][:]).then_inc(eo_stored[s], 16)
            sync.wait_ge(h_done, 1)
            sync.dma_start(hidden.rearrange("(n p) d -> p n d", p=T), H[:]).then_inc(h_stored, 16)
            sync.wait_ge(h_stored, 16)
            for s in subs:
                sync.wait_ge(gh_stored[s], 16 * (ROUNDS + 1))
                sync.wait_ge(eo_stored[s], 16 * (ROUNDS + 1))

        @block.gpsimd
        def _(pool):
            n = block_masks(pool, consts, IPT, NF, maskL[:], maskR[:])
            n = identity(pool, consts, n, ident[:])
            pool.memset(half[:], -0.5).then_inc(consts, 1)
            pool.wait_ge(consts, n + 1)

            def rstd(s, n):
                pool.wait_ge(var_ready[s], n)
                pool.tensor_tensor(stat[s][:, 2, :], stat[s][:, 1, :], half[:], ALU.pow).then_inc(rstd_ready[s], 1)

            rstd(0, 1)
            rstd(0, 2)
            rstd(1, 1)
            with pool.Fori(0, ROUNDS - 1) as r:
                rstd(1, 2 * r + 2)
                rstd(0, 2 * r + 3)
                rstd(0, 2 * r + 4)
                rstd(1, 2 * r + 3)
            rstd(1, 2 * ROUNDS)

        N_CONSTS = 10 + 2 + 1

        @block.scalar
        def _(act):
            act.wait_ge(loaded, N_LOADS)

            def turned(s, n):
                act.wait_ge(t_ready[s], n)
                act.activation(hT[s][:], bank(s, 3)[0:D, 0:C], ACT.Copy).then_inc(hT_ready[s], 1)

            def exps(s, r):
                act.wait_ge(shifted[s], r + 1)
                act.activation(P[s][:], P[s][:], ACT.Exp).then_inc(exped[s], 1)

            def gelus(s, r):
                act.wait_ge(h1_ready[s], r + 1)
                for e in range(EXPERTS):
                    last = act.activation(act1[s][:, e, :], bank(s, e // 2)[:, (e % 2) * C:(e % 2 + 1) * C],
                                          ACT.Gelu, bias=b1c[:, e:e + 1])
                last.then_inc(gelu_ready[s], 1)

            def half_round(a, ra, b, rb):
                turned(b, 2 * rb + 2)
                turned(a, 2 * ra + 1)
                exps(a, ra)
                gelus(b, rb)

            turned(0, 1)
            exps(0, 0)
            half_round(1, 0, 0, 0)
            with act.Fori(0, ROUNDS - 1) as r:
                half_round(0, r + 1, 1, r)
                half_round(1, r + 1, 0, r + 1)
            turned(1, 2 * ROUNDS)
            gelus(1, ROUNDS - 1)

        @block.tensor
        def _(pe):
            pe.wait_ge(consts, N_CONSTS)
            pe.wait_ge(masks_ready, 2)
            pe.wait_ge(loaded, N_LOADS)

            def keep_busy(s, n, count):
                for _ in range(count):
                    pe.matmul(bank(s, n)[0:T, 0:2 * C], mask_left[:], spread(mask_right[:], 1, 2),
                              start=True, stop=True, skip_group_check=True)

            def transposed(s, n):
                wait_apart(pe, xh_ready[s], n, pe_passed)
                for t in range(NT):
                    last = pe.transpose(bank(s, 3)[0:D, t * T:(t + 1) * T], xh[s][:, t, :], ident[:])
                last.then_inc(t_ready[s], 1)

            def scores(s, r):
                pe.wait_ge(hT_ready[s], 2 * r + 1)
                pe.matmul(bank(s, 0)[0:T, 0:C], mask_left[:], mask_right[:],
                          start=True, stop=False, skip_group_check=True)
                for t in range(NT):
                    at = slice(t * T, (t + 1) * T)
                    last = pe.matmul(bank(s, 0)[0:T, at], hT[s][:, at], hT[s][:, at],
                                     start=False, stop=(t == NT - 1), skip_group_check=True)
                last.then_inc(s_ready[s], 1)

            def attend(s, r):
                pe.wait_ge(p_ready[s], r + 1)
                for t in range(NT):
                    last = pe.transpose(bank(s, 1)[0:T, t * T:(t + 1) * T], P[s][:, t, :], ident[:])
                last.then_inc(pT_ready[s], 1)
                pe.wait_ge(pT_out[s], r + 1)
                for t in range(NT):
                    last = pe.matmul(bank(s, 2)[0:T, t * D:(t + 1) * D], pT[s][:, t * T:(t + 1) * T],
                                     xh[s][:, t, :], start=True, stop=True)
                last.then_inc(o_ready[s], 1)

            def project(s, r):
                pe.wait_ge(hT_ready[s], 2 * r + 2)
                for e in range(EXPERTS):
                    last = pe.matmul(bank(s, e // 2)[:, (e % 2) * C:(e % 2 + 1) * C], w1[:, e, :], hT[s][:],
                                     start=True, stop=True)
                last.then_inc(h1_ready[s], 1)
                for t in range(NT):
                    last = pe.matmul(bank(s, 3)[0:T, C + t * GF:C + (t + 1) * GF],
                                     hT[s][:, t * T:(t + 1) * T], wg[:], start=True, stop=True)
                last.then_inc(gat_ready[s], 1)

            def experts(s, r):
                pe.wait_ge(gelu_ready[s], r + 1)
                for t in range(NT):
                    to = bank(s, 2)[0:T, t * EXPERTS * D:(t + 1) * EXPERTS * D]
                    for e in range(EXPERTS):
                        last = pe.matmul(to[:, e * D:(e + 1) * D], act1[s][:, e, t * T:(t + 1) * T],
                                         w2[:, e, :], start=True, stop=True)
                last.then_inc(eo_ready[s], 1)

            def half_round(a, ra, b, rb):
                keep_busy(b, 1, 16)
                transposed(b, 2 * rb + 2)
                transposed(a, 2 * ra + 1)
                scores(a, ra)
                project(b, rb)
                keep_busy(a, 1, 8)
                attend(a, ra)
                experts(b, rb)

            transposed(0, 1)
            scores(0, 0)
            attend(0, 0)
            half_round(1, 0, 0, 0)
            with pe.Fori(0, ROUNDS - 1) as r:
                half_round(0, r + 1, 1, r)
                half_round(1, r + 1, 0, r + 1)
            transposed(1, 2 * ROUNDS)
            project(1, ROUNDS - 1)
            experts(1, ROUNDS - 1)

        @block.vector
        def _(dve):
            dve.wait_ge(consts, N_CONSTS)
            dve.tensor_copy(mask_left[:], maskL[:, 0, :]).then_inc(masks_ready, 1)
            dve.tensor_copy(mask_right[:], maskR[:].rearrange("p n t -> p (n t)")).then_inc(masks_ready, 1)
            dve.wait_ge(loaded, N_LOADS)
            for s in subs:
                dve.sem_inc(gh_stored[s], 16)
                dve.sem_inc(eo_stored[s], 16)
            for s in subs:
                dve.sem_inc(back[s], 1)

            total, var, rstd = (lambda s: stat[s][:, 0, :]), (lambda s: stat[s][:, 1, :]), (lambda s: stat[s][:, 2, :])

            def statistics(s, ch):
                ch.step(dve.reduce_sum(total(s), xr[s][:], AX.X))
                yield
                ch.settle()
                ch.step(dve.scalar_tensor_tensor(xc[s][:], spread(total(s), 2, D), -1.0 / D,
                                                 xr[s][:], ALU.mult, ALU.add))
                yield
                ch.settle()
                ch.step(dve.tensor_tensor(sq[s][:], xc[s][:], xc[s][:], ALU.mult))
                yield
                ch.settle()
                ch.step(dve.reduce_sum(total(s), sq[s][:], AX.X))
                yield
                ch.settle()
                dve.tensor_scalar(var(s), total(s), 1.0 / D, EPS, ALU.mult, ALU.add).then_inc(var_ready[s], 1)
                yield

            def normalised(s, n):
                dve.wait_ge(rstd_ready[s], n)
                dve.tensor_tensor(xh[s][:], xc[s][:], spread(rstd(s), 2, D), ALU.mult).then_inc(xh_ready[s], 1)

            def fetch(s, r):
                ch = Chain(dve, front[s], FRONT, r)
                dve.wait_ge(back[s], BACK * r + 1)
                dve.sem_inc(dve_passed, 1)
                ch.step(dve.tensor_copy(xr[s][:], H[:, tiles(r, s), :]))
                return ch

            def keep(s, r, ch):
                ch.step(dve.tensor_copy(H[:, tiles(r, s), :], xr[s][:]))
                ch.close()

            def shift(s, r, ch):
                score = bank(s, 0)[0:T, 0:C].rearrange("p (n t) -> p n t", n=NT)
                dve.wait_ge(s_ready[s], r + 1)
                ch.step(dve.reduce_max(mx[s][:, 0, :], score, AX.X))
                ch.settle()
                dve.tensor_tensor(P[s][:], score, spread(mx[s][:, 0, :], 2, T), ALU.subtract)\
                    .then_inc(shifted[s], 1)

            def attend(s, r, ch):
                dve.wait_ge(exped[s], r + 1)
                ch.step(dve.reduce_sum(mx[s][:, 0, :], P[s][:], AX.X))
                ch.settle()
                ch.step(dve.reciprocal(mx[s][:, 1, :], mx[s][:, 0, :]))
                ch.settle()
                dve.tensor_tensor(P[s][:], P[s][:], spread(mx[s][:, 1, :], 2, T), ALU.mult).then_inc(p_ready[s], 1)
                dve.wait_ge(pT_ready[s], r + 1)
                dve.tensor_copy(pT[s][:], bank(s, 1)[0:T, 0:C]).then_inc(pT_out[s], 1)
                dve.wait_ge(o_ready[s], r + 1)
                ch.step(dve.tensor_tensor(xr[s][:], xr[s][:],
                                          bank(s, 2)[0:T, 0:NT * D].rearrange("p (n d) -> p n d", n=NT), ALU.add))
                ch.close()

            def gat_rows(s, r):
                dve.wait_ge(gat_ready[s], r + 1)
                dve.wait_ge(gh_stored[s], 16 * (r + 1))
                dve.tensor_copy(gh[s][:], bank(s, 3)[0:T, C:C + NT * GF].rearrange("p (n d) -> p n d", n=NT))\
                    .then_inc(gh_out[s], 1)

            def expert_rows(s, rounds):
                dve.wait_ge(eo_ready[s], rounds)
                dve.wait_ge(eo_stored[s], 16 * rounds)
                dve.tensor_tensor(eo[s][:], bank(s, 2)[0:T, :].rearrange("p (n d) -> p n d", n=NT),
                                  spread(bias[:], 1, NT), ALU.add).then_inc(eo_out[s], 1)

            def half_round(a, ra, b, rb, first=False):
                pre, post = fetch(a, ra), Chain(dve, back[b], BACK, rb, before=1)
                dve.wait_ge(front[b], FRONT * rb + FRONT)
                dve.sem_inc(dve_passed, 1)
                one = statistics(b, post)
                next(one)
                pre.settle()
                dve.sem_inc(dve_passed, 1)
                other = statistics(a, pre)
                next(other)
                for _ in one:
                    next(other)
                keep(b, rb, post)
                normalised(b, 2 * rb + 2)
                normalised(a, 2 * ra + 1)
                if not first:
                    expert_rows(a, ra)
                shift(a, ra, pre)
                gat_rows(b, rb)
                attend(a, ra, pre)

            pre = fetch(0, 0)
            pre.settle()
            for _ in statistics(0, pre):
                pass
            normalised(0, 1)
            shift(0, 0, pre)
            attend(0, 0, pre)
            half_round(1, 0, 0, 0, first=True)
            with dve.Fori(0, ROUNDS - 1) as r:
                half_round(0, r + 1, 1, r)
                half_round(1, r + 1, 0, r + 1)
            post = Chain(dve, back[1], BACK, ROUNDS - 1, before=1)
            dve.wait_ge(front[1], FRONT * ROUNDS)
            for _ in statistics(1, post):
                pass
            keep(1, ROUNDS - 1, post)
            normalised(1, 2 * ROUNDS)
            gat_rows(1, ROUNDS - 1)
            for s in subs:
                expert_rows(s, ROUNDS)
                dve.wait_ge(back[s], BACK * ROUNDS + 1)
            dve.sem_inc(h_done, 1)


def route_edges(nc, keys_sorted, count_i, last_counts, gat_h, att_src, att_dst, src_table, agg):
    TF = GF + GH
    BT = 4
    SUBS = 2
    ROUNDS = COLS // (BT * SUBS)
    STRIDE = 7
    WIN = 3 * STRIDE
    STARTS = NF // STRIDE - 2
    HALF = (NF + 1) // 2
    NO_TOKEN = 64.0
    SLOPE = 0.2
    PARTS = 3
    DECODE = 14
    PREP = 24
    subs = range(SUBS)
    with ExitStack() as ctx:
        sb, ps, sem = tools(nc, ctx)
        h_nodes = sb("h_nodes", [128, NF, GF])
        att = sb("att", [128, 2, GF])
        prod = sb("prod", [128, NF, GF])
        src_rows = sb("src_rows", [128, NF, TF])
        a_dst = sb("a_dst", [128, NF, GH])
        bound = sb("bound", [128, NF, GH])
        rest = sb("rest", [128, NF, GH])
        dst_parts = sb("dst_parts", [128, PARTS, NF * GH], BF16)
        top = sb("top", [128, 2, GH])
        last_row = sb("last_row", [128, TF])
        z = sb("z_r", [128, 2, NF, GH])
        dense = sb("dense", [128, NF, TF])
        zeros = sb("zeros_r", [128, 512])
        source = sb("source", [128, COLS], I32)
        tok_i = sb("tok_i_r", [128, COLS], I32)
        img_i = sb("img_i_r", [128, COLS], I32)
        empty = sb("empty", [128, COLS])
        img = sb("img_r", [128, COLS + BT * SUBS], BF16)
        tok = sb("tok_r", [128, COLS + BT * SUBS])
        ends = sb("ends", [128, 2, 2, ROUNDS])
        start_i = sb("start_i", [128, ROUNDS + 1], I32)
        start_f = sb("start_f", [128, ROUNDS])
        wide_f = sb("wide_f", [128, 1])
        wide_i = sb("wide_i", [128, 1], I32)
        iota_f = sb("iota_r", [128, 128])
        iota_b = sb("iota_rb", [128, 128, BT], BF16)
        ident_f = sb("ident_rf", [128, 128])
        ident = sb("ident_r", [128, 128], BF16)
        node4 = [sb(f"node4_{s}", [128, BT], I32) for s in subs]
        gathered = [sb(f"gathered{s}", [128, BT, TF]) for s in subs]
        from_src = [sb(f"from_src{s}", [128, BT, TF]) for s in subs]
        logit = [sb(f"logit{s}", [128, 3, BT, GH]) for s in subs]
        from_dst = [sb(f"from_dst{s}", [128, BT, GH]) for s in subs]
        val = [sb(f"val{s}", [128, BT, TF]) for s in subs]
        hot_b = [sb(f"hot_b{s}", [128, 128, BT], BF16) for s in subs]
        hot_T = [sb(f"hot_T{s}", [128, BT * 128], BF16) for s in subs]
        hot_f = [sb(f"hot_f{s}", [128, BT, 128]) for s in subs]
        hot_tok = [sb(f"hot_tok_r{s}", [128, BT * NF]) for s in subs]
        picked = [sb(f"picked{s}", [128, BT * NF * GH]) for s in subs]
        spread_val = [sb(f"spread_val{s}", [128, BT * NF * TF]) for s in subs]
        psum = ps("psum_r", [128, 8 * 512])

        nodes_in = sem("r_nodes_in")
        prep = sem("r_prep")
        top_ready = sem("r_top_ready")
        top_all = sem("r_top_all")
        rows_ready = sem("r_rows_ready")
        rows_stored = sem("r_rows_stored")
        last_in = sem("r_last_in")
        dense_logit = sem("r_dense_logit")
        dense_exp = sem("r_dense_exp")
        dense_ready = sem("r_dense_ready")
        iota_ready = sem("r_iota")
        ident_set = sem("r_ident")
        decode = sem("r_decode")
        decoded = sem("r_decoded")
        ends_ready = sem("r_ends_ready")
        ends_all = sem("r_ends_all")
        opened = sem("r_opened")
        copied = [sem(f"r_copied{s}") for s in subs]
        src_in = [sem(f"r_src_in{s}") for s in subs]
        src_taken = [sem(f"r_src_taken{s}") for s in subs]
        chain = [sem(f"r_chain{s}") for s in subs]
        hot_ready = [sem(f"r_hot_ready{s}") for s in subs]
        turned = [sem(f"r_turned{s}") for s in subs]
        turned_out = [sem(f"r_turned_out{s}") for s in subs]
        cast = [sem(f"r_cast{s}") for s in subs]
        dst_ready = [sem(f"r_dst_ready{s}") for s in subs]
        logit_ready = [sem(f"r_logit{s}") for s in subs]
        exp_ready = [sem(f"r_exp{s}") for s in subs]
        batch_ready = [sem(f"r_batch{s}") for s in subs]
        batch_used = [sem(f"r_batch_used{s}") for s in subs]
        sums_ready = sem("r_sums_ready")
        sums_read = sem("r_sums_read")
        passed = sem("r_passed")
        pe_passed = sem("r_pe_passed")
        block = ctx.enter_context(nc.Block())

        def columns(r, s):
            return bass.ds(r * (BT * SUBS) + s * BT, BT)

        def dst_psum(s, wide, k):
            if wide:
                at = (3 + 2 * s + k // 2) * 512 + (k % 2) * NF * GH
                return psum[:, at:at + NF * GH]
            return psum[:, (6 + s) * 512 + k * WIN * GH:(6 + s) * 512 + (k + 1) * WIN * GH]

        def turned_psum(s, wide):
            bank = (2 if wide else 5) * 512
            return psum[:, bank:bank + 512].bitcast(BF16)[:, s * BT * 128:(s + 1) * BT * 128]

        def start_of(eng, r):
            return eng.value_load(start_i[0:1, bass.ds(r, 1)], min_val=0, max_val=STARTS - 1)

        def both_paths(eng, path):
            wide = eng.value_load(wide_i[0:1, 0:1], min_val=0, max_val=1)
            with eng.If(wide < 1):
                path(False)
            with eng.If(wide > 0):
                path(True)

        @block.sync
        def _(sync):
            by_node = lambda t: t.rearrange("(b t) f -> b t f", t=NF)
            sync.dma_start(h_nodes[:], by_node(gat_h)).then_inc(nodes_in, 16)
            for n, a in enumerate((att_src, att_dst)):
                sync.dma_start(att[:, n, :], a.rearrange("h e -> (h e)").partition_broadcast(128))\
                    .then_inc(nodes_in, 16)
            sync.wait_ge(rows_ready, 1)
            sync.dma_start(by_node(src_table), src_rows[:]).then_inc(rows_stored, 16)
            sync.wait_ge(rows_stored, 16)
            sync.dma_start(last_row[:], src_table[NODES - 1].partition_broadcast(128)).then_inc(last_in, 16)

        @block.gpsimd
        def _(pool):
            pool.iota(iota_f[:], pattern=[[1, 128]], base=0, channel_multiplier=0,
                      allow_small_or_imprecise_dtypes=True).then_inc(iota_ready, 1)
            identity(pool, ident_set, 0, ident_f[:])
            pool.wait_ge(top_ready, 1)
            pool.partition_all_reduce(top[:, 1, :], top[:, 0, :], 128, bass.bass_isa.ReduceOp.max)\
                .then_inc(top_all, 1)
            pool.wait_ge(ends_ready, 2)
            pool.partition_all_reduce(ends[:, 1, :, :].rearrange("p n r -> p (n r)"),
                                      ends[:, 0, :, :].rearrange("p n r -> p (n r)"), 128,
                                      bass.bass_isa.ReduceOp.max).then_inc(ends_all, 1)
            pool.wait_ge(rows_stored, 16)
            count = pool.value_load(count_i[0:1, 0:1], min_val=0, max_val=COLS)
            for s in subs:
                pool.sem_inc(src_taken[s], 1)

            def gather(r):
                for s in subs:
                    pool.wait_ge(src_taken[s], r + 1)
                    pool.sem_inc(passed, 1)
                    pool.tensor_copy(node4[s][:], source[:, columns(r, s)]).then_inc(copied[s], 1)
                    pool.wait_ge(copied[s], r + 1)
                    pool.sem_inc(passed, 1)
                    for k in range(BT):
                        pool.indirect_dma_start(
                            gathered[s][:, k, :], None, src_table,
                            bass.IndirectOffsetOnAxis(ap=node4[s][:, k:k + 1].bitcast(U32), axis=0))\
                            .then_inc(src_in[s], 16)
            edge_rounds(pool, count, gather)

        @block.scalar
        def _(act):
            act.wait_ge(dense_logit, 1)
            act.activation(z[:], z[:], ACT.Exp).then_inc(dense_exp, 1)
            act.wait_ge(decoded, 1)
            count = act.value_load(count_i[0:1, 0:1], min_val=0, max_val=COLS)
            for s in subs:
                act.sem_inc(batch_used[s], 1)

            def path(wide):
                def out_of_psum(s, r):
                    act.wait_ge(turned[s], r + 1)
                    act.activation(hot_T[s][:], turned_psum(s, wide), ACT.Copy).then_inc(turned_out[s], 1)

                def batches(r):
                    def widen(s):
                        act.wait_ge(batch_used[s], r + 1)
                        act.activation(hot_f[s][:], hot_b[s][:].rearrange("p i k -> p k i"), ACT.Copy)\
                            .then_inc(cast[s], 1)

                    widen(0)
                    for s in subs:
                        act.wait_ge(logit_ready[s], r + 1)
                        act.activation(val[s][:, :, GF:TF], logit[s][:, 2, :, :], ACT.Exp).then_inc(exp_ready[s], 1)
                    widen(1)
                    for s in subs:
                        out_of_psum(s, r + 1)

                for s in subs:
                    out_of_psum(s, 0)
                edge_rounds(act, count, batches)
            both_paths(act, path)

        @block.tensor
        def _(pe):
            pe.wait_ge(decoded, 1)
            count = pe.value_load(count_i[0:1, 0:1], min_val=0, max_val=COLS)

            def path(wide):
                sums = [(0, HALF * TF), (1, (NF - HALF) * TF)] if wide else [(n, WIN * TF) for n in range(STARTS)]
                width = NF if wide else WIN
                for n, size in sums:
                    pe.matmul(psum[:, n * 512:n * 512 + size], zeros[:, 0:128], zeros[:, 0:size],
                              start=True, stop=False, skip_group_check=True)

                def targets(s, r):
                    pe.wait_ge(hot_ready[s], r + 1)
                    for k in range(BT):
                        last = pe.transpose(turned_psum(s, wide)[:, k * 128:(k + 1) * 128], hot_b[s][:, :, k], ident[:])
                    last.then_inc(turned[s], 1)

                def target_rows(s, r, start):
                    pe.wait_ge(turned_out[s], r + 1)
                    for k in range(BT):
                        for n in range(PARTS):
                            rows = dst_parts[:, n, :] if wide else dst_parts[:, n, bass.ds(start * (STRIDE * GH), WIN * GH)]
                            last = pe.matmul(dst_psum(s, wide, k), hot_T[s][:, k * 128:(k + 1) * 128], rows,
                                             start=(n == 0), stop=(n == PARTS - 1), skip_group_check=True)
                    last.then_inc(dst_ready[s], 1)

                def batches(r):
                    after = None if wide else start_of(pe, r + 1)
                    start = None if wide else start_of(pe, r)
                    for s in subs:
                        targets(s, r + 1)
                        target_rows(s, r + 1, after)
                        wait_apart(pe, cast[s], r + 1, pe_passed)
                        wait_apart(pe, batch_ready[s], r + 2, pe_passed)
                        for k in range(BT):
                            base = k * width * TF
                            if wide:
                                for n, size in sums:
                                    at = base + n * HALF * TF
                                    last = pe.matmul(psum[:, n * 512:n * 512 + size], hot_f[s][:, k, :],
                                                     spread_val[s][:, at:at + size],
                                                     start=False, stop=False, skip_group_check=True)
                            else:
                                last = pe.matmul(psum[:, bass.ds(start * 512, WIN * TF)], hot_f[s][:, k, :],
                                                 spread_val[s][:, base:base + WIN * TF],
                                                 start=False, stop=False, skip_group_check=True)
                        last.then_inc(batch_used[s], 1)

                first = None if wide else start_of(pe, 0)
                for s in subs:
                    targets(s, 0)
                    target_rows(s, 0, first)
                edge_rounds(pe, count, batches)
                for n, size in sums:
                    last = pe.matmul(psum[:, n * 512:n * 512 + size], zeros[:, 0:128], zeros[:, 0:size],
                                     start=False, stop=True, skip_group_check=True)
                last.then_inc(sums_ready, 1)
            both_paths(pe, path)

        @block.vector
        def _(dve):
            ch = Chain(dve, decode, DECODE, 0)
            keys_i = keys_sorted[:].bitcast(I32)
            ch.step(dve.memset(zeros[:], 0.0))
            ch.step(dve.tensor_scalar(source[:], keys_i, (1 << SRC_BITS) - 1, None, ALU.bitwise_and))
            ch.step(dve.tensor_scalar(img_i[:], keys_i, SRC_BITS, (1 << IMG_BITS) - 1,
                                      ALU.logical_shift_right, ALU.bitwise_and))
            ch.step(dve.tensor_scalar(tok_i[:], keys_i, SRC_BITS + IMG_BITS, 63,
                                      ALU.logical_shift_right, ALU.bitwise_and))
            ch.step(dve.tensor_scalar(empty[:], keys_sorted[:], 0.0, NO_TOKEN, ALU.is_equal, ALU.mult))
            ch.step(dve.memset(img[:, COLS:], 0.0))
            ch.step(dve.memset(tok[:, COLS:], NO_TOKEN))
            ch.step(dve.memset(start_i[:, ROUNDS:], 0))
            dve.wait_ge(iota_ready, 1)
            ch.step(dve.tensor_copy(iota_b[:], spread(iota_f[:], 2, BT)))
            dve.wait_ge(ident_set, 2)
            ch.step(dve.tensor_copy(ident[:], ident_f[:]))
            ch.settle()
            ch.step(dve.tensor_copy(img[:, 0:COLS], img_i[:]))
            ch.step(dve.tensor_tensor(tok[:, 0:COLS], tok_i[:], empty[:], ALU.add))
            ch.step(dve.tensor_tensor(empty[:], tok_i[:], empty[:], ALU.subtract))
            ch.settle()
            per_round = "p (r k) -> p r k"
            dve.reduce_max(ends[:, 0, 0, :], empty[:].rearrange(per_round, r=ROUNDS), AX.X).then_inc(ends_ready, 1)
            dve.wait_ge(ends_ready, 1)
            ch.step(dve.tensor_scalar(empty[:], tok[:, 0:COLS], -1.0, None, ALU.mult))
            ch.settle()
            dve.reduce_max(ends[:, 0, 1, :], empty[:].rearrange(per_round, r=ROUNDS), AX.X).then_inc(ends_ready, 1)
            ch.close()

            ch = Chain(dve, prep, PREP, 0)
            split = lambda t: t.rearrange("p t (h e) -> p t h e", e=EXPERTS)
            a_src = src_rows[:, :, GF:TF]
            dve.wait_ge(nodes_in, 48)
            ch.step(dve.tensor_tensor(prod[:], h_nodes[:], spread(att[:, 0, :], 1, NF), ALU.mult))
            dve.tensor_copy(src_rows[:, :, 0:GF], h_nodes[:])
            ch.settle()
            dve.reduce_sum(a_src, split(prod[:]), AX.X).then_inc(rows_ready, 1)
            dve.wait_ge(rows_ready, 1)
            dve.reduce_max(top[:, 0, :], a_src.rearrange("p t h -> p h t"), AX.X).then_inc(top_ready, 1)
            ch.step(dve.tensor_tensor(prod[:], h_nodes[:], spread(att[:, 1, :], 1, NF), ALU.mult))
            ch.settle()
            ch.step(dve.reduce_sum(a_dst[:], split(prod[:]), AX.X))
            ch.settle()
            left = a_dst
            for n in range(PARTS):
                part = dst_parts[:, n, :].rearrange("p (t h) -> p t h", h=GH)
                ch.step(dve.tensor_copy(part, left[:]))
                ch.settle()
                if n < PARTS - 1:
                    ch.step(dve.tensor_tensor(rest[:], left[:], part, ALU.subtract))
                    ch.settle()
                    left = rest

            dve.wait_ge(ends_all, 1)
            below = ends[:, 1, 1, :]
            ch.step(dve.tensor_scalar(start_f[:], below, -float(STRIDE), None, ALU.is_le))
            for n in range(2, STARTS):
                ch.settle()
                ch.step(dve.scalar_tensor_tensor(start_f[:], below, -float(n * STRIDE), start_f[:],
                                                 ALU.is_le, ALU.add))
            ch.settle()
            ch.step(dve.tensor_copy(start_i[:, 0:ROUNDS], start_f[:]))
            ch.settle()
            ch.step(dve.scalar_tensor_tensor(start_f[:], start_f[:], -float(STRIDE), ends[:, 1, 0, :],
                                             ALU.mult, ALU.add))
            ch.settle()
            ch.step(dve.reduce_max(wide_f[:], start_f[:], AX.X))
            ch.settle()
            ch.step(dve.tensor_scalar(wide_i[:], wide_f[:], float(WIN), None, ALU.is_ge))
            ch.settle()
            dve.sem_inc(decoded, 1)

            dve.wait_ge(top_all, 1)
            ch.step(dve.tensor_tensor(z[:, 0, :, :], a_src, a_dst[:], ALU.add))
            raw_bound = prod[:, :, 0:GH]
            ch.step(dve.tensor_tensor(raw_bound, a_dst[:], spread(top[:, 1, :], 1, NF), ALU.add))
            ch.settle()
            ch.step(dve.scalar_tensor_tensor(bound[:], raw_bound, SLOPE, raw_bound, ALU.mult, ALU.max))
            dve.wait_ge(last_in, 16)
            ch.step(dve.tensor_tensor(z[:, 1, :, :], a_dst[:], spread(last_row[:, GF:TF], 1, NF), ALU.add))
            ch.settle()
            z_flat = z[:].rearrange("p n t h -> p (n t h)")
            ch.step(dve.scalar_tensor_tensor(z_flat, z_flat, SLOPE, z_flat, ALU.mult, ALU.max))
            ch.settle()
            dve.tensor_tensor(z[:], z[:], spread(bound[:], 1, 2), ALU.subtract).then_inc(dense_logit, 1)
            dve.wait_ge(dense_exp, 1)
            ch.step(dve.tensor_tensor(z[:, 1, :, :], z[:, 1, :, :], spread(last_counts[:], 2, GH), ALU.mult))
            ch.settle()
            ch.step(dve.tensor_tensor(split(dense[:, :, 0:GF]), split(h_nodes[:]),
                                      spread(z[:, 0, :, :], 3, EXPERTS), ALU.mult))
            ch.step(dve.tensor_tensor(split(prod[:]), spread(z[:, 1, :, :], 3, EXPERTS),
                                      spread(last_row[:, 0:GF].rearrange("p (h e) -> p h e", e=EXPERTS), 1, NF),
                                      ALU.mult))
            ch.close()
            ch.settle()
            dve.tensor_tensor(dense[:, :, 0:GF], dense[:, :, 0:GF], prod[:], ALU.add).then_inc(dense_ready, 1)
            dve.tensor_tensor(dense[:, :, GF:TF], z[:, 0, :, :], z[:, 1, :, :], ALU.add).then_inc(dense_ready, 1)
            dve.wait_ge(dense_ready, 2)

            count = dve.value_load(count_i[0:1, 0:1], min_val=0, max_val=COLS)

            def path(wide):
                width = NF if wide else WIN

                def one_hot(s, r):
                    dve.tensor_tensor(hot_b[s][:], spread(img[:, columns(r, s)], 1, 128), iota_b[:], ALU.is_equal)\
                        .then_inc(hot_ready[s], 1)

                def batches(r):
                    start = None if wide else start_of(dve, r)
                    c = [Chain(dve, chain[s], 6, r) for s in subs]
                    tokens = iota_f[:, 0:NF] if wide else iota_f[:, bass.ds(start * STRIDE, WIN)]
                    hots = [hot_tok[s][:, 0:BT * width].rearrange("p (k t) -> p k t", k=BT) for s in subs]
                    picks = [picked[s][:, 0:BT * width * GH].rearrange("p (k t h) -> p k t h", k=BT, h=GH)
                             for s in subs]
                    for s in subs:
                        dve.wait_ge(batch_ready[s], r + 1)
                        c[s].step(dve.tensor_tensor(hots[s], spread(tok[:, columns(r, s)], 2, width),
                                                    spread(tokens, 1, BT), ALU.is_equal))
                    for s in subs:
                        dve.wait_ge(src_in[s], 16 * BT * (r + 1))
                        dve.tensor_copy(from_src[s][:], gathered[s][:]).then_inc(src_taken[s], 1)
                    for s in subs:
                        dve.wait_ge(dst_ready[s], r + 1)
                        c[s].settle()
                        if wide:
                            for n in range(2):
                                at = (3 + 2 * s + n) * 512
                                got = psum[:, at:at + 2 * NF * GH].rearrange("p (k t h) -> p k t h", k=2, h=GH)
                                last = dve.tensor_tensor(picks[s][:, 2 * n:2 * n + 2], got,
                                                         spread(hots[s][:, 2 * n:2 * n + 2, :], 3, GH), ALU.mult)
                            c[s].step(last)
                        else:
                            at = (6 + s) * 512
                            got = psum[:, at:at + BT * WIN * GH].rearrange("p (k t h) -> p k t h", k=BT, h=GH)
                            c[s].step(dve.tensor_tensor(picks[s], got, spread(hots[s], 3, GH), ALU.mult))
                    for s in subs:
                        c[s].settle()
                        c[s].step(dve.reduce_sum(from_dst[s][:], picks[s].rearrange("p k t h -> p k h t"), AX.X))
                    for s in subs:
                        c[s].settle()
                        dve.wait_ge(src_taken[s], r + 2)
                        dve.tensor_tensor(logit[s][:, 0, :, :], from_src[s][:, :, GF:TF], from_dst[s][:], ALU.add)
                        c[s].step(dve.tensor_tensor(logit[s][:, 1, :, :], from_dst[s][:], spread(top[:, 1, :], 1, BT),
                                                    ALU.add))
                    for s in subs:
                        c[s].settle()
                        both = logit[s][:, 0:2, :, :].rearrange("p n k h -> p (n k h)")
                        c[s].step(dve.scalar_tensor_tensor(both, both, SLOPE, both, ALU.mult, ALU.max))
                    for s in subs:
                        c[s].settle()
                        dve.tensor_tensor(logit[s][:, 2, :, :], logit[s][:, 0, :, :], logit[s][:, 1, :, :],
                                          ALU.subtract).then_inc(logit_ready[s], 1)
                    for s in subs:
                        dve.wait_ge(exp_ready[s], r + 1)
                        c[s].step(dve.tensor_tensor(split(val[s][:, :, 0:GF]), split(from_src[s][:, :, 0:GF]),
                                                    spread(val[s][:, :, GF:TF], 3, EXPERTS), ALU.mult))
                    for s in subs:
                        dve.wait_ge(cast[s], r + 1)
                        one_hot(s, r + 1)
                        c[s].settle()
                        dve.tensor_tensor(spread_val[s][:, 0:BT * width * TF]
                                          .rearrange("p (k t f) -> p k t f", k=BT, f=TF),
                                          spread(hots[s], 3, TF), spread(val[s][:], 2, width), ALU.mult)\
                            .then_inc(batch_ready[s], 1)
                        c[s].close()

                for s in subs:
                    one_hot(s, 0)
                    dve.sem_inc(batch_ready[s], 1)
                edge_rounds(dve, count, batches)
                dve.wait_ge(sums_ready, 1)
                if wide:
                    for n, at in enumerate((slice(0, HALF), slice(HALF, NF))):
                        size = (at.stop - at.start) * TF
                        dve.tensor_tensor(agg[:, at, :],
                                          psum[:, n * 512:n * 512 + size].rearrange("p (t f) -> p t f", f=TF),
                                          dense[:, at, :], ALU.add).then_inc(sums_read, 1)
                    dve.wait_ge(sums_read, 2)
                else:
                    dve.tensor_copy(agg[:], dense[:]).then_inc(sums_read, 1)
                    for n in range(STARTS):
                        at = slice(n * STRIDE, n * STRIDE + WIN)
                        dve.wait_ge(sums_read, n + 1)
                        dve.tensor_tensor(agg[:, at, :], agg[:, at, :],
                                          psum[:, n * 512:n * 512 + WIN * TF].rearrange("p (t f) -> p t f", f=TF),
                                          ALU.add).then_inc(sums_read, 1)
                    dve.wait_ge(sums_read, STARTS + 1)
            both_paths(dve, path)


def mix_experts(nc, agg, hidden, expert_out, b_gat, gamma, beta, out):
    TF = GF + GH
    with ExitStack() as ctx:
        sb, ps, sem = tools(nc, ctx)
        hid = sb("hid", [128, NF, D])
        eo = sb("eo_m", [128, NF, EXPERTS * D])
        part = [sb(f"part{n}", [128, NF, D]) for n in range(2)]
        rows = sb("rows_m", [128, 3, GF])
        den = sb("den", [128, NF, GH])
        y = sb("y_m", [128, NF, GF])
        y2 = sb("y2_m", [128, NF, GF])
        stat = sb("stat_m", [128, 4, NF])
        half = sb("half_m", [128, NF])
        score = sb("score", [128, NF, EXPERTS])
        rank = sb("rank", [128, NF, EXPERTS])
        better = sb("better", [128, NF])
        gate = sb("gate", [128, NF, EXPERTS])
        rows_in = sem("m_rows_in")
        hid_in = sem("m_hid_in")
        eo_in = sem("m_eo_in")
        half_set = sem("m_half_set")
        var_ready = sem("m_var")
        rstd_ready = sem("m_rstd")
        shifted = sem("m_shifted")
        exped = sem("m_exped")
        chain = sem("m_chain")
        out_parts = sem("m_out_parts")
        out_ready = sem("m_out_ready")
        stored = sem("m_stored")
        block = ctx.enter_context(nc.Block())
        by_node = lambda t: t.rearrange("(b t) f -> b t f", t=NF)

        @block.sync
        def _(sync):
            for n, row in enumerate((b_gat, gamma, beta)):
                sync.dma_start(rows[:, n, :], row.partition_broadcast(128)).then_inc(rows_in, 16)
            sync.dma_start(hid[:], by_node(hidden)).then_inc(hid_in, 16)
            sync.dma_start(eo[:], by_node(expert_out)).then_inc(eo_in, 16)
            sync.wait_ge(out_ready, 1)
            sync.dma_start(out, hid[:]).then_inc(stored, 16)
            sync.wait_ge(stored, 16)

        @block.gpsimd
        def _(pool):
            pool.memset(half[:], -0.5).then_inc(half_set, 1)
            pool.wait_ge(half_set, 1)
            pool.wait_ge(var_ready, 1)
            pool.tensor_tensor(stat[:, 2, :], stat[:, 1, :], half[:], ALU.pow).then_inc(rstd_ready, 1)

        @block.scalar
        def _(act):
            act.wait_ge(shifted, 1)
            act.activation(gate[:], gate[:], ACT.Exp).then_inc(exped, 1)

        @block.vector
        def _(dve):
            ch = Chain(dve, chain, 41, 0)

            def then(ins):
                ch.step(ins)
                ch.settle()

            split = lambda t: t.rearrange("p t (h e) -> p t h e", e=EXPERTS)
            total, var, rstd, mean = (stat[:, n, :] for n in range(4))
            then(dve.tensor_scalar(den[:], agg[:, :, GF:TF], 1e-16, None, ALU.add))
            then(dve.reciprocal(den[:], den[:]))
            then(dve.tensor_tensor(split(y[:]), split(agg[:, :, 0:GF]), spread(den[:], 3, EXPERTS), ALU.mult))
            dve.wait_ge(rows_in, 48)
            then(dve.tensor_tensor(y[:], y[:], spread(rows[:, 0, :], 1, NF), ALU.add))
            then(dve.reduce_sum(total, y[:], AX.X))
            then(dve.scalar_tensor_tensor(y2[:], spread(total, 2, GF), -1.0 / GF, y[:], ALU.mult, ALU.add))
            then(dve.tensor_tensor(y[:], y2[:], y2[:], ALU.mult))
            then(dve.reduce_sum(total, y[:], AX.X))
            dve.tensor_scalar(var, total, 1.0 / GF, EPS, ALU.mult, ALU.add).then_inc(var_ready, 1)
            dve.wait_ge(rstd_ready, 1)
            then(dve.tensor_tensor(y[:], y2[:], spread(rstd, 2, GF), ALU.mult))
            then(dve.tensor_tensor(y2[:], y[:], spread(rows[:, 1, :], 1, NF), ALU.mult))
            then(dve.tensor_tensor(y[:], y2[:], spread(rows[:, 2, :], 1, NF), ALU.add))
            then(dve.reduce_sum(score[:], y[:].rearrange("p t (h e) -> p t e h", e=EXPERTS), AX.X))
            then(dve.tensor_scalar(score[:], score[:], 1.0 / GH, None, ALU.mult))
            for e in range(EXPERTS):
                then(dve.memset(rank[:, :, e], float(e)))
            for e in range(EXPERTS):
                for j in range(e):
                    then(dve.tensor_tensor(better[:], score[:, :, e], score[:, :, j], ALU.is_gt))
                    then(dve.tensor_tensor(rank[:, :, j], rank[:, :, j], better[:], ALU.add))
                    then(dve.tensor_tensor(rank[:, :, e], rank[:, :, e], better[:], ALU.subtract))
            then(dve.reduce_max(mean, score[:], AX.X))
            dve.tensor_tensor(gate[:], score[:], spread(mean, 2, EXPERTS), ALU.subtract).then_inc(shifted, 1)
            dve.wait_ge(exped, 1)
            then(dve.tensor_scalar(rank[:], rank[:], 1.5, None, ALU.is_lt))
            then(dve.tensor_tensor(gate[:], gate[:], rank[:], ALU.mult))
            then(dve.reduce_sum(total, gate[:], AX.X))
            then(dve.reciprocal(var, total))
            then(dve.tensor_tensor(gate[:], gate[:], spread(var, 2, EXPERTS), ALU.mult))
            dve.wait_ge(hid_in, 16)
            dve.wait_ge(eo_in, 16)
            ch.close()
            for e in range(EXPERTS):
                dve.tensor_tensor(part[e % 2][:], eo[:, :, e * D:(e + 1) * D], spread(gate[:, :, e], 2, D), ALU.mult)\
                    .then_inc(out_parts, 1)
                dve.wait_ge(out_parts, 2 * e + 1)
                dve.tensor_tensor(hid[:], hid[:], part[e % 2][:], ALU.add).then_inc(out_parts, 1)
                dve.wait_ge(out_parts, 2 * e + 2)
            dve.sem_inc(out_ready, 1)



def early_fusion(nc, x, txt, ln1_g, ln1_b, W_patch, b_patch, ln2_g, ln2_b, cls, pos, attn_g, attn_b, Wqkv, Wo, bo,
                 ff_g, ff_b, W1, b1, W2, b2, f_g, f_b, gat_w, att_src, att_dst, b_gat, gamma, beta, eW1, eb1, eW2,
                 eb2, edge_index, out):
    def scratch(name, shape):
        return nc.dram_tensor(name, shape, F32).ap()

    tokens = scratch("tokens", (B * NV, D))
    fused = scratch("fused", (NODES, D))
    hidden = scratch("hidden", (NODES, D))
    gat_h = scratch("gat_h", (NODES, GF))
    expert_out = scratch("expert_out", (NODES, EXPERTS * D))
    src_table = scratch("src_table", (NODES, GF + GH))
    with ExitStack() as ctx:
        sb, _, _ = tools(nc, ctx)
        keys_sorted = sb("keys_sorted", [128, COLS])
        count_i = sb("count_i", [128, 1], I32)
        last_counts = sb("last_counts", [128, NF])
        embed_and_sort(nc, x, ln1_g, ln1_b, W_patch, b_patch, ln2_g, ln2_b, cls, pos, tokens, edge_index,
                       keys_sorted, count_i, last_counts)
        agg = sb("agg", [128, NF, GF + GH])
        run_vit(nc, tokens, attn_g, attn_b, Wqkv, Wo, bo, ff_g, ff_b, W1, b1, W2, b2, f_g, f_b, txt, fused)
        fuse_and_expert(nc, fused, gat_w, eW1, eb1, eW2, eb2, hidden, gat_h, expert_out)
        route_edges(nc, keys_sorted, count_i, last_counts, gat_h, att_src, att_dst, src_table, agg)
        mix_experts(nc, agg, hidden, expert_out, b_gat, gamma, beta, out)


_INS = ['x', 'txt', 'L0_tok_ln_p1_g', 'L0_tok_ln_p1_b', 'L0_tok_W_patch', 'L0_tok_b_patch',
        'L0_tok_ln_p2_g', 'L0_tok_ln_p2_b', 'L0_tok_cls', 'L0_tok_pos', 'L0_tok_attn_ln_g',
        'L0_tok_attn_ln_b', 'L0_tok_Wqkv', 'L0_tok_Wo', 'L0_tok_bo', 'L0_tok_ff_ln_g', 'L0_tok_ff_ln_b',
        'L0_tok_W1', 'L0_tok_b1', 'L0_tok_W2', 'L0_tok_b2', 'L0_tok_ln_f_g', 'L0_tok_ln_f_b',
        'L0_ffn_W_gat', 'L0_ffn_att_src', 'L0_ffn_att_dst', 'L0_ffn_b_gat', 'L0_ffn_ln_gamma',
        'L0_ffn_ln_beta', 'L0_ffn_W1', 'L0_ffn_b1', 'L0_ffn_W2', 'L0_ffn_b2', 'L0_ffn_edge_index']
_OUTS = [((B, NF, D), 'float32')]


def kernel(**inputs):
    import numpy as _np
    import concourse.bacc as _bacc
    from concourse import mybir as _mybir
    from concourse.bass_utils import run_bass_kernel_spmd as _run

    nc = _bacc.Bacc("TRN2", target_bir_lowering=False, num_devices=1)
    arrays, args = {}, []
    for name in _INS:
        a = _np.ascontiguousarray(inputs[name])
        arrays[f"in_{name}_dram"] = a
        args.append(nc.dram_tensor(f"in_{name}_dram", a.shape, _mybir.dt.from_np(a.dtype), kind="ExternalInput").ap())
    for i, (shape, dtype) in enumerate(_OUTS):
        dt = _mybir.dt.from_np(_np.dtype(dtype))
        args.append(nc.dram_tensor(f"out_{i}_dram", shape, dt, kind="ExternalOutput").ap())
    early_fusion(nc, *args)
    r = _run(nc, [arrays], core_ids=[0])
    got = tuple(r.results[0][f"out_{i}_dram"] for i in range(len(_OUTS)))
    return got[0]
```
